# Optimizing a Trainium2 kernel written in Bass

```python
import numpy as np
import jax
import jax.numpy as jnp

def _softmax(x, axis=-1):
    return jax.nn.softmax(x, axis=axis)

def _gelu(x):
    return jax.nn.gelu(x, approximate=True)

def _silu(x):
    return jax.nn.silu(x)

def _sigmoid(x):
    return jax.nn.sigmoid(x)

def _layernorm(x, axis=-1, eps=1e-05):
    m = jnp.mean(x, axis=axis, keepdims=True)
    v = jnp.var(x, axis=axis, keepdims=True)
    return (x - m) / jnp.sqrt(v + eps)

def _scatter_add(tgt, idx, src, axis=0):
    return tgt.at[idx].add(src)

def _segment_sum(src, seg, n):
    return jax.ops.segment_sum(src, seg, n)
kernel_name = 'mk_xattn_ffn_d2_seqx_r8_ec600f'

def setup_inputs(seed: int=0):
    np.random.seed(seed)
    _w = jnp.asarray

    def _rec_inputs():
        import jax
        import jax.numpy as jnp
        _rk = jax.random.key(seed)
        x = -0.0003929 + 0.9999 * jax.random.normal(jax.random.fold_in(_rk, 1), (8, 100, 256), jnp.float32)
        _lenS = 100 - jax.random.randint(jax.random.fold_in(_rk, 7), (8,), 0, max(1, 100 // 4) + 1, jnp.int32)
        _lenS2 = 1444 - jax.random.randint(jax.random.fold_in(_rk, 8), (8,), 0, max(1, 1444 // 4) + 1, jnp.int32)
        _ctx_1024P = jax.random.normal(jax.random.fold_in(_rk, 11), (8, 16, 128), jnp.float32)
        _ctx_1024c = jax.random.dirichlet(jax.random.fold_in(_rk, 511), 0.3 * jnp.ones((16,), jnp.float32), (8, 1444))
        _ctx_1024t = jnp.einsum('bsk,bkd->bsd', _ctx_1024c, _ctx_1024P)
        _ctx_1024t = _ctx_1024t * jax.lax.rsqrt(jnp.mean(jnp.square(_ctx_1024t)) + 1e-12) * 0.953939
        ctx_1024 = -0.000494167 + 1.00018 * (_ctx_1024t + 0.3 * jax.random.normal(jax.random.fold_in(_rk, 611), (8, 1444, 128), jnp.float32))
        _validS = jnp.arange(100)[None, :] < _lenS[:, None]
        _validS2 = jnp.arange(1444)[None, :] < _lenS2[:, None]
        _causal = jnp.tril(jnp.ones((100, 100), dtype=bool))
        mask_BxS2_bf1 = jnp.ones((8, 1444), dtype=bool)
        return (x, ctx_1024, mask_BxS2_bf1)
    x, ctx_1024, mask_BxS2_bf1 = _rec_inputs()

    def _L0_xattn_setup():
        import jax, jax.numpy as jnp
        import numpy as np
        N_HEADS = 16
        N_KV_HEADS = 8
        HEAD_DIM = 128
        D_TEXT = 256
        D_VISION = 128
        GROUPS = N_HEADS // N_KV_HEADS
        key = jax.random.key(seed)
        ks = jax.random.split(key, 6)
        B, T_text, T_vis = (4, 256, 72)
        text_hidden = jax.random.normal(ks[0], (B, T_text, D_TEXT), dtype=jnp.float32)
        vision_tokens = jax.random.normal(ks[1], (B, T_vis, D_VISION), dtype=jnp.float32)
        vision_mask = jnp.ones((B, T_vis), dtype=bool)
        s = 0.02
        Wq = jax.random.normal(ks[2], (D_TEXT, N_HEADS * HEAD_DIM), dtype=jnp.float32) * s
        Wk = jax.random.normal(ks[3], (D_VISION, N_KV_HEADS * HEAD_DIM), dtype=jnp.float32) * s
        Wv = jax.random.normal(ks[4], (D_VISION, N_KV_HEADS * HEAD_DIM), dtype=jnp.float32) * s
        Wo = jax.random.normal(ks[5], (N_HEADS * HEAD_DIM, D_TEXT), dtype=jnp.float32) * s
        return {'text_hidden': text_hidden, 'vision_tokens': vision_tokens, 'vision_mask': vision_mask, 'Wq': Wq, 'Wk': Wk, 'Wv': Wv, 'Wo': Wo}
    _L0_xattn_all = _L0_xattn_setup()
    _L0_xattn_in = {k: v for k, v in _L0_xattn_all.items() if k in ('Wq', 'Wk', 'Wv', 'Wo')}
    del _L0_xattn_all

    def _L0_ffn_setup():
        import jax, jax.numpy as jnp
        import numpy as np

        def ternary_quantize(t, threshold, scale):
            return jnp.where(t > threshold, scale, jnp.where(t < -threshold, -scale, 0.0)).astype(t.dtype)
        key = jax.random.key(seed)
        k1, k2, k3 = jax.random.split(key, 3)
        B, S, D = (4, 512, 256)
        x = jax.random.normal(k1, (B, S, D), dtype=jnp.float32)
        weight = jax.random.normal(k2, (D, D), dtype=jnp.float32) * 0.02
        rram_variation = jax.random.normal(k3, (D, D), dtype=jnp.float32) * 0.05
        return {'x': x, 'weight': weight, 'rram_variation': rram_variation}
    _L0_ffn_all = _L0_ffn_setup()
    _L0_ffn_in = {k: v for k, v in _L0_ffn_all.items() if k in ('weight', 'rram_variation')}
    del _L0_ffn_all

    def _L1_xattn_setup():
        import jax, jax.numpy as jnp
        import numpy as np
        EPS = 1e-05

        def rmsnorm(x, g, eps=EPS):
            var = jnp.mean(jnp.square(x), axis=-1, keepdims=True)
            return x * jax.lax.rsqrt(var + eps) * g
        key = jax.random.key(seed)
        ks = jax.random.split(key, 8)
        B, Sq, Skv = (2, 512, 64)
        dim, cdim, H, D = (256, 128, 16, 128)
        inner = H * D
        s = lambda f: 1.0 / np.sqrt(f)
        return {'hidden_states': jax.random.normal(ks[0], (B, Sq, dim), jnp.float32), 'encoder_hidden_states': jax.random.normal(ks[1], (B, Skv, cdim), jnp.float32), 'Wq': jax.random.normal(ks[2], (dim, inner), jnp.float32) * s(dim), 'Wk': jax.random.normal(ks[3], (cdim, inner), jnp.float32) * s(cdim), 'Wv': jax.random.normal(ks[4], (cdim, inner), jnp.float32) * s(cdim), 'Wo': jax.random.normal(ks[5], (inner, dim), jnp.float32) * s(inner), 'gq': jnp.ones((D,), jnp.float32), 'gk': jnp.ones((D,), jnp.float32)}
    _L1_xattn_all = _L1_xattn_setup()
    _L1_xattn_in = {k: v for k, v in _L1_xattn_all.items() if k in ('Wq', 'Wk', 'Wv', 'Wo', 'gq', 'gk')}
    del _L1_xattn_all

    def _L1_ffn_setup():
        import jax, jax.numpy as jnp
        import numpy as np
        HIDDEN = 256
        FFN = 176
        N_EXPERTS = 64
        TOP_K = 6
        N_SHARED = 2
        SHARED_FFN = FFN * N_SHARED
        ROUTED_SCALING = 1.0
        EPS = 1e-20

        def _moe_forward(x, gate_w, w_gate_up, w_down, ws_gate_up, ws_down):
            T = x.shape[0]
            logits = jnp.einsum('th,eh->te', x.astype(jnp.float32), gate_w.astype(jnp.float32))
            scores = jax.nn.softmax(logits, axis=-1)
            topk_w, topk_ids = jax.lax.top_k(scores, TOP_K)
            topk_w = topk_w / (jnp.sum(topk_w, axis=-1, keepdims=True) + EPS)
            topk_w = topk_w * ROUTED_SCALING
            comb = jnp.zeros((T, N_EXPERTS), dtype=x.dtype)
            comb = comb.at[jnp.arange(T)[:, None], topk_ids].add(topk_w.astype(x.dtype))
            gu = jnp.einsum('th,efh->tef', x, w_gate_up)
            g, u = (gu[..., :FFN], gu[..., FFN:])
            act = jax.nn.silu(g) * u
            act = act * comb[:, :, None]
            routed = jnp.einsum('tef,ehf->th', act, w_down)
            sgu = jnp.einsum('th,fh->tf', x, ws_gate_up)
            sg, su = (sgu[..., :SHARED_FFN], sgu[..., SHARED_FFN:])
            shared = jnp.einsum('tf,hf->th', jax.nn.silu(sg) * su, ws_down)
            return routed + shared
        key = jax.random.key(seed)
        k0, k1, k2, k3, k4, k5 = jax.random.split(key, 6)
        hidden_states = jax.random.normal(k0, (1, 32, HIDDEN), dtype=jnp.float32)
        gate_w = jax.random.normal(k1, (N_EXPERTS, HIDDEN), dtype=jnp.float32) * 0.05
        w_gate_up = jax.random.normal(k2, (N_EXPERTS, 2 * FFN, HIDDEN), dtype=jnp.float32) * 0.02
        w_down = jax.random.normal(k3, (N_EXPERTS, HIDDEN, FFN), dtype=jnp.float32) * 0.02
        ws_gate_up = jax.random.normal(k4, (2 * SHARED_FFN, HIDDEN), dtype=jnp.float32) * 0.02
        ws_down = jax.random.normal(k5, (HIDDEN, SHARED_FFN), dtype=jnp.float32) * 0.02
        return {'hidden_states': hidden_states, 'gate_w': gate_w, 'w_gate_up': w_gate_up, 'w_down': w_down, 'ws_gate_up': ws_gate_up, 'ws_down': ws_down}
    _L1_ffn_all = _L1_ffn_setup()
    _L1_ffn_in = {k: v for k, v in _L1_ffn_all.items() if k in ('gate_w', 'w_gate_up', 'w_down', 'ws_gate_up', 'ws_down')}
    del _L1_ffn_all
    return {'x': x, 'ctx_1024': ctx_1024, 'mask_BxS2_bf1': mask_BxS2_bf1, 'L0_xattn_Wq': _L0_xattn_in['Wq'], 'L0_xattn_Wk': _L0_xattn_in['Wk'], 'L0_xattn_Wv': _L0_xattn_in['Wv'], 'L0_xattn_Wo': _L0_xattn_in['Wo'], 'L0_ffn_weight': _L0_ffn_in['weight'], 'L0_ffn_rram_variation': _L0_ffn_in['rram_variation'], 'L1_xattn_Wq': _L1_xattn_in['Wq'], 'L1_xattn_Wk': _L1_xattn_in['Wk'], 'L1_xattn_Wv': _L1_xattn_in['Wv'], 'L1_xattn_Wo': _L1_xattn_in['Wo'], 'L1_xattn_gq': _L1_xattn_in['gq'], 'L1_xattn_gk': _L1_xattn_in['gk'], 'L1_ffn_gate_w': _L1_ffn_in['gate_w'], 'L1_ffn_w_gate_up': _L1_ffn_in['w_gate_up'], 'L1_ffn_w_down': _L1_ffn_in['w_down'], 'L1_ffn_ws_gate_up': _L1_ffn_in['ws_gate_up'], 'L1_ffn_ws_down': _L1_ffn_in['ws_down']}

def reference(x, ctx_1024, mask_BxS2_bf1, L0_xattn_Wq, L0_xattn_Wk, L0_xattn_Wv, L0_xattn_Wo, L0_ffn_weight, L0_ffn_rram_variation, L1_xattn_Wq, L1_xattn_Wk, L1_xattn_Wv, L1_xattn_Wo, L1_xattn_gq, L1_xattn_gk, L1_ffn_gate_w, L1_ffn_w_gate_up, L1_ffn_w_down, L1_ffn_ws_gate_up, L1_ffn_ws_down):
    import jax
    import jax.numpy as jnp

    def _L0_xattn_ref(text_hidden, vision_tokens, vision_mask, Wq, Wk, Wv, Wo):
        import jax, jax.numpy as jnp
        import numpy as np
        N_HEADS = 16
        N_KV_HEADS = 8
        HEAD_DIM = 128
        D_TEXT = 256
        D_VISION = 128
        GROUPS = N_HEADS // N_KV_HEADS
        B, T_text, _ = text_hidden.shape
        T_vis = vision_tokens.shape[1]
        scale = jnp.float32(np.sqrt(HEAD_DIM))
        q = (text_hidden @ Wq).reshape(B, T_text, N_HEADS, HEAD_DIM).transpose(0, 2, 1, 3)
        k = (vision_tokens @ Wk).reshape(B, T_vis, N_KV_HEADS, HEAD_DIM).transpose(0, 2, 1, 3)
        v = (vision_tokens @ Wv).reshape(B, T_vis, N_KV_HEADS, HEAD_DIM).transpose(0, 2, 1, 3)
        k = jnp.repeat(k, GROUPS, axis=1)
        v = jnp.repeat(v, GROUPS, axis=1)
        scores = jnp.einsum('bhtd,bhsd->bhts', q, k) / scale
        mask = vision_mask[:, None, None, :]
        scores = jnp.where(mask, scores, -jnp.inf)
        attn = jax.nn.softmax(scores, axis=-1)
        attn = jnp.nan_to_num(attn, nan=0.0)
        out = jnp.einsum('bhts,bhsd->bhtd', attn, v)
        out = out.transpose(0, 2, 1, 3).reshape(B, T_text, N_HEADS * HEAD_DIM)
        return out @ Wo

    def _L0_ffn_ref(x, weight, rram_variation):
        import jax, jax.numpy as jnp
        import numpy as np

        def ternary_quantize(t, threshold, scale):
            return jnp.where(t > threshold, scale, jnp.where(t < -threshold, -scale, 0.0)).astype(t.dtype)
        TH_X, SC_X = (0.33, 0.5)
        TH_W, SC_W = (0.2, 0.6)
        x_q = ternary_quantize(x, TH_X, SC_X)
        w_q = ternary_quantize(weight, TH_W, SC_W)
        w_rram = w_q + rram_variation
        return jnp.einsum('bsd,od->bso', x_q, w_rram)

    def _L1_xattn_ref(hidden_states, encoder_hidden_states, Wq, Wk, Wv, Wo, gq, gk):
        import jax, jax.numpy as jnp
        import numpy as np
        EPS = 1e-05

        def rmsnorm(x, g, eps=EPS):
            var = jnp.mean(jnp.square(x), axis=-1, keepdims=True)
            return x * jax.lax.rsqrt(var + eps) * g
        B, Sq, _ = hidden_states.shape
        Skv = encoder_hidden_states.shape[1]
        D = gq.shape[0]
        H = Wq.shape[1] // D
        scale = 1.0 / np.sqrt(D)
        q = (hidden_states @ Wq).reshape(B, Sq, H, D)
        k = (encoder_hidden_states @ Wk).reshape(B, Skv, H, D)
        v = (encoder_hidden_states @ Wv).reshape(B, Skv, H, D)
        q = rmsnorm(q, gq)
        k = rmsnorm(k, gk)
        scores = jnp.einsum('bqhd,bkhd->bhqk', q, k) * scale
        attn = jax.nn.softmax(scores, axis=-1)
        out = jnp.einsum('bhqk,bkhd->bqhd', attn, v)
        out = out.reshape(B, Sq, H * D)
        return out @ Wo

    def _L1_ffn_ref(hidden_states, gate_w, w_gate_up, w_down, ws_gate_up, ws_down):
        import jax, jax.numpy as jnp
        import numpy as np
        HIDDEN = 256
        FFN = 176
        N_EXPERTS = 64
        TOP_K = 6
        N_SHARED = 2
        SHARED_FFN = FFN * N_SHARED
        ROUTED_SCALING = 1.0
        EPS = 1e-20

        def _moe_forward(x, gate_w, w_gate_up, w_down, ws_gate_up, ws_down):
            T = x.shape[0]
            logits = jnp.einsum('th,eh->te', x.astype(jnp.float32), gate_w.astype(jnp.float32))
            scores = jax.nn.softmax(logits, axis=-1)
            topk_w, topk_ids = jax.lax.top_k(scores, TOP_K)
            topk_w = topk_w / (jnp.sum(topk_w, axis=-1, keepdims=True) + EPS)
            topk_w = topk_w * ROUTED_SCALING
            comb = jnp.zeros((T, N_EXPERTS), dtype=x.dtype)
            comb = comb.at[jnp.arange(T)[:, None], topk_ids].add(topk_w.astype(x.dtype))
            gu = jnp.einsum('th,efh->tef', x, w_gate_up)
            g, u = (gu[..., :FFN], gu[..., FFN:])
            act = jax.nn.silu(g) * u
            act = act * comb[:, :, None]
            routed = jnp.einsum('tef,ehf->th', act, w_down)
            sgu = jnp.einsum('th,fh->tf', x, ws_gate_up)
            sg, su = (sgu[..., :SHARED_FFN], sgu[..., SHARED_FFN:])
            shared = jnp.einsum('tf,hf->th', jax.nn.silu(sg) * su, ws_down)
            return routed + shared
        B, S, H = hidden_states.shape
        x = hidden_states.reshape(-1, H)
        out = _moe_forward(x, gate_w, w_gate_up, w_down, ws_gate_up, ws_down)
        return out.reshape(B, S, H)
    x = x + _L0_xattn_ref(_layernorm(x, axis=-1), ctx_1024, mask_BxS2_bf1, L0_xattn_Wq, L0_xattn_Wk, L0_xattn_Wv, L0_xattn_Wo)
    x = x + _L0_ffn_ref(_layernorm(x, axis=-1), L0_ffn_weight, L0_ffn_rram_variation)
    x = x + _L1_xattn_ref(_layernorm(x, axis=-1), ctx_1024, L1_xattn_Wq, L1_xattn_Wk, L1_xattn_Wv, L1_xattn_Wo, L1_xattn_gq, L1_xattn_gk)
    x = x + _L1_ffn_ref(_layernorm(x, axis=-1), L1_ffn_gate_w, L1_ffn_w_gate_up, L1_ffn_w_down, L1_ffn_ws_gate_up, L1_ffn_ws_down)
    return x

_drawn_inputs = setup_inputs


def setup_inputs(seed=0):
    import zlib

    import numpy as np

    out = dict(_drawn_inputs(seed))
    spreads = {'L1_xattn_gq': (1.0, 0.2), 'L1_xattn_gk': (1.0, 0.2)}
    factors = {'L0_xattn_Wq': 4.802,
     'L0_xattn_Wk': 4.7,
     'L1_ffn_gate_w': 8.0,
     'L1_ffn_w_gate_up': 8.0,
     'L1_ffn_w_down': 8.0,
     'L1_ffn_ws_gate_up': 3.373,
     'L1_ffn_ws_down': 3.363}
    for name, (base, spread) in spreads.items():
        noise = np.random.default_rng([zlib.crc32(name.encode()), seed]).standard_normal(out[name].shape)
        drawn = base * np.exp(spread * noise) if base else spread * noise
        out[name] = jnp.asarray(drawn.astype(out[name].dtype))
    for name, factor in factors.items():
        out[name] = (out[name] * factor).astype(out[name].dtype)
    return out
```

```python
from contextlib import ExitStack

import concourse.bass as bass
from concourse import mybir

F32 = mybir.dt.float32
F32R = mybir.dt.float32r
BF16 = mybir.dt.bfloat16
U8 = mybir.dt.uint8
ALU = mybir.AluOpType
ACT = mybir.ActivationFunctionType
AX_X = mybir.AxisListType.X

NB = 8
Q = 100
D = 256
DC = D // 128
C = 128
KEYS = 1444
H = 16
HD = 128
KB = -(-KEYS // 128)
KT = KEYS - (KB - 1) * 128
HG = 4
NG = H // HG
STEPS = NB * NG
CHUNKS = [(0, 512), (512, 512), (1024, KEYS - 1024)]
TB = 4
NT = KB // TB
INV = float(HD) ** -0.5
BIG = 1.0e30
LN_EPS = 1e-5


class Count:

    def __init__(self, sem):
        self.sem, self.n = sem, 0

    def by(self, instruction, step=1):
        instruction.then_inc(self.sem, step)
        self.n += step

    def then_wait(self, engine, instruction, step=1):
        self.by(instruction, step)
        engine.wait_ge(self.sem, self.n)


class Core:

    def __init__(self, nc, whole):
        self.nc, self.whole, self.phase = nc, whole, whole

    def sem(self, name):
        return self.whole.enter_context(self.nc.semaphore(name))

    def sb(self, name, shape, dt=F32):
        return self.phase.enter_context(self.nc.sbuf_tensor(name, shape, dt))

    def ps(self, name, shape, dt=F32):
        return self.phase.enter_context(self.nc.psum_tensor(name, shape, dt))


def newton_rsqrt(dve, chain, v, root, r, t):
    chain.then_wait(dve, dve.reciprocal(r, root))
    chain.then_wait(dve, dve.tensor_tensor(t, r, r, ALU.mult))
    chain.then_wait(dve, dve.tensor_tensor(t, t, v, ALU.mult))
    chain.then_wait(dve, dve.tensor_scalar(t, t, -0.5, 1.5, ALU.mult, ALU.add))
    chain.then_wait(dve, dve.tensor_tensor(r, r, t, ALU.mult))


def setup_phase(k, x_in, X, ident, sel):
    nc = k.nc
    loaded, made = k.sem("x_loaded"), k.sem("consts_made")
    with nc.Block() as block:
        @block.sync
        def _(sp):
            sp.dma_start(X[0:Q, :, :], x_in.rearrange("b q d -> q b d")).then_inc(loaded, 16)
            sp.wait_ge(loaded, 16)

        @block.gpsimd
        def _(pool):
            chain = Count(made)
            chain.by(pool.memset(sel[:], 0.0))
            chain.then_wait(pool, pool.memset(ident[:], 0.0))
            chain.then_wait(pool, pool.affine_select(out=ident[:], in_=ident[:], compare_op=ALU.not_equal, fill=1.0,
                                                     base=0, pattern=[[-1, 128]], channel_multiplier=1))
            for part in range(3):
                chain.then_wait(pool, pool.affine_select(
                    out=sel[:], in_=sel[:], compare_op=ALU.not_equal, fill=1.0,
                    base=-32 * part, pattern=[[-1, H], [0, 128]], channel_multiplier=1))


def norm_phase(k, tag, X, ident, xn, xnT, after=None):
    nc = k.nc
    dve_s, root_s, var_s = k.sem(f"{tag}_dve"), k.sem(f"{tag}_root"), k.sem(f"{tag}_var")
    tr_s, out_s = k.sem(f"{tag}_turned"), k.sem(f"{tag}_taken")
    with ExitStack() as k.phase:
        stats, mv = k.sb(f"{tag}_stats", [128, NB, 6]), k.sb(f"{tag}_mv", [128, NB, 2])
        var, root = k.sb(f"{tag}_varr", [128, NB]), k.sb(f"{tag}_rootv", [128, NB])
        rstd, t = k.sb(f"{tag}_rstd", [128, NB]), k.sb(f"{tag}_t", [128, NB])
        u, w = k.sb(f"{tag}_u", [128, NB, D]), k.sb(f"{tag}_w", [128, NB, D])
        turned = k.ps(f"{tag}_ps", [128, 4, 512])
        with nc.Block() as block:
            @block.vector
            def _(dve):
                chain = Count(dve_s)
                for b in range(NB):
                    chain.by(dve.bn_stats(stats[0:Q, b, :], X[0:Q, b, :]))
                dve.wait_ge(dve_s, chain.n)
                for b in range(NB):
                    chain.by(dve.bn_aggr(mv[0:Q, b, :], stats[0:Q, b, :]))
                dve.wait_ge(dve_s, chain.n)
                dve.tensor_scalar(var[0:Q, :], mv[0:Q, :, 1], LN_EPS, None, ALU.add).then_inc(var_s, 1)
                dve.wait_ge(root_s, 1)
                dve.wait_ge(var_s, 1)
                newton_rsqrt(dve, chain, var[0:Q, :], root[0:Q, :], rstd[0:Q, :], t[0:Q, :])
                for b in range(NB):
                    ins = dve.tensor_scalar(xn[0:Q, b, :], X[0:Q, b, :], mv[0:Q, b, 0:1], rstd[0:Q, b:b + 1],
                                            ALU.subtract, ALU.mult)
                    chain.by(ins)
                dve.wait_ge(dve_s, chain.n)
                if after:
                    after(dve, chain, xn, u, w)
                dve.tensor_copy(t[0:Q, :], rstd[0:Q, :]).then_inc(var_s, 1)
                for i in range(NB * DC // 4):
                    dve.wait_ge(tr_s, i + 1)
                    for j in range(4):
                        b, c = divmod(4 * i + j, DC)
                        ins = dve.tensor_copy(xnT[:, c, b, :], turned[:, i, 128 * j:128 * j + Q])
                    ins.then_inc(out_s, 1)
                dve.wait_ge(out_s, NB * DC // 4)

            @block.scalar
            def _(act):
                act.wait_ge(var_s, 1)
                act.activation(root[0:Q, :], var[0:Q, :], ACT.Sqrt).then_inc(root_s, 1)

            @block.tensor
            def _(pe):
                pe.wait_ge(var_s, 2)
                for i in range(NB * DC // 4):
                    for j in range(4):
                        b, c = divmod(4 * i + j, DC)
                        ins = pe.transpose(turned[:, i, 128 * j:128 * j + Q], xn[0:Q, b, 128 * c:128 * (c + 1)],
                                           ident[0:Q, 0:Q])
                    ins.then_inc(tr_s, 1)
    k.phase = k.whole


def combine_phase(k, tag, kv, WqT_in, WkT_in, WvT_in, Wo_in, gains, A, Bw):
    nc = k.nc
    gain_s = k.sem(f"{tag}_gain")
    wk_in, wv_in = k.sem(f"{tag}_wk_in"), k.sem(f"{tag}_wv_in")
    wq_in, wo_in = ([k.sem(f"{tag}_{n}_in{i}") for i in range(2)] for n in ("wq", "wo"))
    mm_s, out_s = k.sem(f"{tag}_mm"), k.sem(f"{tag}_out")
    gin = k.sem(f"{tag}_gin")
    with ExitStack() as k.phase:
        WqT, WkT = k.sb(f"{tag}_WqT", [128, H, D]), k.sb(f"{tag}_WkT", [128, kv, C])
        WvT, Wo = k.sb(f"{tag}_WvT", [128, kv, C]), k.sb(f"{tag}_Wo", [128, H, D])
        g = k.sb(f"{tag}_g", [128, 3])
        ps = k.ps(f"{tag}_ps", [128, 8, 512])
        with nc.Block() as block:
            @block.sync
            def _(sp):
                sp.dma_start(WkT[:], WkT_in).then_inc(wk_in, 16)
                if gains:
                    for i in range(2):
                        sp.dma_start(g[:, i:i + 1], gains[i]).then_inc(gin, 16)
                for half in range(2):
                    hs = slice(half * H // 2, (half + 1) * H // 2)
                    sp.dma_start(WqT[:, hs, :], WqT_in[:, hs, :]).then_inc(wq_in[half], 16)
                sp.dma_start(WvT[:], WvT_in).then_inc(wv_in, 16)
                for half in range(2):
                    hs = slice(half * H // 2, (half + 1) * H // 2)
                    sp.dma_start(Wo[:, hs, :], Wo_in[:, hs, :]).then_inc(wo_in[half], 16)

            @block.gpsimd
            def _(pool):
                if gains:
                    pool.wait_ge(gin, 32)
                    pool.tensor_tensor(g[:, 2:3], g[:, 0:1], g[:, 1:2], ALU.mult).then_inc(gain_s, 1)
                    pool.wait_ge(gain_s, 1)
                    pool.wait_ge(wk_in, 16)
                    pool.tensor_scalar(WkT[:], WkT[:], g[:, 2:3], None, ALU.mult).then_inc(gain_s, 1)

            @block.tensor
            def _(pe):
                pe.wait_ge(wk_in, 16)
                if gains:
                    pe.wait_ge(gain_s, 2)
                for h in range(H):
                    pe.wait_ge(wq_in[h // (H // 2)], 16)
                    if h >= 8:
                        pe.wait_ge(out_s, h - 7)
                    for c in range(DC):
                        ins = pe.matmul(ps[:, h % 8, C * c:C * (c + 1)], WqT[:, h, 128 * c:128 * (c + 1)],
                                        WkT[:, h * kv // H, :], start=True, stop=True)
                    ins.then_inc(mm_s, 1)
                pe.wait_ge(wv_in, 16)
                for h in range(H):
                    pe.wait_ge(wo_in[h // (H // 2)], 16)
                    pe.wait_ge(out_s, H + h - 7)
                    pe.matmul(ps[:, h % 8, 0:D], WvT[:, h * kv // H, :], Wo[:, h, :],
                              start=True, stop=True).then_inc(mm_s, 1)

            @block.vector
            def _(dve):
                for h in range(H):
                    dve.wait_ge(mm_s, h + 1)
                    dve.tensor_copy(A[:, :, h, :], ps[:, h % 8, 0:DC * C].rearrange("p (c n) -> p c n", c=DC))\
                       .then_inc(out_s, 1)
                for h in range(H):
                    dve.wait_ge(mm_s, H + h + 1)
                    dve.tensor_copy(Bw[:, h, :], ps[:, h % 8, 0:D]).then_inc(out_s, 1)
    k.phase = k.whole


def attention_phase(k, tag, rms, X, xnT, ident, sel, A, Bw, sc, ctxT_in, ctxN_in, mask_in, rT_in):
    nc = k.nc
    sem = lambda name: k.sem(f"{tag}_{name}")
    ctxT_loaded, ctxN_loaded, side_loaded = sem("ctxT_loaded"), sem("ctxN_loaded"), sem("side_loaded")
    ctxT_hi_s, ctxT_split = sem("ctxT_hi"), sem("ctxT_split")
    ctxN_hi_s, ctxN_split = sem("ctxN_hi"), sem("ctxN_split")
    side_made = sem("side_made")
    x_copied, qnat_ready, qn_scaled, qT_ready, q_copied, qhi_s, qlo_s = (
        sem(n) for n in ("x_copied", "qnat_ready", "qn_scaled", "qT_ready", "q_copied", "qhi", "qlo"))
    row_ready, row_copied = sem("row_ready"), sem("row_copied")
    scores_ready, scores_taken, max_ready, exp_done = (
        sem(n) for n in ("scores_ready", "scores_taken", "max_ready", "exp_done"))
    turned, ehi_s, elo_s = sem("turned"), sem("ehi"), sem("elo")
    pv_thirds, o_copied, y_ready, y_added, rden_s = (
        sem(n) for n in ("pv_thirds", "o_copied", "y_ready", "y_added", "rden"))
    zeroed, passed, passed_pe, passed_sp = (sem(n) for n in ("zeroed", "passed", "passed_pe", "passed_sp"))

    with ExitStack() as k.phase:
        sb, ps = (lambda n, s, d=F32: k.sb(f"{tag}_{n}", s, d)), (lambda n: k.ps(f"{tag}_{n}", [128, 512]))
        ctxT_raw, ctxN_raw = sb("ctxT_raw", [128, KEYS]), sb("ctxN_raw", [128, KB, C])
        ctxT_hi, ctxT_lo = sb("ctxT_hi", [128, 2, KEYS], F32R), sb("ctxT_lo", [128, 2, KEYS], F32R)
        ctxN_hi, ctxN_lo = sb("ctxN_hi", [128, KB, C], F32R), sb("ctxN_lo", [128, KB, C], F32R)
        xs = sb("xs", [128, DC, Q])
        qn, qT = sb("qn", [128, HG, C]), sb("qT", [128, HG, Q])
        q_hi, q_lo = sb("q_hi", [128, HG, Q], F32R), sb("q_lo", [128, HG, Q], F32R)
        E = sb("E", [128, HG, KB * 128])
        e_hi, e_lo = sb("e_hi", [128, KB, HG, Q], F32R), sb("e_lo", [128, KB, HG, Q], F32R)
        side = sb("side", [128, 2, KEYS])
        mx, negm, den = sb("mx", [128, HG, 3]), sb("negm", [128, HG]), sb("den", [128, 2 * HG])
        rden = sb("rden", [128, HG])
        OT = sb("OT", [128, HG, Q])
        if rms:
            rT = sb("rT", [128, 2, KEYS], BF16)
        else:
            mask_u8 = sb("mask_u8", [128, KEYS], U8)
            seen = sb("seen", [128, 2])
        S_ps = [ps("S0"), ps("S1")]
        T_ps = [ps("T0"), ps("T1")]
        O_ps, QT_ps, row_ps, misc = ps("O"), ps("QT"), ps("row"), ps("misc")

        def batch_of(G):
            return (G % STEPS) // NG

        def group_of(G):
            return G % NG

        def run(step, boundary, drain, first=lambda b: None):
            def steps_of(eng):
                first(0)
                step(0, False)
                boundary(0)
                with eng.Fori(1, NG) as g:
                    step(g, True)
                with eng.Fori(1, NB) as b:
                    first(b)
                    step(NG * b, True)
                    boundary(b)
                    with eng.Fori(1, NG) as g:
                        step(NG * b + g, True)
                drain(STEPS)
            return steps_of

        with nc.Block() as block:
            @block.sync
            def _(sp):
                def load_T(b):
                    sp.dma_start(ctxT_raw[:], ctxT_in[b]).then_inc(ctxT_loaded, 16)

                def load_N(b):
                    n = (KB - 1) * 128
                    sp.dma_start(ctxN_raw[:, 0:KB - 1, :], ctxN_in[b, 0:n, :].rearrange("(j p) c -> p j c", p=128))\
                      .then_inc(ctxN_loaded, 16)
                    sp.dma_start(ctxN_raw[0:KT, KB - 1, :], ctxN_in[b, n:KEYS, :]).then_inc(ctxN_loaded, 16)

                def load_side(b, slot):
                    if rms:
                        for part in range(3):
                            sp.dma_start(rT[32 * part:32 * part + H, slot, :], rT_in[b, part])\
                              .then_inc(side_loaded, 16)
                    else:
                        sp.dma_start(mask_u8[0:Q, :], mask_in[b].partition_broadcast(Q)).then_inc(side_loaded, 16)

                if rms:
                    sp.wait_ge(zeroed, 1)
                load_T(0)
                load_side(0, 0)
                sp.wait_ge(zeroed, 3)
                load_N(0)
                with sp.Fori(0, NB) as b:
                    nb = (b + 1) % NB
                    sp.wait_ge(ctxT_split, b + 1)
                    load_T(nb)
                    if rms:
                        sp.wait_ge(row_ready, 3 * H * b + 3)
                    else:
                        sp.wait_ge(side_made, b + 1)
                    sp.sem_inc(passed_sp, 1)
                    load_side(nb, (b + 1) % 2)
                    sp.wait_ge(ctxN_split, b + 1)
                    load_N(nb)
                sp.wait_ge(ctxT_loaded, 16 * (NB + 1))
                sp.wait_ge(ctxN_loaded, 32 * (NB + 1))
                sp.wait_ge(side_loaded, (48 if rms else 16) * (NB + 1))

            @block.gpsimd
            def _(pool):
                if rms:
                    pool.memset(rT[:], 0.0).then_inc(zeroed, 1)
                else:
                    pool.memset(side[:, 0, 0:1], 0.0).then_inc(zeroed, 1)
                pool.memset(E[:], 0.0).then_inc(zeroed, 1)
                pool.memset(ctxN_raw[:, KB - 1, :], 0.0).then_inc(zeroed, 1)

            @block.tensor
            def _(pe):
                def row(n_G, h, c):
                    lo, w = CHUNKS[c]
                    n3 = 3 * (HG * n_G + h) + c
                    if not (isinstance(n3, int) and n3 == 0):
                        pe.wait_ge(row_copied, n3)
                    pe.matmul(row_ps[:, 0:w], sel[:, HG * group_of(n_G) + h, :], rT[:, batch_of(n_G) % 2, lo:lo + w],
                              start=True, stop=True).then_inc(row_ready, 1)

                def scores(G, h):
                    b = batch_of(G)
                    for c, (lo, w) in enumerate(CHUNKS):
                        n3 = 3 * h + c
                        if h == 0 and c == 0:
                            pe.wait_ge(ctxT_split, b + 1)
                        pe.wait_ge(qlo_s, HG * G + h + 1)
                        if not (isinstance(G, int) and G == 0 and n3 < 2):
                            pe.wait_ge(scores_taken, 12 * G + n3 - 1)
                        out = S_ps[n3 % 2][0:Q, 0:w]
                        hi, lo_ = ctxT_hi[:, b % 2, lo:lo + w], ctxT_lo[:, b % 2, lo:lo + w]
                        pe.matmul(out, q_hi[:, h, :], hi, start=True, stop=False)
                        pe.matmul(out, q_hi[:, h, :], lo_, start=False, stop=False)
                        pe.matmul(out, q_lo[:, h, :], hi, start=False, stop=True).then_inc(scores_ready, 1)
                        if rms:
                            if h == HG - 1:
                                row(G + 1, 0, c)
                            else:
                                row(G, h + 1, c)

                def q_natural(G):
                    pe.wait_ge(x_copied, G + 1)
                    if not (isinstance(G, int) and G < 2):
                        pe.wait_ge(y_added, 4 * (G - 2) + 1)
                    for c in range(DC):
                        ins = pe.matmul(misc[0:Q, :], xs[:, c, :],
                                        A[:, c, bass.ds(HG * group_of(G), HG), :].rearrange("p h n -> p (h n)"),
                                        start=(c == 0), stop=(c == DC - 1))
                    ins.then_inc(qnat_ready, 1)

                def q_turn(G):
                    pe.wait_ge(qn_scaled, G + 1)
                    if not (isinstance(G, int) and G == 0):
                        pe.wait_ge(q_copied, G)
                    for h in range(HG):
                        ins = pe.transpose(QT_ps[:, Q * h:Q * (h + 1)], qn[0:Q, h, :], ident[0:Q, 0:Q])
                    ins.then_inc(qT_ready, 1)

                def turn(G, h, t):
                    n3 = NT * h + t
                    if t == 0:
                        pe.wait_ge(exp_done, HG * G + h + 1)
                    if not (isinstance(G, int) and G == 0 and n3 < 2):
                        pe.wait_ge(elo_s, 12 * G + n3 - 1)
                    for j in range(TB):
                        ins = pe.transpose(T_ps[n3 % 2][:, 128 * j:128 * j + Q],
                                           E[0:Q, h, 128 * (TB * t + j):128 * (TB * t + j + 1)], ident[0:Q, 0:Q])
                    ins.then_inc(turned, 1)

                def context_product(G, t):
                    if t == 0:
                        pe.wait_ge(ctxN_split, batch_of(G) + 1)
                        pe.wait_ge(o_copied, G + 1)
                    pe.wait_ge(elo_s, 12 * G + 10 + t)
                    out = O_ps[:, 0:HG * Q]
                    for j in range(TB * t, TB * (t + 1)):
                        eh = e_hi[:, j, :, :].rearrange("p h q -> p (h q)")
                        el = e_lo[:, j, :, :].rearrange("p h q -> p (h q)")
                        pe.matmul(out, ctxN_hi[:, j, :], eh, start=(j == 0), stop=False)
                        pe.matmul(out, ctxN_hi[:, j, :], el, start=False, stop=False)
                        ins = pe.matmul(out, ctxN_lo[:, j, :], eh, start=False, stop=(j == KB - 1))
                    ins.then_inc(pv_thirds, 1)

                def project(G, pair):
                    if pair == 0:
                        pe.wait_ge(o_copied, G + 2)
                        pe.wait_ge(qn_scaled, G + 2)
                    else:
                        pe.wait_ge(y_added, 4 * G + 3)
                    for i in range(2):
                        h = 2 * pair + i
                        ins = pe.matmul(misc[0:Q, D * i:D * (i + 1)], OT[:, h, :], Bw[:, HG * group_of(G) + h, :],
                                        start=True, stop=True)
                    ins.then_inc(y_ready, 1)

                def step(G, lag):
                    scores(G, 0)
                    q_natural(G + 1)
                    if lag:
                        for t in range(NT):
                            turn(G - 1, 2, t)
                    q_turn(G + 1)
                    scores(G, 1)
                    if lag:
                        for t in range(NT):
                            turn(G - 1, 3, t)
                    scores(G, 2)
                    for t in range(NT):
                        if lag:
                            context_product(G - 1, t)
                        turn(G, 0, t)
                    scores(G, 3)
                    if lag:
                        project(G - 1, 0)
                    for t in range(NT):
                        turn(G, 1, t)
                    if lag:
                        project(G - 1, 1)

                def drain(G):
                    for h in (2, 3):
                        for t in range(NT):
                            turn(G - 1, h, t)
                    for t in range(NT):
                        context_product(G - 1, t)
                    for pair in range(2):
                        project(G - 1, pair)

                pe.sem_inc(y_ready, 1)
                q_natural(0)
                q_turn(0)
                if rms:
                    pe.wait_ge(side_loaded, 48)
                    for c in range(3):
                        row(0, 0, c)
                pe.wait_ge(zeroed, 3)

                def boundary(b):
                    if rms:
                        pe.wait_ge(side_loaded, 48 * (b + 2))
                        pe.sem_inc(passed_pe, 1)
                run(step, boundary, drain)(pe)

            @block.vector
            def _(dve):
                def split_T(b, slot):
                    dve.wait_ge(ctxT_hi_s, b + 1)
                    dve.tensor_tensor(ctxT_lo[:, slot, :], ctxT_raw[:], ctxT_hi[:, slot, :],
                                      ALU.subtract).then_inc(ctxT_split, 1)

                def make_side(b, slot):
                    dve.wait_ge(side_loaded, 16 * (b + 1))
                    dve.tensor_reduce(seen[0:Q, bass.ds(slot, 1)], mask_u8[0:Q, :], AX_X, ALU.max)
                    dve.tensor_scalar(side[0:Q, 0, :], mask_u8[0:Q, :], BIG, -BIG, ALU.mult, ALU.add)\
                       .then_inc(side_made, 1)
                    dve.wait_ge(side_made, b + 1)

                def split_N(b):
                    dve.wait_ge(ctxN_hi_s, b + 1)
                    dve.tensor_tensor(ctxN_lo[:], ctxN_raw[:], ctxN_hi[:], ALU.subtract).then_inc(ctxN_split, 1)

                def soft(G, h):
                    for c, (lo, w) in enumerate(CHUNKS):
                        n3 = 3 * h + c
                        dve.wait_ge(scores_ready, 12 * G + n3 + 1)
                        if rms:
                            dve.wait_ge(row_copied, 12 * G + n3 + 1)
                            in1 = side[0:Q, h % 2, lo:lo + w]
                        else:
                            in1 = side[0:Q, 0, lo:lo + w]
                        if c == 0 and not (isinstance(G, int) and G == 0):
                            dve.wait_ge(turned, 12 * (G - 1) + NT * (h + 1))
                        dve.sem_inc(passed, 1)
                        dve.tensor_tensor_reduce(E[0:Q, h, lo:lo + w], S_ps[n3 % 2][0:Q, 0:w], in1, 1.0, -3.0e38,
                                                 ALU.mult if rms else ALU.add, ALU.max,
                                                 mx[0:Q, h, c:c + 1]).then_inc(scores_taken, 1)
                    dve.wait_ge(scores_taken, 12 * G + 3 * (h + 1))
                    dve.tensor_reduce(negm[0:Q, h:h + 1], mx[0:Q, h, :], AX_X, ALU.max, negate=True)\
                       .then_inc(max_ready, 1)

                def scale_q(G):
                    dve.wait_ge(qnat_ready, G + 1)
                    if not (isinstance(G, int) and G == 0):
                        dve.wait_ge(qT_ready, G)
                    s = sc[0:Q, bass.ds(H * batch_of(G) + HG * group_of(G), HG)]
                    dve.tensor_tensor(qn[0:Q, :, :], misc[0:Q, :].rearrange("p (h n) -> p h n", h=HG),
                                      s.unsqueeze(2).to_broadcast([Q, HG, C]), ALU.mult).then_inc(qn_scaled, 1)

                def q_low(G, h):
                    dve.wait_ge(qhi_s, HG * G + h + 1)
                    dve.tensor_tensor(q_lo[:, h, :], qT[:, h, :], q_hi[:, h, :],
                                      ALU.subtract).then_inc(qlo_s, 1)

                def e_low(G, h, t):
                    n3 = NT * h + t
                    dve.wait_ge(ehi_s, 12 * G + n3 + 1)
                    dve.tensor_tensor(e_lo[:, TB * t:TB * (t + 1), h, :],
                                      T_ps[n3 % 2][:, :].rearrange("p (j q) -> p j q", j=TB)[:, :, 0:Q],
                                      e_hi[:, TB * t:TB * (t + 1), h, :], ALU.subtract).then_inc(elo_s, 1)

                def reciprocals(G):
                    dve.wait_ge(exp_done, HG * (G + 1))
                    dve.reciprocal(rden[0:Q, :], den[0:Q, bass.ds(HG * (G % 2), HG)]).then_inc(rden_s, 1)
                    if not rms:
                        dve.wait_ge(rden_s, 2 * G + 1)
                        dve.tensor_scalar(rden[0:Q, :], rden[0:Q, :], seen[0:Q, bass.ds(batch_of(G) % 2, 1)], None,
                                          ALU.mult).then_inc(rden_s, 1)

                def add_y(G, pair):
                    dve.wait_ge(y_ready, 2 * G + pair + 2)
                    if pair == 0:
                        dve.wait_ge(rden_s, (1 if rms else 2) * (G + 1))
                    for i in range(2):
                        h = 2 * pair + i
                        dve.wait_ge(y_added, 4 * G + h + 1)
                        x = X[0:Q, batch_of(G), :]
                        dve.scalar_tensor_tensor(out=x, in0=misc[0:Q, D * i:D * (i + 1)], scalar=rden[0:Q, h:h + 1],
                                                 in1=x, op0=ALU.mult, op1=ALU.add).then_inc(y_added, 1)

                def step(G, lag):
                    soft(G, 0)
                    scale_q(G + 1)
                    if lag:
                        for t in range(NT):
                            e_low(G - 1, 2, t)
                    soft(G, 1)
                    q_low(G + 1, 0)
                    if lag:
                        for t in range(NT):
                            e_low(G - 1, 3, t)
                        reciprocals(G - 1)
                    soft(G, 2)
                    q_low(G + 1, 1)
                    for t in range(NT):
                        e_low(G, 0, t)
                    soft(G, 3)
                    q_low(G + 1, 2)
                    if lag:
                        add_y(G - 1, 0)
                    for t in range(NT):
                        e_low(G, 1, t)
                    q_low(G + 1, 3)
                    if lag:
                        add_y(G - 1, 1)

                def drain(G):
                    for h in (2, 3):
                        for t in range(NT):
                            e_low(G - 1, h, t)
                    reciprocals(G - 1)
                    for pair in range(2):
                        add_y(G - 1, pair)
                    dve.wait_ge(y_added, 4 * G + 1)

                def boundary(b):
                    split_N(b)
                    split_T(b + 1, (b + 1) % 2)

                def first(b):
                    if not rms:
                        make_side(b, b % 2)

                dve.sem_inc(y_added, 1)
                split_T(0, 0)
                scale_q(0)
                for h in range(HG):
                    q_low(0, h)
                run(step, boundary, drain, first)(dve)

            @block.scalar
            def _(act):
                def split_T(b, slot):
                    act.wait_ge(ctxT_loaded, 16 * (b + 1))
                    act.activation(ctxT_hi[:, slot, :], ctxT_raw[:], ACT.Copy).then_inc(ctxT_hi_s, 1)

                def split_N(b):
                    act.wait_ge(ctxN_loaded, 32 * (b + 1))
                    if not (isinstance(b, int) and b == 0):
                        act.wait_ge(pv_thirds, NT * NG * b)
                    act.activation(ctxN_hi[:], ctxN_raw[:], ACT.Copy).then_inc(ctxN_hi_s, 1)

                def copy_x(G):
                    if not (isinstance(G, int) and G == 0):
                        act.wait_ge(qnat_ready, G)
                    act.activation(xs[:], xnT[:, :, batch_of(G), :], ACT.Copy).then_inc(x_copied, 1)

                def copy_row(G, h):
                    if not rms:
                        return
                    for c, (lo, w) in enumerate(CHUNKS):
                        n3 = 3 * h + c
                        act.wait_ge(row_ready, 12 * G + n3 + 1)
                        if not (isinstance(G, int) and G == 0 and n3 < 6):
                            act.wait_ge(scores_taken, 12 * G + n3 - 5)
                        act.activation(side[0:Q, h % 2, lo:lo + w], row_ps[0:Q, 0:w], ACT.Copy)\
                           .then_inc(row_copied, 1)

                def exps(G, h):
                    act.wait_ge(max_ready, HG * G + h + 1)
                    act.activation(E[0:Q, h, 0:KEYS], E[0:Q, h, 0:KEYS], ACT.Exp, bias=negm[0:Q, h:h + 1],
                                   accum_out=den[0:Q, bass.ds(HG * (G % 2) + h, 1)]).then_inc(exp_done, 1)

                def copy_q(G):
                    act.wait_ge(qT_ready, G + 1)
                    if not (isinstance(G, int) and G == 0):
                        act.wait_ge(qlo_s, HG * G)
                    act.activation(qT[:].rearrange("p h q -> p (h q)"), QT_ps[:, 0:HG * Q], ACT.Copy)\
                       .then_inc(q_copied, 1)
                    act.wait_ge(q_copied, G + 1)

                def q_high(G, h):
                    if not (isinstance(G, int) and G == 0):
                        act.wait_ge(scores_ready, 12 * (G - 1) + 3 * (h + 1))
                    act.activation(q_hi[:, h, :], qT[:, h, :], ACT.Copy).then_inc(qhi_s, 1)

                def e_high(G, h, t):
                    n3 = NT * h + t
                    act.wait_ge(turned, 12 * G + n3 + 1)
                    if h == 0 and not (isinstance(G, int) and G == 0):
                        act.wait_ge(pv_thirds, NT * (G - 1) + t + 1)
                    act.activation(e_hi[:, TB * t:TB * (t + 1), h, :],
                                   T_ps[n3 % 2][:, :].rearrange("p (j q) -> p j q", j=TB)[:, :, 0:Q],
                                   ACT.Copy).then_inc(ehi_s, 1)

                def copy_o(G):
                    act.wait_ge(pv_thirds, NT * (G + 1))
                    act.wait_ge(y_ready, 2 * G + 1)
                    act.activation(OT[:].rearrange("p h q -> p (h q)"), O_ps[:, 0:HG * Q], ACT.Copy)\
                       .then_inc(o_copied, 1)

                def step(G, lag):
                    copy_x(G + 1)
                    copy_row(G, 1)
                    if lag:
                        for t in range(NT):
                            e_high(G - 1, 2, t)
                    exps(G, 0)
                    copy_q(G + 1)
                    q_high(G + 1, 0)
                    copy_row(G, 2)
                    if lag:
                        for t in range(NT):
                            e_high(G - 1, 3, t)
                    exps(G, 1)
                    q_high(G + 1, 1)
                    copy_row(G, 3)
                    exps(G, 2)
                    for t in range(NT):
                        e_high(G, 0, t)
                    if lag:
                        copy_o(G - 1)
                    q_high(G + 1, 2)
                    copy_row(G + 1, 0)
                    for t in range(NT):
                        e_high(G, 1, t)
                    exps(G, 3)
                    q_high(G + 1, 3)

                def drain(G):
                    for h in (2, 3):
                        for t in range(NT):
                            e_high(G - 1, h, t)
                    copy_o(G - 1)

                def boundary(b):
                    split_N(b)
                    split_T(b + 1, (b + 1) % 2)

                act.sem_inc(o_copied, 1)
                act.wait_ge(zeroed, 3)
                copy_x(0)
                split_T(0, 0)
                copy_q(0)
                for h in range(HG):
                    q_high(0, h)
                copy_row(0, 0)
                run(step, boundary, drain)(act)
    k.phase = k.whole


def ternary_phase(k, X, ident, xnT, wT_in, rT_in):
    nc = k.nc
    win, w_s, mm, added = k.sem("ffn_in"), k.sem("ffn_w"), k.sem("ffn_mm"), k.sem("ffn_added")
    with ExitStack() as k.phase:
        w, r = k.sb("ffn_wt", [128, DC, D]), k.sb("ffn_r", [128, DC, D])
        a, b2 = k.sb("ffn_a", [128, DC, D]), k.sb("ffn_b", [128, DC, D])
        ps = k.ps("ffn_ps", [128, NB, 512])
        with nc.Block() as block:
            @block.sync
            def _(sp):
                sp.dma_start(w[:], wT_in).then_inc(win, 16)
                sp.dma_start(r[:], rT_in).then_inc(win, 16)

            @block.vector
            def _(dve):
                chain = Count(w_s)
                dve.wait_ge(win, 32)
                chain.by(dve.tensor_scalar(a[:], w[:], 0.2, 0.6, ALU.is_gt, ALU.mult))
                chain.then_wait(dve, dve.tensor_scalar(b2[:], w[:], -0.2, 0.6, ALU.is_lt, ALU.mult))
                chain.then_wait(dve, dve.tensor_tensor(a[:], a[:], b2[:], ALU.subtract))
                chain.by(dve.tensor_tensor(w[:], a[:], r[:], ALU.add))
                for b in range(NB):
                    dve.wait_ge(mm, b + 1)
                    dve.tensor_tensor(X[0:Q, b, :], X[0:Q, b, :], ps[0:Q, b, 0:D],
                                      ALU.add).then_inc(added, 1)
                dve.wait_ge(added, NB)

            @block.tensor
            def _(pe):
                pe.wait_ge(w_s, 4)
                for b in range(NB):
                    for c in range(DC):
                        ins = pe.matmul(ps[0:Q, b, 0:D], xnT[:, c, b, :], w[:, c, :],
                                        start=(c == 0), stop=(c == DC - 1))
                    ins.then_inc(mm, 1)
    k.phase = k.whole


def ternary(dve, chain, xn, u, w):
    chain.by(dve.tensor_scalar(u[0:Q], xn[0:Q], 0.33, 0.5, ALU.is_gt, ALU.mult))
    chain.then_wait(dve, dve.tensor_scalar(w[0:Q], xn[0:Q], -0.33, 0.5, ALU.is_lt, ALU.mult))
    chain.then_wait(dve, dve.tensor_tensor(xn[0:Q], u[0:Q], w[0:Q], ALU.subtract))


def query_norm_phase(k, xnT, Wq_in, sc):
    nc = k.nc
    win, mm, sq_s, red_s, root_s, dve_s = (k.sem(f"qn_{n}") for n in ("in", "mm", "sq", "red", "root", "dve"))
    with ExitStack() as k.phase:
        Wq = k.sb("qn_W", [128, DC, H * HD])
        sq = k.sb("qn_sqb", [128, 4, 512])
        ss, root, t = k.sb("qn_ss", [128, NB * H]), k.sb("qn_rootv", [128, NB * H]), k.sb("qn_t", [128, NB * H])
        ps = k.ps("qn_ps", [128, 4, 512])
        with nc.Block() as block:
            @block.sync
            def _(sp):
                for c in range(DC):
                    sp.dma_start(Wq[:, c, :], Wq_in[:, c, :]).then_inc(win, 16)

            @block.tensor
            def _(pe):
                pe.wait_ge(win, 32)
                for b in range(NB):
                    for g in range(NG):
                        n = NG * b + g
                        if n >= 4:
                            pe.wait_ge(sq_s, n - 3)
                        for c in range(DC):
                            ins = pe.matmul(ps[0:Q, n % 4, :], xnT[:, c, b, :], Wq[:, c, 512 * g:512 * (g + 1)],
                                            start=(c == 0), stop=(c == DC - 1))
                        ins.then_inc(mm, 1)

            @block.scalar
            def _(act):
                for n in range(STEPS):
                    act.wait_ge(mm, n + 1)
                    if n >= 4:
                        act.wait_ge(red_s, n - 3)
                    act.activation(sq[0:Q, n % 4, :], ps[0:Q, n % 4, :], ACT.Square).then_inc(sq_s, 1)
                act.wait_ge(dve_s, 1)
                act.activation(root[0:Q, :], ss[0:Q, :], ACT.Sqrt).then_inc(root_s, 1)

            @block.vector
            def _(dve):
                for n in range(STEPS):
                    dve.wait_ge(sq_s, n + 1)
                    dve.tensor_reduce(ss[0:Q, HG * n:HG * (n + 1)],
                                      sq[0:Q, n % 4, :].rearrange("p (h d) -> p h d", h=HG), AX_X,
                                      ALU.add).then_inc(red_s, 1)
                dve.wait_ge(red_s, STEPS)
                chain = Count(dve_s)
                chain.then_wait(dve, dve.tensor_scalar(ss[0:Q, :], ss[0:Q, :], 1.0 / HD, LN_EPS, ALU.mult, ALU.add))
                dve.wait_ge(root_s, 1)
                newton_rsqrt(dve, chain, ss[0:Q, :], root[0:Q, :], sc[0:Q, :], t[0:Q, :])
                chain.then_wait(dve, dve.tensor_scalar(sc[0:Q, :], sc[0:Q, :], INV, None, ALU.mult))
    k.phase = k.whole


def key_norm_phase(k, ident, ctxT_in, Wk_in, rT_out):
    nc = k.nc
    sem = lambda n: k.sem(f"kn_{n}")
    win, whi, wlo = sem("w_in"), sem("w_hi"), sem("w_lo")
    raw_in, chi, clo, mm, sq_s, red_s = (sem(n) for n in ("raw_in", "ctx_hi", "ctx_lo", "mm", "sq", "red"))
    zero_s, root_s, var_s, chain_s, turned, parts_s, stored = (
        sem(n) for n in ("zero", "root", "var", "chain", "turned", "parts", "stored"))
    W = H * HD
    NCH = W // 512
    with ExitStack() as k.phase:
        Wk, Wk_hi, Wk_lo = k.sb("kn_W", [128, W]), k.sb("kn_Wh", [128, W], F32R), k.sb("kn_Wl", [128, W], F32R)
        raw = k.sb("kn_raw", [128, 2, KB * 128])
        c_hi, c_lo = k.sb("kn_ch", [128, KB, 128], F32R), k.sb("kn_cl", [128, KB, 128], F32R)
        sq = k.sb("kn_sqb", [128, 4, 512])
        ss, root, r, t = (k.sb(f"kn_{n}", [128, KB, H]) for n in ("ss", "rootv", "r", "t"))
        rows, p1f = k.sb("kn_rows", [128, KEYS]), k.sb("kn_p1f", [128, KEYS])
        parts = k.sb("kn_partsb", [128, 3, KEYS], BF16)
        ps = k.ps("kn_ps", [128, 4, 512])
        tp = k.ps("kn_tp", [128, 3, 512])
        with nc.Block() as block:
            @block.gpsimd
            def _(pool):
                pool.memset(raw[:], 0.0).then_inc(zero_s, 1)

            @block.sync
            def _(sp):
                sp.dma_start(Wk[:], Wk_in).then_inc(win, 16)
                sp.sem_inc(stored, 1)
                sp.wait_ge(zero_s, 1)
                sp.dma_start(raw[:, 0, 0:KEYS], ctxT_in[0]).then_inc(raw_in, 16)
                with sp.Fori(0, NB) as b:
                    sp.wait_ge(clo, KB * b + 1)
                    sp.dma_start(raw[:, (b + 1) % 2, 0:KEYS], ctxT_in[(b + 1) % NB]).then_inc(raw_in, 16)
                    sp.wait_ge(parts_s, 5 * b + 6)
                    for i in range(3):
                        sp.dma_start(rT_out[b, i], parts[0:H, i, :]).then_inc(stored, 16)
                sp.wait_ge(stored, 48 * NB + 1)
                sp.wait_ge(raw_in, 16 * (NB + 1))

            @block.tensor
            def _(pe):
                pe.wait_ge(wlo, 1)
                with pe.Fori(0, NB) as b:
                    for j in range(KB):
                        pe.wait_ge(clo, KB * b + j + 1)
                        for m in range(NCH):
                            n = NCH * j + m
                            out = ps[:, n % 4, :]
                            pe.wait_ge(sq_s, NCH * KB * b + n + 1)
                            ws = slice(512 * m, 512 * (m + 1))
                            pe.matmul(out, c_hi[:, j, :], Wk_hi[:, ws], start=True, stop=False)
                            pe.matmul(out, c_hi[:, j, :], Wk_lo[:, ws], start=False, stop=False)
                            pe.matmul(out, c_lo[:, j, :], Wk_hi[:, ws], start=False, stop=True).then_inc(mm, 1)
                    pe.wait_ge(chain_s, 5 * b + 5)
                    pe.wait_ge(parts_s, 5 * b + 1)
                    for j in range(KB):
                        ins = pe.transpose(tp[0:H, j // 4, 128 * (j % 4):128 * (j % 4 + 1)], r[:, j, :], ident[:])
                    ins.then_inc(turned, 1)

            @block.scalar
            def _(act):
                act.wait_ge(win, 16)
                act.activation(Wk_hi[:], Wk[:], ACT.Copy).then_inc(whi, 1)
                for i in range(4):
                    act.activation(sq[:, i, 0:1], Wk[:, 0:1], ACT.Copy).then_inc(sq_s, 1)
                with act.Fori(0, NB) as b:
                    act.wait_ge(raw_in, 16 * (b + 1))

                    def split(j):
                        act.activation(c_hi[:, j, :], raw[:, b % 2, 128 * j:128 * (j + 1)], ACT.Copy)\
                           .then_inc(chi, 1)

                    split(0)
                    for j in range(KB):
                        if j + 1 < KB:
                            split(j + 1)
                        for m in range(NCH):
                            n = NCH * j + m
                            act.wait_ge(mm, NCH * KB * b + n + 1)
                            act.wait_ge(red_s, NCH * KB * b + n + 1)
                            act.activation(sq[:, n % 4, :], ps[:, n % 4, :], ACT.Square).then_inc(sq_s, 1)
                    act.wait_ge(var_s, b + 1)
                    act.activation(root[:], ss[:], ACT.Sqrt).then_inc(root_s, 1)

            @block.vector
            def _(dve):
                dve.wait_ge(whi, 1)
                dve.tensor_tensor(Wk_lo[:], Wk[:], Wk_hi[:], ALU.subtract).then_inc(wlo, 1)
                dve.sem_inc(parts_s, 1)
                dve.wait_ge(sq_s, 4)
                for i in range(4):
                    dve.memset(t[:, 0, i:i + 1], 0.0).then_inc(red_s, 1)
                with dve.Fori(0, NB) as b:

                    def split(j):
                        dve.wait_ge(chi, KB * b + j + 1)
                        dve.tensor_tensor(c_lo[:, j, :], raw[:, b % 2, 128 * j:128 * (j + 1)], c_hi[:, j, :],
                                          ALU.subtract).then_inc(clo, 1)

                    split(0)
                    for j in range(KB):
                        if j + 1 < KB:
                            split(j + 1)
                        for m in range(NCH):
                            n = NCH * j + m
                            dve.wait_ge(sq_s, NCH * KB * b + n + 5)
                            dve.tensor_reduce(ss[:, j, HG * m:HG * (m + 1)],
                                              sq[:, n % 4, :].rearrange("p (h d) -> p h d", h=HG), AX_X,
                                              ALU.add).then_inc(red_s, 1)
                    dve.wait_ge(red_s, NCH * KB * (b + 1) + 4)
                    dve.tensor_scalar(ss[:], ss[:], 1.0 / HD, LN_EPS, ALU.mult, ALU.add).then_inc(var_s, 1)
                    dve.wait_ge(root_s, b + 1)
                    dve.wait_ge(var_s, b + 1)
                    dve.reciprocal(r[:], root[:]).then_inc(chain_s, 1)
                    dve.wait_ge(chain_s, 5 * b + 1)
                    dve.tensor_tensor(t[:], r[:], r[:], ALU.mult).then_inc(chain_s, 1)
                    dve.wait_ge(chain_s, 5 * b + 2)
                    dve.tensor_tensor(t[:], t[:], ss[:], ALU.mult).then_inc(chain_s, 1)
                    dve.wait_ge(chain_s, 5 * b + 3)
                    dve.tensor_scalar(t[:], t[:], -0.5, 1.5, ALU.mult, ALU.add).then_inc(chain_s, 1)
                    dve.wait_ge(chain_s, 5 * b + 4)
                    dve.tensor_tensor(r[:], r[:], t[:], ALU.mult).then_inc(chain_s, 1)
                    dve.wait_ge(turned, b + 1)
                    dve.wait_ge(stored, 48 * b + 1)
                    rt = tp[0:H, :, :].rearrange("p a n -> p (a n)")[:, 0:KEYS]
                    dve.tensor_copy(parts[0:H, 0, :], rt).then_inc(parts_s, 1)
                    dve.wait_ge(parts_s, 5 * b + 2)
                    dve.tensor_tensor(rows[0:H, :], rt, parts[0:H, 0, :], ALU.subtract).then_inc(parts_s, 1)
                    dve.wait_ge(parts_s, 5 * b + 3)
                    dve.tensor_copy(parts[0:H, 1, :], rows[0:H, :]).then_inc(parts_s, 1)
                    dve.wait_ge(parts_s, 5 * b + 4)
                    dve.tensor_tensor(p1f[0:H, :], rows[0:H, :], parts[0:H, 1, :], ALU.subtract).then_inc(parts_s, 1)
                    dve.wait_ge(parts_s, 5 * b + 5)
                    dve.tensor_copy(parts[0:H, 2, :], p1f[0:H, :]).then_inc(parts_s, 1)
    k.phase = k.whole


E_ALL = 64 + 2
ROUTED = 64
TOPK = 6
FFN = 176
FC = 88
NF = FFN // FC
TOK = NB * Q
TC = 2
TW = TOK // TC


def router_phase(k, xn, xnT, ident, gateT_in, comb, combT_out):
    nc = k.nc
    sem = lambda n: k.sem(f"rt_{n}")
    gin, mm, chain_s, exp_s, turned, row_s, stored, neg_s = (
        sem(n) for n in ("in", "mm", "chain", "exp", "turned", "row", "stored", "neg"))
    with ExitStack() as k.phase:
        gate = k.sb("rt_gate", [128, DC, ROUTED])
        neg, Z, p = k.sb("rt_negm", [128, NB]), k.sb("rt_Z", [128, NB]), k.sb("rt_p", [128, NB, ROUTED])
        top, rest = k.sb("rt_top", [128, NB, 8]), k.sb("rt_rest", [128, NB, ROUTED])
        tot = k.sb("rt_tot", [128, NB])
        rows = k.sb("rt_rows", [128, NB, Q])
        ps = k.ps("rt_ps", [128, NB, ROUTED])
        tp = k.ps("rt_tp", [128, 2, 512])
        with nc.Block() as block:
            @block.sync
            def _(sp):
                sp.dma_start(gate[:], gateT_in).then_inc(gin, 16)
                sp.wait_ge(row_s, 3)
                sp.dma_start(combT_out, rows[0:E_ALL, :, :].rearrange("p b q -> p (b q)")).then_inc(stored, 16)
                sp.wait_ge(stored, 16)

            @block.tensor
            def _(pe):
                pe.wait_ge(gin, 16)
                for b in range(NB):
                    for c in range(DC):
                        ins = pe.matmul(ps[0:Q, b, :], xnT[:, c, b, :], gate[:, c, :],
                                        start=(c == 0), stop=(c == DC - 1))
                ins.then_inc(mm, 1)
                pe.wait_ge(neg_s, 2)
                for b in range(NB):
                    ins = pe.transpose(tp[0:E_ALL, b // 4, 128 * (b % 4):128 * (b % 4) + Q], comb[0:Q, b, :],
                                       ident[0:Q, 0:Q])
                ins.then_inc(turned, 1)

            @block.scalar
            def _(act):
                act.wait_ge(neg_s, 1)
                for b in range(NB):
                    act.activation(p[0:Q, b, :], ps[0:Q, b, :], ACT.Exp, bias=neg[0:Q, b:b + 1],
                                   accum_out=Z[0:Q, b:b + 1]).then_inc(exp_s, 1)

            @block.vector
            def _(dve):
                chain = Count(chain_s)
                dve.wait_ge(mm, 1)
                dve.tensor_reduce(neg[0:Q, :], ps[0:Q, :, :], AX_X, ALU.max, negate=True).then_inc(neg_s, 1)
                dve.wait_ge(exp_s, NB)
                chain.then_wait(dve, dve.reciprocal(Z[0:Q, :], Z[0:Q, :]))
                for b in range(NB):
                    chain.by(dve.tensor_scalar(p[0:Q, b, :], p[0:Q, b, :], Z[0:Q, b:b + 1], None, ALU.mult))
                dve.wait_ge(chain_s, chain.n)
                for b in range(NB):
                    chain.by(dve.max(top[0:Q, b, :], p[0:Q, b, :]))
                dve.wait_ge(chain_s, chain.n)
                chain.by(dve.tensor_reduce(tot[0:Q, :], top[0:Q, :, 0:TOPK], AX_X, ALU.add))
                chain.then_wait(dve, dve.memset(top[0:Q, :, TOPK:8], -1.0))
                for b in range(NB):
                    chain.by(dve.match_replace(rest[0:Q, b, :], top[0:Q, b, :], p[0:Q, b, :], 0.0))
                dve.wait_ge(chain_s, chain.n)
                chain.then_wait(dve, dve.tensor_scalar(tot[0:Q, :], tot[0:Q, :], 1e-20, None, ALU.add))
                chain.then_wait(dve, dve.reciprocal(tot[0:Q, :], tot[0:Q, :]))
                chain.then_wait(dve, dve.tensor_tensor(p[0:Q, :, :], p[0:Q, :, :], rest[0:Q, :, :], ALU.subtract))
                for b in range(NB):
                    chain.by(dve.tensor_scalar(comb[0:Q, b, 0:ROUTED], p[0:Q, b, :], tot[0:Q, b:b + 1], None,
                                               ALU.mult))
                chain.by(dve.memset(comb[0:Q, :, ROUTED:E_ALL], 1.0))
                dve.wait_ge(chain_s, chain.n)
                dve.tensor_copy(tot[0:Q, :], Z[0:Q, :]).then_inc(neg_s, 1)
                dve.wait_ge(turned, 1)
                for i in range(2):
                    dve.tensor_copy(rows[0:E_ALL, 4 * i:4 * i + 4, :],
                                    tp[0:E_ALL, i, :].rearrange("p (b q) -> p b q", b=4)[:, :, 0:Q])\
                       .then_inc(row_s, 1)
                dve.wait_ge(row_s, 2)
                dve.tensor_copy(rows[0:1, 0, 0:1], rows[0:1, 0, 0:1]).then_inc(row_s, 1)
    k.phase = k.whole


def experts_phase(k, X, xnT, ident, wgu_in, wd_in, combT_in, out):
    nc = k.nc
    sem = lambda n: k.sem(f"ex_{n}")
    w_in = [sem("w_in0"), sem("w_in1")]
    gu_s, silu_s, up_s, act_s, down_s, z_s, sum_s, turned, added, stored = (
        sem(n) for n in ("gu", "silu", "up", "act", "down", "z", "sum", "turned", "added", "stored"))
    xT = xnT[:].rearrange("p c b q -> p c (b q)")
    with ExitStack() as k.phase:
        wgu, wd = k.sb("ex_wgu", [128, 2, DC, 2 * FFN]), k.sb("ex_wd", [128, 2, NF, D])
        cb = k.sb("ex_cb", [128, 2, TOK])
        silu, a = k.sb("ex_silu", [128, 2, TW]), k.sb("ex_a", [128, 2, TW])
        yT = k.sb("ex_yT", [128, DC, TOK])
        zero = k.sb("ex_zero", [128, 128])
        acc = k.ps("ex_acc", [128, DC * TC, 512])
        gu = k.ps("ex_gu", [128, 4, 512])
        SUB = TC * NF
        with nc.Block() as block:
            @block.sync
            def _(sp):
                def load(e, slot):
                    sp.dma_start(wgu[:, slot], wgu_in[e]).then_inc(w_in[slot], 16)
                    sp.dma_start(wd[0:FC, slot], wd_in[e]).then_inc(w_in[slot], 16)
                    sp.dma_start(cb[:, slot, :], combT_in[e].partition_broadcast(128)).then_inc(w_in[slot], 16)
                load(0, 0)
                load(1, 1)
                with sp.Fori(1, E_ALL // 2) as pair:
                    for s in range(2):
                        sp.wait_ge(down_s, 2 + SUB * (2 * pair + s - 1))
                        load(2 * pair + s, s)
                for b in range(NB):
                    sp.wait_ge(added, b + 1)
                    sp.dma_start(out[b], X[0:Q, b, :]).then_inc(stored, 16)
                sp.wait_ge(stored, 16 * NB)

            @block.tensor
            def _(pe):
                pe.wait_ge(z_s, 1)
                for i in range(DC * TC):
                    pe.matmul(acc[:, i, 0:TW], zero[:], xT[:, 0, 0:TW], start=True, stop=False, skip_group_check=True)
                for i in range(2):
                    pe.matmul(gu[:, i, 0:2], zero[:], zero[:, 0:2], start=True, stop=True).then_inc(down_s, 1)

                with pe.Fori(0, E_ALL // 2) as pair:
                    for s in range(2):
                        n0 = SUB * (2 * pair + s)

                        def up(i):
                            t, f = divmod(i, NF)
                            if i == 0:
                                pe.wait_ge(w_in[s], 48 * (pair + 1))
                            pe.wait_ge(act_s, n0 + i + 1)
                            for half in range(2):
                                for c in range(DC):
                                    m0 = FFN * half + FC * f
                                    ins = pe.matmul(gu[0:FC, 2 * (i % 2) + half, 0:TW], wgu[:, s, c, m0:m0 + FC],
                                                    xT[:, c, TW * t:TW * (t + 1)], start=(c == 0), stop=(c == DC - 1))
                            ins.then_inc(gu_s, 1)

                        def down(i):
                            t, f = divmod(i, NF)
                            pe.wait_ge(act_s, n0 + i + 3)
                            for c in range(DC):
                                ins = pe.matmul(acc[:, DC * t + c, 0:TW], wd[0:FC, s, f, 128 * c:128 * (c + 1)],
                                                a[0:FC, i % 2, :], start=False, stop=False, skip_group_check=True)
                            ins.then_inc(down_s, 1)

                        for i in range(SUB):
                            up(i)
                            if i:
                                down(i - 1)
                        down(SUB - 1)
                pe.wait_ge(sum_s, DC * TC)
                for b in range(NB):
                    if b >= 4:
                        pe.wait_ge(added, b - 3)
                    for c in range(DC):
                        ins = pe.transpose(gu[0:Q, b % 4, 128 * c:128 * (c + 1)], yT[:, c, Q * b:Q * (b + 1)],
                                           ident[:])
                    ins.then_inc(turned, 1)

            @block.scalar
            def _(act):
                with act.Fori(0, E_ALL) as e:
                    for i in range(SUB):
                        act.wait_ge(gu_s, SUB * e + i + 1)
                        act.wait_ge(act_s, SUB * e + i + 1)
                        act.activation(silu[0:FC, i % 2, :], gu[0:FC, 2 * (i % 2), 0:TW], ACT.Silu).then_inc(silu_s, 1)

            @block.vector
            def _(dve):
                dve.memset(zero[:], 0.0).then_inc(z_s, 1)
                for i in range(2):
                    dve.memset(a[:, i, :], 0.0).then_inc(act_s, 1)
                with dve.Fori(0, E_ALL // 2) as pair:
                    for s, i in ((s, i) for s in range(2) for i in range(SUB)):
                        t, f = divmod(i, NF)
                        n = SUB * (2 * pair + s) + i
                        dve.wait_ge(silu_s, n + 1)
                        if i == 0:
                            dve.wait_ge(w_in[s], 48 * (pair + 1))
                        dve.tensor_tensor(silu[0:FC, i % 2, :], silu[0:FC, i % 2, :],
                                          cb[0:FC, s, TW * t:TW * (t + 1)], ALU.mult).then_inc(up_s, 1)
                        dve.wait_ge(up_s, n + 1)
                        dve.wait_ge(down_s, n + 1)
                        dve.tensor_tensor(a[0:FC, i % 2, :], gu[0:FC, 2 * (i % 2) + 1, 0:TW], silu[0:FC, i % 2, :],
                                          ALU.mult).then_inc(act_s, 1)
                dve.wait_ge(down_s, 2 + SUB * E_ALL)
                for t in range(TC):
                    for c in range(DC):
                        dve.tensor_copy(yT[:, c, TW * t:TW * (t + 1)], acc[:, DC * t + c, 0:TW]).then_inc(sum_s, 1)
                for b in range(NB):
                    dve.wait_ge(turned, b + 1)
                    dve.tensor_tensor(X[0:Q, b, :], X[0:Q, b, :], gu[0:Q, b % 4, 0:D], ALU.add).then_inc(added, 1)
    k.phase = k.whole


def program(nc, a, out, upto=9):
    with ExitStack() as whole:
        k = Core(nc, whole)
        X, ident = k.sb("X", [128, NB, D]), k.sb("ident", [128, 128])
        sel = k.sb("sel", [128, H, 128], BF16)
        sc = k.sb("sc", [128, NB * H])
        rT = nc.dram_tensor("r_rows", (NB, 3, H, KEYS), BF16).ap()
        combT = nc.dram_tensor("comb_rows", (E_ALL, TOK), F32).ap()
        xnT = k.sb("xnT", [128, DC, NB, Q])
        sc_made = k.sem("sc_made")
        setup_phase(k, a["x"], X, ident, sel)
        with nc.Block() as block:
            @block.vector
            def _(dve):
                dve.memset(sc[:], INV).then_inc(sc_made, 1)

        for layer, kv in ((0, H // 2), (1, H)):
            t = f"l{layer}"
            if upto <= 2 * layer: break
            with ExitStack() as k.whole_layer:
                A = k.whole_layer.enter_context(nc.sbuf_tensor(f"{t}_A", [128, DC, H, C], F32))
                Bw = k.whole_layer.enter_context(nc.sbuf_tensor(f"{t}_B", [128, H, D], F32))
                if layer:
                    key_norm_phase(k, ident, a["ctxT"], a["Wk1"], rT)
                combine_phase(k, f"{t}c", kv, a[f"WqT{layer}"], a[f"WkT{layer}"], a[f"WvT{layer}"], a[f"Wo{layer}"],
                              (a["gq"], a["gk"]) if layer else None, A, Bw)
                with nc.sbuf_tensor(f"{t}_xn", [128, NB, D], F32) as xn:
                    norm_phase(k, f"{t}n", X, ident, xn, xnT)
                if layer:
                    query_norm_phase(k, xnT, a["Wq1"], sc)
                attention_phase(k, t, bool(layer), X, xnT, ident, sel, A, Bw, sc, a["ctxT"], a["ctxN"],
                                a["mask"], rT)
            if upto <= 2 * layer + 1: break
            if layer == 0:
                with nc.sbuf_tensor("f0_xn", [128, NB, D], F32) as xn:
                    norm_phase(k, "f0", X, ident, xn, xnT, after=ternary)
                ternary_phase(k, X, ident, xnT, a["wT"], a["rramT"])
            else:
                with nc.sbuf_tensor("m1_xn", [128, NB, D], F32) as xn, \
                        nc.sbuf_tensor("m1_comb", [128, NB, E_ALL], F32) as comb:
                    norm_phase(k, "m1", X, ident, xn, xnT)
                    router_phase(k, xn, xnT, ident, a["gateT"], comb, combT)
                    experts_phase(k, X, xnT, ident, a["wgu"], a["wd"], combT, out)
        if upto < 9:
            s = k.sem("dbg")
            with nc.Block() as block:
                @block.sync
                def _(sp):
                    sp.dma_start(out.rearrange("b q d -> q b d"), X[0:Q]).then_inc(s, 16)
                    sp.wait_ge(s, 16)


def laid_out(i):
    import numpy as np

    def heads_T(w, n):
        return np.ascontiguousarray(w.reshape(w.shape[0], n, HD).transpose(2, 1, 0))

    a = {"x": i["x"], "ctxN": i["ctx_1024"], "ctxT": np.ascontiguousarray(i["ctx_1024"].transpose(0, 2, 1)),
         "mask": i["mask_BxS2_bf1"].view(np.uint8)}
    for layer, kv in ((0, H // 2), (1, H)):
        w = {n: i[f"L{layer}_xattn_{n}"] for n in ("Wq", "Wk", "Wv", "Wo")}
        a[f"WqT{layer}"] = heads_T(w["Wq"], H)
        a[f"WkT{layer}"] = heads_T(w["Wk"], kv)
        a[f"WvT{layer}"] = heads_T(w["Wv"], kv)
        a[f"Wo{layer}"] = np.ascontiguousarray(w["Wo"].reshape(H, HD, D).transpose(1, 0, 2))
    a["Wq1"] = np.ascontiguousarray(i["L1_xattn_Wq"].reshape(DC, 128, H * HD).transpose(1, 0, 2))
    a["Wk1"] = i["L1_xattn_Wk"]
    a["gq"], a["gk"] = i["L1_xattn_gq"].reshape(HD, 1), i["L1_xattn_gk"].reshape(HD, 1)
    for n, m in (("wT", "weight"), ("rramT", "rram_variation")):
        a[n] = np.ascontiguousarray(i[f"L0_ffn_{m}"].T.reshape(DC, 128, D).transpose(1, 0, 2))
    a["gateT"] = np.ascontiguousarray(i["L1_ffn_gate_w"].T.reshape(DC, 128, ROUTED).transpose(1, 0, 2))
    sgu = i["L1_ffn_ws_gate_up"].reshape(2, 2, FFN, D).transpose(1, 0, 2, 3).reshape(2, 2 * FFN, D)
    gu = np.concatenate([i["L1_ffn_w_gate_up"], sgu])
    a["wgu"] = np.ascontiguousarray(gu.transpose(0, 2, 1).reshape(E_ALL, DC, 128, 2 * FFN).transpose(0, 2, 1, 3))
    down = np.concatenate([i["L1_ffn_w_down"], i["L1_ffn_ws_down"].reshape(D, 2, FFN).transpose(1, 0, 2)])
    a["wd"] = np.ascontiguousarray(down.transpose(0, 2, 1).reshape(E_ALL, NF, FC, D).transpose(0, 2, 1, 3))
    return {n: np.ascontiguousarray(v) for n, v in a.items()}


def kernel(**inputs):
    import numpy as np
    import concourse.bacc as bacc
    from concourse.bass_utils import run_bass_kernel_spmd

    arrays = laid_out({n: np.asarray(v) for n, v in inputs.items()})
    nc = bacc.Bacc("TRN2", target_bir_lowering=False, num_devices=1)
    aps = {n: nc.dram_tensor(f"in_{n}", v.shape, mybir.dt.from_np(v.dtype), kind="ExternalInput").ap()
           for n, v in arrays.items()}
    out = nc.dram_tensor("out", (NB, Q, D), F32, kind="ExternalOutput").ap()
    program(nc, aps, out)
    r = run_bass_kernel_spmd(nc, [{f"in_{n}": v for n, v in arrays.items()}], core_ids=[0])
    return r.results[0]["out"]
```

```python
from contextlib import ExitStack

import concourse.bass as bass
from concourse import mybir

F32 = mybir.dt.float32
F32R = mybir.dt.float32r
BF16 = mybir.dt.bfloat16
U8 = mybir.dt.uint8
U32 = mybir.dt.uint32
I32 = mybir.dt.int32
ALU = mybir.AluOpType
ACT = mybir.ActivationFunctionType
AX_X = mybir.AxisListType.X

NB = 8
Q = 100
D = 256
DC = D // 128
C = 128
KEYS = 1444
H = 16
HD = 128
KB = -(-KEYS // 128)
KT = KEYS - (KB - 1) * 128
HG = 4
NG = H // HG
STEPS = NB * NG
CHUNKS = [(0, 512), (512, 512), (1024, KEYS - 1024)]
TB = 4
NT = KB // TB
SLOTS = 3 * HG
INV = float(HD) ** -0.5
BIG = 1.0e30
LN_EPS = 1e-5


class Count:

    def __init__(self, sem):
        self.sem, self.n = sem, 0

    def by(self, instruction, step=1):
        instruction.then_inc(self.sem, step)
        self.n += step

    def then_wait(self, engine, instruction, step=1):
        self.by(instruction, step)
        engine.wait_ge(self.sem, self.n)


class Core:

    def __init__(self, nc, whole):
        self.nc, self.whole, self.phase = nc, whole, whole
        self.layer, self.sems = ExitStack(), []

    def sem(self, name):
        self.sems.append(self.layer.enter_context(self.nc.semaphore(name)))
        return self.sems[-1]

    def end_layer(self, wait_for=()):
        with self.nc.Block() as block:
            @block.gpsimd
            def _(pool):
                for s, n in wait_for:
                    pool.wait_ge(s, n)
                for s in self.sems:
                    pool.sem_clear(s)
        self.layer.close()
        self.layer, self.sems = ExitStack(), []

    def sb(self, name, shape, dt=F32):
        return self.phase.enter_context(self.nc.sbuf_tensor(name, shape, dt))

    def ps(self, name, shape, dt=F32):
        return self.phase.enter_context(self.nc.psum_tensor(name, shape, dt))


def newton_rsqrt(dve, chain, v, root, r, t):
    chain.then_wait(dve, dve.reciprocal(r, root))
    chain.then_wait(dve, dve.tensor_tensor(t, r, r, ALU.mult))
    chain.then_wait(dve, dve.tensor_tensor(t, t, v, ALU.mult))
    chain.then_wait(dve, dve.tensor_scalar(t, t, -0.5, 1.5, ALU.mult, ALU.add))
    chain.then_wait(dve, dve.tensor_tensor(r, r, t, ALU.mult))


def setup_phase(k, x_in, X, ident, sel):
    nc = k.nc
    loaded, made = k.sem("x_loaded"), k.sem("consts_made")
    with nc.Block() as block:
        @block.sync
        def _(sp):
            sp.dma_start(X[0:Q, :, :], x_in.rearrange("b q d -> q b d")).then_inc(loaded, 16)
            sp.wait_ge(loaded, 16)

        @block.gpsimd
        def _(pool):
            chain = Count(made)
            chain.by(pool.memset(sel[:], 0.0))
            chain.then_wait(pool, pool.memset(ident[:], 0.0))
            chain.then_wait(pool, pool.affine_select(out=ident[:], in_=ident[:], compare_op=ALU.not_equal, fill=1.0,
                                                     base=0, pattern=[[-1, 128]], channel_multiplier=1))
            for part in range(3):
                chain.then_wait(pool, pool.affine_select(
                    out=sel[:], in_=sel[:], compare_op=ALU.not_equal, fill=1.0,
                    base=-32 * part, pattern=[[-1, H], [0, 128]], channel_multiplier=1))


def norm_phase(k, tag, X, ident, xn, xnT, after=None):
    nc = k.nc
    dve_s, root_s, var_s = k.sem(f"{tag}_dve"), k.sem(f"{tag}_root"), k.sem(f"{tag}_var")
    tr_s, out_s = k.sem(f"{tag}_turned"), k.sem(f"{tag}_taken")
    with ExitStack() as k.phase:
        stats, mv = k.sb(f"{tag}_stats", [128, NB, 6]), k.sb(f"{tag}_mv", [128, NB, 2])
        var, root = k.sb(f"{tag}_varr", [128, NB]), k.sb(f"{tag}_rootv", [128, NB])
        rstd, t = k.sb(f"{tag}_rstd", [128, NB]), k.sb(f"{tag}_t", [128, NB])
        u, w = k.sb(f"{tag}_u", [128, NB, D]), k.sb(f"{tag}_w", [128, NB, D])
        turned = k.ps(f"{tag}_ps", [128, 4, 512])
        with nc.Block() as block:
            @block.vector
            def _(dve):
                chain = Count(dve_s)
                for b in range(NB):
                    chain.by(dve.bn_stats(stats[0:Q, b, :], X[0:Q, b, :]))
                dve.wait_ge(dve_s, chain.n)
                for b in range(NB):
                    chain.by(dve.bn_aggr(mv[0:Q, b, :], stats[0:Q, b, :]))
                dve.wait_ge(dve_s, chain.n)
                dve.tensor_scalar(var[0:Q, :], mv[0:Q, :, 1], LN_EPS, None, ALU.add).then_inc(var_s, 1)
                dve.wait_ge(root_s, 1)
                dve.wait_ge(var_s, 1)
                newton_rsqrt(dve, chain, var[0:Q, :], root[0:Q, :], rstd[0:Q, :], t[0:Q, :])
                for b in range(NB):
                    ins = dve.tensor_scalar(xn[0:Q, b, :], X[0:Q, b, :], mv[0:Q, b, 0:1], rstd[0:Q, b:b + 1],
                                            ALU.subtract, ALU.mult)
                    chain.by(ins)
                dve.wait_ge(dve_s, chain.n)
                if after:
                    after(dve, chain, xn, u, w)
                dve.tensor_copy(t[0:Q, :], rstd[0:Q, :]).then_inc(var_s, 1)
                for i in range(NB * DC // 4):
                    dve.wait_ge(tr_s, i + 1)
                    for j in range(4):
                        b, c = divmod(4 * i + j, DC)
                        ins = dve.tensor_copy(xnT[:, c, b, :], turned[:, i, 128 * j:128 * j + Q])
                    ins.then_inc(out_s, 1)
                dve.wait_ge(out_s, NB * DC // 4)

            @block.scalar
            def _(act):
                act.wait_ge(var_s, 1)
                act.activation(root[0:Q, :], var[0:Q, :], ACT.Sqrt).then_inc(root_s, 1)

            @block.tensor
            def _(pe):
                pe.wait_ge(var_s, 2)
                for i in range(NB * DC // 4):
                    for j in range(4):
                        b, c = divmod(4 * i + j, DC)
                        ins = pe.transpose(turned[:, i, 128 * j:128 * j + Q], xn[0:Q, b, 128 * c:128 * (c + 1)],
                                           ident[0:Q, 0:Q])
                    ins.then_inc(tr_s, 1)
    k.phase = k.whole


def combine_phase(k, tag, kv, WqT_in, WkT_in, WvT_in, Wo_in, gains, A, Bw):
    nc = k.nc
    gain_s = k.sem(f"{tag}_gain")
    wk_in, wv_in = k.sem(f"{tag}_wk_in"), k.sem(f"{tag}_wv_in")
    wq_in, wo_in = ([k.sem(f"{tag}_{n}_in{i}") for i in range(2)] for n in ("wq", "wo"))
    mm_s, out_s = k.sem(f"{tag}_mm"), k.sem(f"{tag}_out")
    gin = k.sem(f"{tag}_gin")
    with ExitStack() as k.phase:
        WqT, WkT = k.sb(f"{tag}_WqT", [128, H, D]), k.sb(f"{tag}_WkT", [128, kv, C])
        WvT, Wo = k.sb(f"{tag}_WvT", [128, kv, C]), k.sb(f"{tag}_Wo", [128, H, D])
        g = k.sb(f"{tag}_g", [128, 3])
        ps = k.ps(f"{tag}_ps", [128, 8, 512])
        with nc.Block() as block:
            @block.sync
            def _(sp):
                sp.dma_start(WkT[:], WkT_in).then_inc(wk_in, 16)
                if gains:
                    for i in range(2):
                        sp.dma_start(g[:, i:i + 1], gains[i]).then_inc(gin, 16)
                for half in range(2):
                    hs = slice(half * H // 2, (half + 1) * H // 2)
                    sp.dma_start(WqT[:, hs, :], WqT_in[:, hs, :]).then_inc(wq_in[half], 16)
                sp.dma_start(WvT[:], WvT_in).then_inc(wv_in, 16)
                for half in range(2):
                    hs = slice(half * H // 2, (half + 1) * H // 2)
                    sp.dma_start(Wo[:, hs, :], Wo_in[:, hs, :]).then_inc(wo_in[half], 16)

            @block.gpsimd
            def _(pool):
                if gains:
                    pool.wait_ge(gin, 32)
                    pool.tensor_tensor(g[:, 2:3], g[:, 0:1], g[:, 1:2], ALU.mult).then_inc(gain_s, 1)
                    pool.wait_ge(gain_s, 1)
                    pool.wait_ge(wk_in, 16)
                    pool.tensor_scalar(WkT[:], WkT[:], g[:, 2:3], None, ALU.mult).then_inc(gain_s, 1)

            @block.tensor
            def _(pe):
                pe.wait_ge(wk_in, 16)
                if gains:
                    pe.wait_ge(gain_s, 2)
                for h in range(H):
                    pe.wait_ge(wq_in[h // (H // 2)], 16)
                    if h >= 8:
                        pe.wait_ge(out_s, h - 7)
                    for c in range(DC):
                        ins = pe.matmul(ps[:, h % 8, C * c:C * (c + 1)], WqT[:, h, 128 * c:128 * (c + 1)],
                                        WkT[:, h * kv // H, :], start=True, stop=True)
                    ins.then_inc(mm_s, 1)
                pe.wait_ge(wv_in, 16)
                for h in range(H):
                    pe.wait_ge(wo_in[h // (H // 2)], 16)
                    pe.wait_ge(out_s, H + h - 7)
                    pe.matmul(ps[:, h % 8, 0:D], WvT[:, h * kv // H, :], Wo[:, h, :],
                              start=True, stop=True).then_inc(mm_s, 1)

            @block.vector
            def _(dve):
                for h in range(H):
                    dve.wait_ge(mm_s, h + 1)
                    dve.tensor_copy(A[:, :, h, :], ps[:, h % 8, 0:DC * C].rearrange("p (c n) -> p c n", c=DC))\
                       .then_inc(out_s, 1)
                for h in range(H):
                    dve.wait_ge(mm_s, H + h + 1)
                    dve.tensor_copy(Bw[:, h, :], ps[:, h % 8, 0:D]).then_inc(out_s, 1)
    k.phase = k.whole


def attention_phase(k, tag, rms, X, xnT, ident, sel, A, Bw, sc, ctxT_in, ctxN_in, mask_in, rT_in):
    nc = k.nc
    sem = lambda name: k.sem(f"{tag}_{name}")
    ctxT_loaded, ctxN_loaded, side_loaded = sem("ctxT_loaded"), sem("ctxN_loaded"), sem("side_loaded")
    ctxT_hi_s, ctxT_split = sem("ctxT_hi"), sem("ctxT_split")
    ctxN_hi_s, ctxN_split = sem("ctxN_hi"), sem("ctxN_split")
    side_made = sem("side_made")
    x_copied, qnat_ready, qn_scaled, qT_ready, q_copied, qhi_s, qlo_s = (
        sem(n) for n in ("x_copied", "qnat_ready", "qn_scaled", "qT_ready", "q_copied", "qhi", "qlo"))
    row_ready, row_copied = sem("row_ready"), sem("row_copied")
    scores_ready, scores_taken, max_ready, exp_done = (
        sem(n) for n in ("scores_ready", "scores_taken", "max_ready", "exp_done"))
    turned, ehi_s, elo_s = sem("turned"), sem("ehi"), sem("elo")
    pv_thirds, o_copied, y_ready, y_added, rden_s = (
        sem(n) for n in ("pv_thirds", "o_copied", "y_ready", "y_added", "rden"))
    zeroed, passed, passed_pe, passed_sp = (sem(n) for n in ("zeroed", "passed", "passed_pe", "passed_sp"))

    with ExitStack() as k.phase:
        sb, ps = (lambda n, s, d=F32: k.sb(f"{tag}_{n}", s, d)), (lambda n: k.ps(f"{tag}_{n}", [128, 512]))
        ctxT_raw, ctxN_raw = sb("ctxT_raw", [128, KEYS]), sb("ctxN_raw", [128, KB, C])
        ctxT_hi, ctxT_lo = sb("ctxT_hi", [128, 2, KEYS], F32R), sb("ctxT_lo", [128, 2, KEYS], F32R)
        ctxN_hi, ctxN_lo = sb("ctxN_hi", [128, KB, C], F32R), sb("ctxN_lo", [128, KB, C], F32R)
        xs = sb("xs", [128, DC, Q])
        qn, qT = sb("qn", [128, HG, C]), sb("qT", [128, HG, Q])
        q_hi, q_lo = sb("q_hi", [128, HG, Q], F32R), sb("q_lo", [128, HG, Q], F32R)
        E = sb("E", [128, HG, KB * 128])
        e_hi, e_lo = sb("e_hi", [128, KB, HG, Q], F32R), sb("e_lo", [128, KB, HG, Q], F32R)
        side = sb("side", [128, 2, KEYS])
        mx, negm, den = sb("mx", [128, HG, 3]), sb("negm", [128, HG]), sb("den", [128, 2 * HG * 3])
        rden = sb("rden", [128, HG])
        OT = sb("OT", [128, HG, Q])
        if rms:
            rT = sb("rT", [128, 2, KEYS], BF16)
        else:
            mask_u8 = sb("mask_u8", [128, KEYS], U8)
            seen = sb("seen", [128, 2])
        S_ps = [ps("S0"), ps("S1")]
        T_ps = [ps("T0"), ps("T1"), ps("T2")]
        O_ps, row_ps, misc = ps("O"), ps("row"), ps("misc")

        def batch_of(G):
            return (G % STEPS) // NG

        def group_of(G):
            return G % NG

        def run(eng, step, drain):
            step(0, False, True)
            with eng.Fori(1, NG) as g:
                step(g, True, False)
            with eng.Fori(1, NB) as b:
                step(NG * b, True, True)
                with eng.Fori(1, NG) as g:
                    step(NG * b + g, True, False)
            drain(STEPS)

        with nc.Block() as block:
            @block.sync
            def _(sp):
                def load_T(b):
                    sp.dma_start(ctxT_raw[:], ctxT_in[b]).then_inc(ctxT_loaded, 16)

                def load_N(b):
                    n = (KB - 1) * 128
                    sp.dma_start(ctxN_raw[:, 0:KB - 1, :], ctxN_in[b, 0:n, :].rearrange("(j p) c -> p j c", p=128))\
                      .then_inc(ctxN_loaded, 16)
                    sp.dma_start(ctxN_raw[0:KT, KB - 1, :], ctxN_in[b, n:KEYS, :]).then_inc(ctxN_loaded, 16)

                def load_side(b, slot):
                    if rms:
                        for part in range(3):
                            sp.dma_start(rT[32 * part:32 * part + H, slot, :], rT_in[b, part])\
                              .then_inc(side_loaded, 16)
                    else:
                        sp.dma_start(mask_u8[0:Q, :], mask_in[b].partition_broadcast(Q)).then_inc(side_loaded, 16)

                if rms:
                    sp.wait_ge(zeroed, 1)
                load_T(0)
                load_side(0, 0)
                sp.wait_ge(zeroed, 3)
                load_N(0)
                with sp.Fori(0, NB) as b:
                    nb = (b + 1) % NB
                    sp.wait_ge(ctxT_split, 3 * (b + 1))
                    load_T(nb)
                    if rms:
                        sp.wait_ge(row_ready, 3 * H * b + 3)
                    else:
                        sp.wait_ge(side_made, b + 1)
                    sp.sem_inc(passed_sp, 1)
                    load_side(nb, (b + 1) % 2)
                    sp.wait_ge(ctxN_split, 3 * (b + 1))
                    load_N(nb)
                sp.wait_ge(ctxT_loaded, 16 * (NB + 1))
                sp.wait_ge(ctxN_loaded, 32 * (NB + 1))
                sp.wait_ge(side_loaded, (48 if rms else 16) * (NB + 1))

            @block.gpsimd
            def _(pool):
                if rms:
                    pool.memset(rT[:], 0.0).then_inc(zeroed, 1)
                else:
                    pool.memset(side[:, 0, 0:1], 0.0).then_inc(zeroed, 1)
                pool.memset(E[:], 0.0).then_inc(zeroed, 1)
                pool.memset(ctxN_raw[:, KB - 1, :], 0.0).then_inc(zeroed, 1)

            @block.tensor
            def _(pe):
                def row(n_G, h, c):
                    lo, w = CHUNKS[c]
                    n3 = 3 * (HG * n_G + h) + c
                    if not (isinstance(n3, int) and n3 == 0):
                        pe.wait_ge(row_copied, n3)
                    pe.matmul(row_ps[:, 0:w], sel[:, HG * group_of(n_G) + h, :], rT[:, batch_of(n_G) % 2, lo:lo + w],
                              start=True, stop=True).then_inc(row_ready, 1)

                def scores(G, h, c):
                    b = batch_of(G)
                    lo, w = CHUNKS[c]
                    n3 = 3 * h + c
                    if h == 0:
                        pe.wait_ge(ctxT_split, 3 * b + c + 1)
                    if c == 0:
                        pe.wait_ge(qlo_s, HG * G + h + 1)
                    if not (isinstance(G, int) and G == 0 and n3 < 2):
                        pe.wait_ge(scores_taken, 12 * G + n3 - 1)
                    out = S_ps[n3 % 2][0:Q, 0:w]
                    hi, lo_ = ctxT_hi[:, b % 2, lo:lo + w], ctxT_lo[:, b % 2, lo:lo + w]
                    pe.matmul(out, q_hi[:, h, :], hi, start=True, stop=False)
                    pe.matmul(out, q_hi[:, h, :], lo_, start=False, stop=False)
                    pe.matmul(out, q_lo[:, h, :], hi, start=False, stop=True).then_inc(scores_ready, 1)
                    if rms:
                        if h == HG - 1:
                            row(G + 1, 0, c)
                        else:
                            row(G, h + 1, c)

                def q_natural(G, c):
                    if c == 0:
                        pe.wait_ge(x_copied, G + 1)
                        if not (isinstance(G, int) and G < 2):
                            pe.wait_ge(y_added, 4 * (G - 2) + 1)
                    ins = pe.matmul(misc[0:Q, :], xs[:, c, :],
                                    A[:, c, bass.ds(HG * group_of(G), HG), :].rearrange("p h n -> p (h n)"),
                                    start=(c == 0), stop=(c == DC - 1))
                    if c == DC - 1:
                        ins.then_inc(qnat_ready, 1)

                def q_turn(G):
                    pe.wait_ge(qn_scaled, G + 1)
                    for h in range(HG):
                        ins = pe.transpose(misc[:, Q * h:Q * (h + 1)], qn[0:Q, h, :], ident[0:Q, 0:Q])
                    ins.then_inc(qT_ready, 1)

                def turn(G, h, t):
                    n3 = NT * h + t
                    pe.wait_ge(exp_done, 12 * G + n3 + 1)
                    if not (isinstance(G, int) and G == 0 and n3 < 3):
                        pe.wait_ge(elo_s, 12 * G + n3 - 2)
                    for j in range(TB):
                        ins = pe.transpose(T_ps[n3 % 3][:, 128 * j:128 * j + Q],
                                           E[0:Q, h, 128 * (TB * t + j):128 * (TB * t + j + 1)], ident[0:Q, 0:Q])
                    ins.then_inc(turned, 1)

                def context_product(G, t):
                    if t == 0:
                        pe.wait_ge(y_added, 4 * G + 1)
                    pe.wait_ge(ctxN_split, 3 * batch_of(G) + t + 1)
                    pe.wait_ge(elo_s, 12 * G + 10 + t)
                    out = O_ps[:, 0:HG * Q]
                    for j in range(TB * t, TB * (t + 1)):
                        eh = e_hi[:, j, :, :].rearrange("p h q -> p (h q)")
                        el = e_lo[:, j, :, :].rearrange("p h q -> p (h q)")
                        pe.matmul(out, ctxN_hi[:, j, :], eh, start=(j == 0), stop=False)
                        pe.matmul(out, ctxN_hi[:, j, :], el, start=False, stop=False)
                        ins = pe.matmul(out, ctxN_lo[:, j, :], eh, start=False, stop=(j == KB - 1))
                    ins.then_inc(pv_thirds, 1)

                def project(G, pair):
                    if pair == 0:
                        pe.wait_ge(o_copied, G + 2)
                        pe.wait_ge(q_copied, G + 2)
                    for i in range(2):
                        h = 2 * pair + i
                        ins = pe.matmul((misc, O_ps)[pair][0:Q, D * i:D * (i + 1)], OT[:, h, :], Bw[:, HG * group_of(G) + h, :],
                                        start=True, stop=True)
                    ins.then_inc(y_ready, 1)

                def step(G, lag, new):
                    for s in range(SLOTS):
                        h, c = divmod(s, 3)
                        if rms and new and s == 9:
                            pe.wait_ge(side_loaded, 48 * (batch_of(G) + 2))
                            pe.sem_inc(passed_pe, 1)
                        scores(G, h, c)
                        if s in (1, 2):
                            q_natural(G + 1, s - 1)
                        if s == 5:
                            q_turn(G + 1)
                        if lag and s in (6, 7, 8):
                            context_product(G - 1, s - 6)
                        if lag and s == 11:
                            for pair in range(2):
                                project(G - 1, pair)
                        if s >= 6 or lag:
                            turn(G - (s < 6), (h + 2) % HG, c)

                def drain(G):
                    for h in (2, 3):
                        for t in range(NT):
                            turn(G - 1, h, t)
                    for t in range(NT):
                        context_product(G - 1, t)
                    for pair in range(2):
                        project(G - 1, pair)

                pe.sem_inc(y_ready, 1)
                q_natural(0, 0)
                q_natural(0, 1)
                q_turn(0)
                if rms:
                    pe.wait_ge(side_loaded, 48)
                    for c in range(3):
                        row(0, 0, c)
                pe.wait_ge(zeroed, 3)

                run(pe, step, drain)

            @block.vector
            def _(dve):
                def split_T(b, slot, c):
                    lo, w = CHUNKS[c]
                    dve.wait_ge(ctxT_hi_s, 3 * b + c + 1)
                    dve.tensor_tensor(ctxT_lo[:, slot, lo:lo + w], ctxT_raw[:, lo:lo + w],
                                      ctxT_hi[:, slot, lo:lo + w], ALU.subtract).then_inc(ctxT_split, 1)

                def make_side(b, slot):
                    dve.wait_ge(side_loaded, 16 * (b + 1))
                    dve.tensor_reduce(seen[0:Q, bass.ds(slot, 1)], mask_u8[0:Q, :], AX_X, ALU.max)
                    dve.tensor_scalar(side[0:Q, 0, :], mask_u8[0:Q, :], BIG, -BIG, ALU.mult, ALU.add)\
                       .then_inc(side_made, 1)
                    dve.wait_ge(side_made, b + 1)

                def split_N(b, t):
                    js = slice(TB * t, TB * (t + 1))
                    dve.wait_ge(ctxN_hi_s, 3 * b + t + 1)
                    dve.tensor_tensor(ctxN_lo[:, js, :], ctxN_raw[:, js, :], ctxN_hi[:, js, :],
                                      ALU.subtract).then_inc(ctxN_split, 1)

                def soft(G, h, c):
                    lo, w = CHUNKS[c]
                    n3 = 3 * h + c
                    dve.wait_ge(scores_ready, 12 * G + n3 + 1)
                    if rms:
                        dve.wait_ge(row_copied, 12 * G + n3 + 1)
                    if c == 0 and not (isinstance(G, int) and G == 0):
                        dve.wait_ge(turned, 12 * (G - 1) + NT * (h + 1))
                    dve.sem_inc(passed, 1)
                    dve.tensor_tensor_reduce(E[0:Q, h, lo:lo + w], S_ps[n3 % 2][0:Q, 0:w],
                                             side[0:Q, h % 2 if rms else 0, lo:lo + w], 1.0, -3.0e38,
                                             ALU.mult if rms else ALU.add, ALU.max,
                                             mx[0:Q, h, c:c + 1]).then_inc(scores_taken, 1)

                def maximum(G, h):
                    dve.wait_ge(scores_taken, 12 * G + 3 * (h + 1))
                    dve.tensor_reduce(negm[0:Q, h:h + 1], mx[0:Q, h, :], AX_X, ALU.max, negate=True)\
                       .then_inc(max_ready, 1)

                def scale_q(G):
                    dve.wait_ge(qnat_ready, G + 1)
                    if not (isinstance(G, int) and G == 0):
                        dve.wait_ge(qT_ready, G)
                    s = sc[0:Q, bass.ds(H * batch_of(G) + HG * group_of(G), HG)]
                    dve.tensor_tensor(qn[0:Q, :, :], misc[0:Q, :].rearrange("p (h n) -> p h n", h=HG),
                                      s.unsqueeze(2).to_broadcast([Q, HG, C]), ALU.mult).then_inc(qn_scaled, 1)

                def q_low(G, h):
                    dve.wait_ge(qhi_s, HG * G + h + 1)
                    dve.tensor_tensor(q_lo[:, h, :], qT[:, h, :], q_hi[:, h, :],
                                      ALU.subtract).then_inc(qlo_s, 1)

                def e_low(G, h, t):
                    n3 = NT * h + t
                    dve.wait_ge(ehi_s, 12 * G + n3 + 1)
                    dve.tensor_tensor(e_lo[:, TB * t:TB * (t + 1), h, :],
                                      T_ps[n3 % 3][:, :].rearrange("p (j q) -> p j q", j=TB)[:, :, 0:Q],
                                      e_hi[:, TB * t:TB * (t + 1), h, :], ALU.subtract).then_inc(elo_s, 1)

                def reciprocals(G):
                    k_s = 2 if rms else 3
                    dve.wait_ge(exp_done, 12 * (G + 1))
                    dve.tensor_reduce(rden[0:Q, :], den[0:Q, bass.ds(12 * (G % 2), 12)]
                                      .rearrange("p (h c) -> p h c", c=3), AX_X, ALU.add).then_inc(rden_s, 1)
                    dve.wait_ge(rden_s, k_s * G + 1)
                    dve.reciprocal(rden[0:Q, :], rden[0:Q, :]).then_inc(rden_s, 1)
                    if not rms:
                        dve.wait_ge(rden_s, k_s * G + 2)
                        dve.tensor_scalar(rden[0:Q, :], rden[0:Q, :], seen[0:Q, bass.ds(batch_of(G) % 2, 1)], None,
                                          ALU.mult).then_inc(rden_s, 1)

                def add_y(G, pair):
                    dve.wait_ge(y_ready, 2 * G + pair + 2)
                    if pair == 0:
                        dve.wait_ge(rden_s, (2 if rms else 3) * (G + 1))
                    for i in range(2):
                        h = 2 * pair + i
                        dve.wait_ge(y_added, 4 * G + h + 1)
                        x = X[0:Q, batch_of(G), :]
                        dve.scalar_tensor_tensor(out=x, in0=(misc, O_ps)[pair][0:Q, D * i:D * (i + 1)], scalar=rden[0:Q, h:h + 1],
                                                 in1=x, op0=ALU.mult, op1=ALU.add).then_inc(y_added, 1)

                def step(G, lag, new):
                    if new and not rms:
                        make_side(batch_of(G), batch_of(G) % 2)
                    for s in range(SLOTS):
                        h, c = divmod(s, 3)
                        soft(G, h, c)
                        if c == 2:
                            maximum(G, h)
                        if s == 3:
                            scale_q(G + 1)
                        if s >= 7:
                            e_low(G, (s - 7) // 3, (s - 7) % 3)
                        elif lag:
                            e_low(G - 1, (s + 5) // 3, (s + 5) % 3)
                        if s in (6, 8, 11):
                            q_low(G + 1, {6: 0, 8: 1, 11: 2}[s])
                        if lag and s == 6:
                            reciprocals(G - 1)
                        if lag and s == 11:
                            add_y(G - 1, 0)
                        if new and s in (6, 7, 8):
                            split_T(batch_of(G) + 1, (batch_of(G) + 1) % 2, s - 6)
                        if new and s >= 9:
                            split_N(batch_of(G), s - 9)
                    if lag:
                        add_y(G - 1, 1)
                    q_low(G + 1, 3)

                def drain(G):
                    for i in range(5, 12):
                        e_low(G - 1, i // 3, i % 3)
                    reciprocals(G - 1)
                    for pair in range(2):
                        add_y(G - 1, pair)
                    dve.wait_ge(y_added, 4 * G + 1)

                dve.sem_inc(y_added, 1)
                for c in range(3):
                    split_T(0, 0, c)
                scale_q(0)
                for h in range(HG):
                    q_low(0, h)
                dve.wait_ge(zeroed, 3)
                run(dve, step, drain)

            @block.scalar
            def _(act):
                def split_T(b, slot, c):
                    lo, w = CHUNKS[c]
                    act.wait_ge(ctxT_loaded, 16 * (b + 1))
                    act.activation(ctxT_hi[:, slot, lo:lo + w], ctxT_raw[:, lo:lo + w], ACT.Copy)\
                       .then_inc(ctxT_hi_s, 1)

                def split_N(b, t):
                    js = slice(TB * t, TB * (t + 1))
                    act.wait_ge(ctxN_loaded, 32 * (b + 1))
                    if not (isinstance(b, int) and b == 0):
                        act.wait_ge(pv_thirds, NT * NG * b)
                    act.activation(ctxN_hi[:, js, :], ctxN_raw[:, js, :], ACT.Copy).then_inc(ctxN_hi_s, 1)

                def copy_x(G):
                    if not (isinstance(G, int) and G == 0):
                        act.wait_ge(qnat_ready, G)
                    act.activation(xs[:], xnT[:, :, batch_of(G), :], ACT.Copy).then_inc(x_copied, 1)

                def copy_row(G, h, c):
                    if not rms:
                        return
                    lo, w = CHUNKS[c]
                    n3 = 3 * h + c
                    act.wait_ge(row_ready, 12 * G + n3 + 1)
                    if not (isinstance(G, int) and G == 0 and n3 < 6):
                        act.wait_ge(scores_taken, 12 * G + n3 - 5)
                    act.activation(side[0:Q, h % 2, lo:lo + w], row_ps[0:Q, 0:w], ACT.Copy)\
                       .then_inc(row_copied, 1)

                def exps(G, h, c):
                    lo, w = CHUNKS[c]
                    if c == 0:
                        act.wait_ge(max_ready, HG * G + h + 1)
                    act.activation(E[0:Q, h, lo:lo + w], E[0:Q, h, lo:lo + w], ACT.Exp, bias=negm[0:Q, h:h + 1],
                                   accum_out=den[0:Q, bass.ds(12 * (G % 2) + 3 * h + c, 1)]).then_inc(exp_done, 1)

                def copy_q(G):
                    act.wait_ge(qT_ready, G + 1)
                    if not (isinstance(G, int) and G == 0):
                        act.wait_ge(qlo_s, HG * G)
                    act.activation(qT[:].rearrange("p h q -> p (h q)"), misc[:, 0:HG * Q], ACT.Copy)\
                       .then_inc(q_copied, 1)
                    act.wait_ge(q_copied, G + 1)

                def q_high(G, h):
                    if not (isinstance(G, int) and G == 0):
                        act.wait_ge(scores_ready, 12 * (G - 1) + 3 * (h + 1))
                    act.activation(q_hi[:, h, :], qT[:, h, :], ACT.Copy).then_inc(qhi_s, 1)

                def e_high(G, h, t):
                    n3 = NT * h + t
                    act.wait_ge(turned, 12 * G + n3 + 1)
                    if h == 0 and not (isinstance(G, int) and G == 0):
                        act.wait_ge(pv_thirds, NT * (G - 1) + t + 1)
                    act.activation(e_hi[:, TB * t:TB * (t + 1), h, :],
                                   T_ps[n3 % 3][:, :].rearrange("p (j q) -> p j q", j=TB)[:, :, 0:Q],
                                   ACT.Copy).then_inc(ehi_s, 1)

                def copy_o(G):
                    act.wait_ge(pv_thirds, NT * (G + 1))
                    act.wait_ge(y_ready, 2 * G + 1)
                    act.activation(OT[:].rearrange("p h q -> p (h q)"), O_ps[:, 0:HG * Q], ACT.Copy)\
                       .then_inc(o_copied, 1)

                def step(G, lag, new):
                    copy_x(G + 1)
                    for s in range(SLOTS):
                        h, c = divmod(s, 3)
                        if h == HG - 1:
                            copy_row(G + 1, 0, c)
                        else:
                            copy_row(G, h + 1, c)
                        if s >= 6 or lag:
                            e_high(G - (s < 6), (h + 2) % HG, c)
                        if s >= 3:
                            exps(G, h - 1, c)
                        elif lag:
                            exps(G - 1, HG - 1, c)
                        if s == 5:
                            copy_q(G + 1)
                        if s in (5, 7, 10):
                            q_high(G + 1, {5: 0, 7: 1, 10: 2}[s])
                        if lag and s == 9:
                            copy_o(G - 1)
                        if new and s in (5, 6, 7):
                            split_T(batch_of(G) + 1, (batch_of(G) + 1) % 2, s - 5)
                        if new and s >= 9:
                            split_N(batch_of(G), s - 9)
                    q_high(G + 1, 3)

                def drain(G):
                    for c in range(3):
                        exps(G - 1, HG - 1, c)
                    for i in range(6, 12):
                        e_high(G - 1, i // 3, i % 3)
                    copy_o(G - 1)

                act.sem_inc(o_copied, 1)
                act.wait_ge(zeroed, 3)
                copy_x(0)
                for c in range(3):
                    split_T(0, 0, c)
                copy_q(0)
                for h in range(HG):
                    q_high(0, h)
                for c in range(3):
                    copy_row(0, 0, c)
                run(act, step, drain)
    k.phase = k.whole


def ternary_phase(k, X, ident, xnT, wT_in, rT_in):
    nc = k.nc
    win, w_s, mm, added = k.sem("ffn_in"), k.sem("ffn_w"), k.sem("ffn_mm"), k.sem("ffn_added")
    with ExitStack() as k.phase:
        w, r = k.sb("ffn_wt", [128, DC, D]), k.sb("ffn_r", [128, DC, D])
        a, b2 = k.sb("ffn_a", [128, DC, D]), k.sb("ffn_b", [128, DC, D])
        ps = k.ps("ffn_ps", [128, NB, 512])
        with nc.Block() as block:
            @block.sync
            def _(sp):
                sp.dma_start(w[:], wT_in).then_inc(win, 16)
                sp.dma_start(r[:], rT_in).then_inc(win, 16)

            @block.vector
            def _(dve):
                chain = Count(w_s)
                dve.wait_ge(win, 32)
                chain.by(dve.tensor_scalar(a[:], w[:], 0.2, 0.6, ALU.is_gt, ALU.mult))
                chain.then_wait(dve, dve.tensor_scalar(b2[:], w[:], -0.2, 0.6, ALU.is_lt, ALU.mult))
                chain.then_wait(dve, dve.tensor_tensor(a[:], a[:], b2[:], ALU.subtract))
                chain.by(dve.tensor_tensor(w[:], a[:], r[:], ALU.add))
                for b in range(NB):
                    dve.wait_ge(mm, b + 1)
                    dve.tensor_tensor(X[0:Q, b, :], X[0:Q, b, :], ps[0:Q, b, 0:D],
                                      ALU.add).then_inc(added, 1)
                dve.wait_ge(added, NB)

            @block.tensor
            def _(pe):
                pe.wait_ge(w_s, 4)
                for b in range(NB):
                    for c in range(DC):
                        ins = pe.matmul(ps[0:Q, b, 0:D], xnT[:, c, b, :], w[:, c, :],
                                        start=(c == 0), stop=(c == DC - 1))
                    ins.then_inc(mm, 1)
    k.phase = k.whole


def ternary(dve, chain, xn, u, w):
    chain.by(dve.tensor_scalar(u[0:Q], xn[0:Q], 0.33, 0.5, ALU.is_gt, ALU.mult))
    chain.then_wait(dve, dve.tensor_scalar(w[0:Q], xn[0:Q], -0.33, 0.5, ALU.is_lt, ALU.mult))
    chain.then_wait(dve, dve.tensor_tensor(xn[0:Q], u[0:Q], w[0:Q], ALU.subtract))


def query_norm_phase(k, xnT, Wq_in, sc):
    nc = k.nc
    win, mm, sq_s, red_s, root_s, dve_s = (k.sem(f"qn_{n}") for n in ("in", "mm", "sq", "red", "root", "dve"))
    with ExitStack() as k.phase:
        Wq = k.sb("qn_W", [128, DC, H * HD])
        sq = k.sb("qn_sqb", [128, 4, 512])
        ss, root, t = k.sb("qn_ss", [128, NB * H]), k.sb("qn_rootv", [128, NB * H]), k.sb("qn_t", [128, NB * H])
        ps = k.ps("qn_ps", [128, 4, 512])
        with nc.Block() as block:
            @block.sync
            def _(sp):
                for c in range(DC):
                    sp.dma_start(Wq[:, c, :], Wq_in[:, c, :]).then_inc(win, 16)

            @block.tensor
            def _(pe):
                pe.wait_ge(win, 32)
                for b in range(NB):
                    for g in range(NG):
                        n = NG * b + g
                        if n >= 4:
                            pe.wait_ge(sq_s, n - 3)
                        for c in range(DC):
                            ins = pe.matmul(ps[0:Q, n % 4, :], xnT[:, c, b, :], Wq[:, c, 512 * g:512 * (g + 1)],
                                            start=(c == 0), stop=(c == DC - 1))
                        ins.then_inc(mm, 1)

            @block.scalar
            def _(act):
                for n in range(STEPS):
                    act.wait_ge(mm, n + 1)
                    if n >= 4:
                        act.wait_ge(red_s, n - 3)
                    act.activation(sq[0:Q, n % 4, :], ps[0:Q, n % 4, :], ACT.Square).then_inc(sq_s, 1)
                act.wait_ge(dve_s, 1)
                act.activation(root[0:Q, :], ss[0:Q, :], ACT.Sqrt).then_inc(root_s, 1)

            @block.vector
            def _(dve):
                for n in range(STEPS):
                    dve.wait_ge(sq_s, n + 1)
                    dve.tensor_reduce(ss[0:Q, HG * n:HG * (n + 1)],
                                      sq[0:Q, n % 4, :].rearrange("p (h d) -> p h d", h=HG), AX_X,
                                      ALU.add).then_inc(red_s, 1)
                dve.wait_ge(red_s, STEPS)
                chain = Count(dve_s)
                chain.then_wait(dve, dve.tensor_scalar(ss[0:Q, :], ss[0:Q, :], 1.0 / HD, LN_EPS, ALU.mult, ALU.add))
                dve.wait_ge(root_s, 1)
                newton_rsqrt(dve, chain, ss[0:Q, :], root[0:Q, :], sc[0:Q, :], t[0:Q, :])
                chain.then_wait(dve, dve.tensor_scalar(sc[0:Q, :], sc[0:Q, :], INV, None, ALU.mult))
    k.phase = k.whole


def key_norm_phase(k, ident, ctxT_in, Wk_in, rT_out):
    nc = k.nc
    sem = lambda n: k.sem(f"kn_{n}")
    win, whi, wlo = sem("w_in"), sem("w_hi"), sem("w_lo")
    raw_in, chi, clo, mm, sq_s, red_s = (sem(n) for n in ("raw_in", "ctx_hi", "ctx_lo", "mm", "sq", "red"))
    zero_s, root_s, var_s, chain_s, turned, parts_s, stored = (
        sem(n) for n in ("zero", "root", "var", "chain", "turned", "parts", "stored"))
    W = H * HD
    NCH = W // 512
    with ExitStack() as k.phase:
        Wk, Wk_hi, Wk_lo = k.sb("kn_W", [128, W]), k.sb("kn_Wh", [128, W], F32R), k.sb("kn_Wl", [128, W], F32R)
        raw = k.sb("kn_raw", [128, 2, KB * 128])
        c_hi, c_lo = k.sb("kn_ch", [128, KB, 128], F32R), k.sb("kn_cl", [128, KB, 128], F32R)
        sq = k.sb("kn_sqb", [128, 4, 512])
        ss, root, r, t = (k.sb(f"kn_{n}", [128, KB, H]) for n in ("ss", "rootv", "r", "t"))
        rows, p1f = k.sb("kn_rows", [128, KEYS]), k.sb("kn_p1f", [128, KEYS])
        parts = k.sb("kn_partsb", [128, 3, KEYS], BF16)
        ps = k.ps("kn_ps", [128, 4, 512])
        tp = k.ps("kn_tp", [128, 3, 512])
        with nc.Block() as block:
            @block.gpsimd
            def _(pool):
                pool.memset(raw[:], 0.0).then_inc(zero_s, 1)

            @block.sync
            def _(sp):
                sp.dma_start(Wk[:], Wk_in).then_inc(win, 16)
                sp.sem_inc(stored, 1)
                sp.wait_ge(zero_s, 1)
                sp.dma_start(raw[:, 0, 0:KEYS], ctxT_in[0]).then_inc(raw_in, 16)
                with sp.Fori(0, NB) as b:
                    sp.wait_ge(clo, KB * b + 1)
                    sp.dma_start(raw[:, (b + 1) % 2, 0:KEYS], ctxT_in[(b + 1) % NB]).then_inc(raw_in, 16)
                    sp.wait_ge(parts_s, 5 * b + 6)
                    for i in range(3):
                        sp.dma_start(rT_out[b, i], parts[0:H, i, :]).then_inc(stored, 16)
                sp.wait_ge(stored, 48 * NB + 1)
                sp.wait_ge(raw_in, 16 * (NB + 1))

            @block.tensor
            def _(pe):
                pe.wait_ge(wlo, 1)
                with pe.Fori(0, NB) as b:
                    for j in range(KB):
                        pe.wait_ge(clo, KB * b + j + 1)
                        for m in range(NCH):
                            n = NCH * j + m
                            out = ps[:, n % 4, :]
                            pe.wait_ge(sq_s, NCH * KB * b + n + 1)
                            ws = slice(512 * m, 512 * (m + 1))
                            pe.matmul(out, c_hi[:, j, :], Wk_hi[:, ws], start=True, stop=False)
                            pe.matmul(out, c_hi[:, j, :], Wk_lo[:, ws], start=False, stop=False)
                            pe.matmul(out, c_lo[:, j, :], Wk_hi[:, ws], start=False, stop=True).then_inc(mm, 1)
                    pe.wait_ge(chain_s, 5 * b + 5)
                    pe.wait_ge(parts_s, 5 * b + 1)
                    for j in range(KB):
                        ins = pe.transpose(tp[0:H, j // 4, 128 * (j % 4):128 * (j % 4 + 1)], r[:, j, :], ident[:])
                    ins.then_inc(turned, 1)

            @block.scalar
            def _(act):
                act.wait_ge(win, 16)
                act.activation(Wk_hi[:], Wk[:], ACT.Copy).then_inc(whi, 1)
                for i in range(4):
                    act.activation(sq[:, i, 0:1], Wk[:, 0:1], ACT.Copy).then_inc(sq_s, 1)
                with act.Fori(0, NB) as b:
                    act.wait_ge(raw_in, 16 * (b + 1))

                    def split(j):
                        act.activation(c_hi[:, j, :], raw[:, b % 2, 128 * j:128 * (j + 1)], ACT.Copy)\
                           .then_inc(chi, 1)

                    split(0)
                    for j in range(KB):
                        if j + 1 < KB:
                            split(j + 1)
                        for m in range(NCH):
                            n = NCH * j + m
                            act.wait_ge(mm, NCH * KB * b + n + 1)
                            act.wait_ge(red_s, NCH * KB * b + n + 1)
                            act.activation(sq[:, n % 4, :], ps[:, n % 4, :], ACT.Square).then_inc(sq_s, 1)
                    act.wait_ge(var_s, b + 1)
                    act.activation(root[:], ss[:], ACT.Sqrt).then_inc(root_s, 1)

            @block.vector
            def _(dve):
                dve.wait_ge(whi, 1)
                dve.tensor_tensor(Wk_lo[:], Wk[:], Wk_hi[:], ALU.subtract).then_inc(wlo, 1)
                dve.sem_inc(parts_s, 1)
                dve.wait_ge(sq_s, 4)
                for i in range(4):
                    dve.memset(t[:, 0, i:i + 1], 0.0).then_inc(red_s, 1)
                with dve.Fori(0, NB) as b:

                    def split(j):
                        dve.wait_ge(chi, KB * b + j + 1)
                        dve.tensor_tensor(c_lo[:, j, :], raw[:, b % 2, 128 * j:128 * (j + 1)], c_hi[:, j, :],
                                          ALU.subtract).then_inc(clo, 1)

                    split(0)
                    for j in range(KB):
                        if j + 1 < KB:
                            split(j + 1)
                        for m in range(NCH):
                            n = NCH * j + m
                            dve.wait_ge(sq_s, NCH * KB * b + n + 5)
                            dve.tensor_reduce(ss[:, j, HG * m:HG * (m + 1)],
                                              sq[:, n % 4, :].rearrange("p (h d) -> p h d", h=HG), AX_X,
                                              ALU.add).then_inc(red_s, 1)
                    dve.wait_ge(red_s, NCH * KB * (b + 1) + 4)
                    dve.tensor_scalar(ss[:], ss[:], 1.0 / HD, LN_EPS, ALU.mult, ALU.add).then_inc(var_s, 1)
                    dve.wait_ge(root_s, b + 1)
                    dve.wait_ge(var_s, b + 1)
                    dve.reciprocal(r[:], root[:]).then_inc(chain_s, 1)
                    dve.wait_ge(chain_s, 5 * b + 1)
                    dve.tensor_tensor(t[:], r[:], r[:], ALU.mult).then_inc(chain_s, 1)
                    dve.wait_ge(chain_s, 5 * b + 2)
                    dve.tensor_tensor(t[:], t[:], ss[:], ALU.mult).then_inc(chain_s, 1)
                    dve.wait_ge(chain_s, 5 * b + 3)
                    dve.tensor_scalar(t[:], t[:], -0.5, 1.5, ALU.mult, ALU.add).then_inc(chain_s, 1)
                    dve.wait_ge(chain_s, 5 * b + 4)
                    dve.tensor_tensor(r[:], r[:], t[:], ALU.mult).then_inc(chain_s, 1)
                    dve.wait_ge(turned, b + 1)
                    dve.wait_ge(stored, 48 * b + 1)
                    rt = tp[0:H, :, :].rearrange("p a n -> p (a n)")[:, 0:KEYS]
                    dve.tensor_copy(parts[0:H, 0, :], rt).then_inc(parts_s, 1)
                    dve.wait_ge(parts_s, 5 * b + 2)
                    dve.tensor_tensor(rows[0:H, :], rt, parts[0:H, 0, :], ALU.subtract).then_inc(parts_s, 1)
                    dve.wait_ge(parts_s, 5 * b + 3)
                    dve.tensor_copy(parts[0:H, 1, :], rows[0:H, :]).then_inc(parts_s, 1)
                    dve.wait_ge(parts_s, 5 * b + 4)
                    dve.tensor_tensor(p1f[0:H, :], rows[0:H, :], parts[0:H, 1, :], ALU.subtract).then_inc(parts_s, 1)
                    dve.wait_ge(parts_s, 5 * b + 5)
                    dve.tensor_copy(parts[0:H, 2, :], p1f[0:H, :]).then_inc(parts_s, 1)
    k.phase = k.whole


ROUTED = 64
TOPK = 6
FFN = 176
SHARED = 2
NF = 2
FC = 96
FS = FFN - FC
RT = 128
TILES = (NB * Q * TOPK + ROUTED * (RT - 1)) // RT
ROWS = TILES * RT
FAR = 16384.0
U0 = NB * SHARED
UNITS = U0 + TILES
WS = 8
STORE_LAG = 5


def clear_rows_phase(k, zero, rows_out):
    nc = k.nc
    zeroed, cleared = k.sem("zeroed"), k.sem("rows_cleared")
    flat = rows_out.rearrange("(p a) d -> p (a d)", p=128)
    width = zero.shape[-1]
    with nc.Block() as block:
        @block.vector
        def _(dve):
            dve.memset(zero[:], 0.0).then_inc(zeroed, 1)

        @block.sync
        def _(sp):
            sp.wait_ge(zeroed, 1)
            for w0 in range(0, TILES * D, width):
                sp.dma_start(flat[:, w0:w0 + width], zero[:]).then_inc(cleared, 16)
    return cleared, 16 * (TILES * D // width)


def router_phase(k, xnT, ident, gateT_in, p, tot, chosen, place, key, tile_expert):
    nc = k.nc
    sem = lambda n: k.sem(f"rt_{n}")
    gin, mm, chain_s, exp_s, neg_s, picked, made, counted, numbered, rest_s, spread, ends_s = (
        sem(n) for n in ("in", "mm", "chain", "exp", "neg", "picked", "made", "counted", "numbered", "rest",
                         "spread", "ends"))
    with ExitStack() as k.phase:
        gate = k.sb("rt_gate", [128, DC, ROUTED])
        ones, before = k.sb("rt_ones", [128, 128]), k.sb("rt_before", [128, 128])
        neg, Z = k.sb("rt_negm", [128, NB]), k.sb("rt_Z", [128, NB])
        top, rest = k.sb("rt_top", [128, NB, 8]), k.sb("rt_rest", [128, NB, ROUTED])
        mask, seen = k.sb("rt_mask", [128, NB, ROUTED]), k.sb("rt_seen", [128, NB, ROUTED])
        count, tiles = k.sb("rt_count", [128, ROUTED]), k.sb("rt_tiles", [128, 2, ROUTED])
        ends, first = k.sb("rt_ends", [128, 2, ROUTED]), k.sb("rt_first", [128, ROUTED])
        number, expert, le = k.sb("rt_number", [128, 1]), k.sb("rt_expert", [128, 1]), k.sb("rt_le", [128, ROUTED])
        ps = k.ps("rt_ps", [128, NB, ROUTED])
        rank = k.ps("rt_rank", [128, NB, ROUTED])
        misc = k.ps("rt_misc", [128, 512])
        numps = k.ps("rt_numps", [128, 512])
        with nc.Block() as block:
            @block.sync
            def _(sp):
                sp.dma_start(gate[:], gateT_in).then_inc(gin, 16)
                sp.wait_ge(gin, 16)

            @block.gpsimd
            def _(pool):
                chain = Count(made)
                chain.then_wait(pool, pool.memset(ones[:], 1.0))
                chain.then_wait(pool, pool.affine_select(out=before[:], in_=ones[:], compare_op=ALU.is_gt, fill=0.0,
                                                         base=0, pattern=[[1, 128]], channel_multiplier=-1))

            @block.tensor
            def _(pe):
                pe.wait_ge(gin, 16)
                for b in range(NB):
                    for c in range(DC):
                        ins = pe.matmul(ps[0:Q, b, :], xnT[:, c, b, :], gate[:, c, :],
                                        start=(c == 0), stop=(c == DC - 1))
                ins.then_inc(mm, 1)
                pe.wait_ge(made, 2)
                pe.matmul(numps[:, 0:1], before[:], ones[:, 0:1], start=True, stop=True).then_inc(numbered, 1)
                pe.wait_ge(picked, 1)
                pe.matmul(misc[:, 0:ROUTED], ones[0:Q, :], seen[0:Q, NB - 1, :], start=True, stop=True)\
                  .then_inc(counted, 1)
                for b in range(NB):
                    pe.matmul(rank[0:Q, b, :], before[0:Q, 0:Q], mask[0:Q, b, :], start=True, stop=(b == 0))
                    if b:
                        ins = pe.matmul(rank[0:Q, b, :], ones[0:Q, 0:Q], seen[0:Q, b - 1, :], start=False, stop=True)
                ins.then_inc(counted, 1)
                pe.wait_ge(spread, 1)
                pe.transpose(misc[0:1, 0:128], expert[:], ident[:]).then_inc(counted, 1)

            @block.scalar
            def _(act):
                act.wait_ge(neg_s, 1)
                for b in range(NB):
                    act.activation(p[0:Q, b, :], ps[0:Q, b, :], ACT.Exp, bias=neg[0:Q, b:b + 1],
                                   accum_out=Z[0:Q, b:b + 1]).then_inc(exp_s, 1)

            @block.vector
            def _(dve):
                chain = Count(chain_s)
                dve.wait_ge(mm, 1)
                dve.tensor_reduce(neg[0:Q, :], ps[0:Q, :, :], AX_X, ALU.max, negate=True).then_inc(neg_s, 1)
                dve.wait_ge(exp_s, NB)
                chain.then_wait(dve, dve.reciprocal(Z[0:Q, :], Z[0:Q, :]))
                for b in range(NB):
                    chain.by(dve.tensor_scalar(p[0:Q, b, :], p[0:Q, b, :], Z[0:Q, b:b + 1], None, ALU.mult))
                dve.wait_ge(chain_s, chain.n)
                for b in range(NB):
                    chain.by(dve.max(top[0:Q, b, :], p[0:Q, b, :]))
                dve.wait_ge(chain_s, chain.n)
                chain.by(dve.tensor_reduce(tot[0:Q, :], top[0:Q, :, 0:TOPK], AX_X, ALU.add))
                chain.then_wait(dve, dve.memset(top[0:Q, :, TOPK:8], -2.0))
                for b in range(NB):
                    chain.by(dve.match_replace(rest[0:Q, b, :], top[0:Q, b, :], p[0:Q, b, :], -1.0))
                dve.wait_ge(chain_s, chain.n)
                chain.then_wait(dve, dve.tensor_scalar(mask[0:Q, :, :], rest[0:Q, :, :], 0.0, None, ALU.is_lt))
                chain.then_wait(dve, dve.tensor_copy(seen[0:Q, 0, :], mask[0:Q, 0, :]))
                for b in range(1, NB):
                    chain.then_wait(dve, dve.tensor_tensor(seen[0:Q, b, :], seen[0:Q, b - 1, :], mask[0:Q, b, :],
                                                           ALU.add))
                dve.memset(le[:, 0:1], 0.0).then_inc(picked, 1)
                chain.then_wait(dve, dve.tensor_scalar(tot[0:Q, :], tot[0:Q, :], 1e-20, None, ALU.add))
                chain.then_wait(dve, dve.reciprocal(tot[0:Q, :], tot[0:Q, :]))
                dve.wait_ge(numbered, 1)
                chain.by(dve.tensor_copy(number[:], numps[:, 0:1]))
                dve.wait_ge(counted, 1)
                chain.then_wait(dve, dve.tensor_copy(count[:], misc[:, 0:ROUTED]))
                chain.then_wait(dve, dve.tensor_scalar(tiles[:, 0, :], count[:], 0.0, None, ALU.is_gt))
                last = -(-NB * Q // RT) - 1
                for i in range(1, last + 1):
                    chain.then_wait(dve, dve.scalar_tensor_tensor(
                        out=tiles[:, i % 2, :], in0=count[:], scalar=float(RT * i), in1=tiles[:, 1 - i % 2, :],
                        op0=ALU.is_gt, op1=ALU.add))
                src, step, side = tiles[:, last % 2, :], 1, 0
                while step < ROUTED:
                    dst = ends[:, side, :]
                    chain.by(dve.tensor_copy(dst[:, 0:step], src[:, 0:step]))
                    chain.then_wait(dve, dve.tensor_tensor(dst[:, step:], src[:, step:], src[:, :ROUTED - step], ALU.add))
                    src, step, side = dst, 2 * step, 1 - side
                chain.then_wait(dve, dve.tensor_tensor(first[:], src, tiles[:, last % 2, :], ALU.subtract))
                chain.then_wait(dve, dve.tensor_scalar(le[:], first[:], number[:, 0:1], None, ALU.is_le))
                chain.then_wait(dve, dve.tensor_reduce(expert[:], le[:], AX_X, ALU.add))
                dve.tensor_scalar(expert[:], expert[:], -1.0, None, ALU.add).then_inc(spread, 1)
                chain.then_wait(dve, dve.tensor_scalar(first[:], first[:], -float(RT), FAR, ALU.mult, ALU.add))
                dve.wait_ge(counted, 2)
                chain.then_wait(dve, dve.scalar_tensor_tensor(
                    out=key[0:Q, :, :], in0=rank[0:Q, :, :], scalar=-1.0,
                    in1=first[0:Q, :].unsqueeze(1).to_broadcast([Q, NB, ROUTED]), op0=ALU.mult, op1=ALU.add))
                chain.then_wait(dve, dve.tensor_tensor(key[0:Q, :, :], key[0:Q, :, :], mask[0:Q, :, :], ALU.mult))
                for b in range(NB):
                    chain.by(dve.max(chosen[0:Q, b, :], key[0:Q, b, :]))
                dve.wait_ge(chain_s, chain.n)
                chain.by(dve.tensor_scalar(place[0:Q, :, :], chosen[0:Q, :, 0:TOPK], -1.0, FAR, ALU.mult, ALU.add))
                dve.wait_ge(counted, 3)
                chain.then_wait(dve, dve.tensor_copy(tile_expert[0:1, :], misc[0:1, 0:TILES]))
    k.phase = k.whole


def experts_phase(k, X, xn, xnT, ident, p, tot, chosen, place, key, tile_expert, wgu_in, wd_in, rows_in,
                  results, out):
    nc = k.nc
    sem = lambda n: k.sem(f"ex_{n}")
    w_in = [sem(f"w_in{s}") for s in range(WS)]
    x_in = [sem(f"x_in{s}") for s in range(WS)]
    y_out = [sem(f"y_out{s}") for s in range(WS)]
    back = [sem(f"back{i}") for i in range(TOPK)]
    shared_in, scattered, x_turned, x_ready, up_done, silu_done, act_done, act_turned, act_ready, down_done, \
        shared_added, y_ready, weight_s, added, stored = (
            sem(n) for n in ("shared_in", "scattered", "x_turned", "x_ready", "up", "silu", "act", "act_turned",
                             "act_ready", "down", "shared_added", "y_ready", "weight", "added", "stored"))
    with ExitStack() as k.phase:
        wgu, wd = k.sb("ex_wgu", [128, WS, DC, 2 * FFN]), k.sb("ex_wd", [128, WS, NF, D])
        sgu, sd = k.sb("ex_sgu", [128, SHARED, DC, 2 * FFN]), k.sb("ex_sd", [128, SHARED, NF, D])
        rows = k.sb("ex_rows", [128, WS, D])
        rowsT = k.sb("ex_rowsT", [128, 2, DC, RT])
        silu, hid = k.sb("ex_silu", [128, 2, FFN]), k.sb("ex_hid", [128, 2, FFN])
        hidT = k.sb("ex_hidT", [128, 2, NF, RT])
        y = k.sb("ex_y", [128, WS, D])
        got = k.sb("ex_got", [128, TOPK, NB, D])
        eq, weight = k.sb("ex_eq", [128, NB, ROUTED]), k.sb("ex_weight", [128, NB, TOPK])
        gu_ps = k.ps("ex_gu_ps", [128, 2, 512])
        x_ps, hid_ps = k.ps("ex_x_ps", [128, 2, 512]), k.ps("ex_hid_ps", [128, 2, 512])
        y_ps = k.ps("ex_y_ps", [128, 2, 512])

        def run(engine, step):
            start = U0 + 2 * WS
            groups = (UNITS - 1 - start) // WS
            for n in range(start):
                step(n, n % WS, n // WS, True)
            with engine.Fori(start // WS, start // WS + groups) as g:
                for s in range(WS):
                    step(WS * g + s, s, g, False)
            for n in range(start + WS * groups, UNITS + 2):
                step(n, n % WS, n // WS, True)

        def unit(n, s, lag, peeled):
            m = n - lag
            return m, (s - lag) % WS, (not peeled) or 0 <= m < UNITS, (not peeled) or U0 <= m < UNITS

        with nc.Block() as block:
            @block.gpsimd
            def _(pool):
                for b in range(NB):
                    for i in range(TOPK):
                        pool.indirect_dma_start(rows_in, bass.IndirectOffsetOnAxis(place[0:Q, b, i:i + 1], 0),
                                                xn[0:Q, b, :], None).then_inc(scattered, 16)
                for s in range(WS):
                    pool.wait_ge(y_out[s], 16 * ((TILES - 1 - s) // WS + 1))
                for i in range(TOPK):
                    for b in range(NB):
                        pool.indirect_dma_start(got[0:Q, i, b, :], None, results,
                                                bass.IndirectOffsetOnAxis(place[0:Q, b, i:i + 1], 0))\
                            .then_inc(back[i], 16)

            @block.sync
            def _(sp):
                for h in range(SHARED):
                    sp.dma_start(sgu[:, h], wgu_in[ROUTED + h]).then_inc(shared_in, 16)
                    sp.dma_start(sd[0:FC, h], wd_in[ROUTED + h]).then_inc(shared_in, 16)

                def weights(j, s):
                    e = sp.value_load(tile_expert[0:1, j:j + 1] if isinstance(j, int)
                                      else tile_expert[0:1, bass.ds(j, 1)], min_val=0, max_val=ROUTED - 1)
                    sp.dma_start(wgu[:, s], wgu_in[e]).then_inc(w_in[s], 16)
                    sp.dma_start(wd[0:FC, s], wd_in[e]).then_inc(w_in[s], 16)

                def tokens(j, s):
                    at = RT * j
                    sp.dma_start(rows[:, s, :], rows_in[at:at + RT] if isinstance(j, int)
                                 else rows_in[bass.ds(at, RT)]).then_inc(x_in[s], 16)

                for j in range(WS):
                    weights(j, j)
                sp.wait_ge(scattered, 16 * NB * TOPK)
                for j in range(WS):
                    tokens(j, j)

                def step(n, s, g, peeled):
                    m, _, _, tile = unit(n, s, 0, peeled)
                    if tile and (not peeled or m >= U0 + WS):
                        sp.wait_ge(down_done, m - WS + 1)
                        sp.sem_inc(passed, 1)
                        weights(m - U0, s)
                        tokens(m - U0, s)
                passed = sem("sp_passed")
                run(sp, step)
                for b in range(NB):
                    sp.wait_ge(added, (TOPK - 1) * NB + b + 1)
                    sp.dma_start(out[b], X[0:Q, b, :]).then_inc(stored, 16)
                sp.wait_ge(stored, 16 * NB)

            @block.tensor
            def _(pe):
                def step(n, s, g, peeled):
                    m, _, real, tile = unit(n, s, 0, peeled)
                    if real:
                        if tile:
                            pe.wait_ge(w_in[s], 32 * (g - U0 // WS + 1))
                            pe.wait_ge(x_ready, m - U0 + 1)
                        elif m == 0:
                            pe.wait_ge(shared_in, 32 * SHARED)
                        if not peeled or m >= 2:
                            pe.wait_ge(act_done, m - 1)
                        rows_n = RT if tile else Q
                        for c in range(DC):
                            x = rowsT[:, s % 2, c, :] if tile else xnT[:, c, m // SHARED, :]
                            w = wgu[:, s, c, :] if tile else sgu[:, m % SHARED, c, :]
                            ins = pe.matmul(gu_ps[0:rows_n, s % 2, 0:2 * FFN], x, w, start=(c == 0),
                                            stop=(c == DC - 1))
                        ins.then_inc(up_done, 1)
                    m, slot, real, tile = unit(n, s, 1, peeled)
                    if real:
                        pe.wait_ge(act_done, m + 1)
                        if not peeled or m >= 2:
                            pe.wait_ge(act_ready, m - 1)
                        rows_n = RT if tile else Q
                        for f in range(NF):
                            ins = pe.transpose(hid_ps[0:FC, slot % 2, RT * f:RT * f + rows_n],
                                               hid[0:rows_n, slot % 2, FS * f:FS * f + FC], ident[0:rows_n, 0:rows_n])
                        ins.then_inc(act_turned, 1)
                    m, slot, real, tile = unit(n, s, -1, peeled)
                    if tile:
                        j = m - U0
                        pe.wait_ge(x_in[slot], 16 * (g - U0 // WS + (1 if s < WS - 1 else 2)))
                        if not peeled or j >= 2:
                            pe.wait_ge(x_ready, j - 1)
                        for c in range(DC):
                            ins = pe.transpose(x_ps[:, slot % 2, RT * c:RT * (c + 1)],
                                               rows[:, slot, 128 * c:128 * (c + 1)], ident[:])
                        ins.then_inc(x_turned, 1)
                    m, slot, real, tile = unit(n, s, 2, peeled)
                    if real:
                        pe.wait_ge(act_ready, m + 1)
                        if tile:
                            j = m - U0
                            if peeled and j < 2:
                                pe.wait_ge(shared_added, NB - 1 + j)
                            else:
                                pe.wait_ge(y_ready, j - 1)
                        elif m % SHARED == 0 and m >= 2 * SHARED:
                            pe.wait_ge(shared_added, m // SHARED - 1)
                        rows_n, bank = (RT, slot % 2) if tile else (Q, m // SHARED % 2)
                        for f in range(NF):
                            ins = pe.matmul(y_ps[0:rows_n, bank, 0:D], hidT[0:FC, slot % 2, f, 0:rows_n],
                                            wd[0:FC, slot, f, :] if tile else sd[0:FC, m % SHARED, f, :],
                                            start=(f == 0 and (tile or m % SHARED == 0)),
                                            stop=(f == NF - 1 and (tile or m % SHARED == SHARED - 1)))
                        ins.then_inc(down_done, 1)
                run(pe, step)

            @block.scalar
            def _(act):
                def step(n, s, g, peeled):
                    m, _, real, tile = unit(n, s, 0, peeled)
                    if real:
                        act.wait_ge(up_done, m + 1)
                        if not peeled or m >= 2:
                            act.wait_ge(act_done, m - 1)
                        rows_n = RT if tile else Q
                        act.activation(silu[0:rows_n, s % 2, :], gu_ps[0:rows_n, s % 2, 0:FFN], ACT.Silu)\
                           .then_inc(silu_done, 1)
                    m, slot, real, tile = unit(n, s, 2, peeled)
                    if tile:
                        j = m - U0
                        act.wait_ge(down_done, m + 1)
                        if not peeled or j >= WS:
                            act.wait_ge(y_out[slot], 16 * (g - U0 // WS - (1 if s < 2 else 0)))
                        act.copy(y[:, slot, :], y_ps[:, slot % 2, 0:D]).then_inc(y_ready, 1)
                    m, slot, real, tile = unit(n, s, 3, peeled)
                    if tile:
                        act.wait_ge(y_ready, m - U0 + 1)
                        at = RT * (m - U0)
                        act.dma_start(results[at:at + RT] if peeled else results[bass.ds(at, RT)], y[:, slot, :])\
                           .then_inc(y_out[slot], 16)
                run(act, step)
                step(UNITS + 2, (UNITS + 2) % WS, (UNITS + 2) // WS, True)

            @block.vector
            def _(dve):
                chain = Count(weight_s)

                def step(n, s, g, peeled):
                    m, slot, real, tile = unit(n, s, 1, peeled)
                    if real:
                        dve.wait_ge(act_turned, m + 1)
                        if not peeled or m >= 2:
                            dve.wait_ge(down_done, m - 1)
                        rows_n = RT if tile else Q
                        dve.tensor_copy(hidT[0:FC, slot % 2, :, 0:rows_n],
                                        hid_ps[0:FC, slot % 2, 0:NF * RT].rearrange("p (f r) -> p f r", f=NF)
                                        [:, :, 0:rows_n]).then_inc(act_ready, 1)
                    m, slot, real, tile = unit(n, s, -1, peeled)
                    if tile:
                        dve.wait_ge(x_turned, m - U0 + 1)
                        dve.wait_ge(up_done, m - 1)
                        dve.tensor_copy(rowsT[:, slot % 2, :, :].rearrange("p c r -> p (c r)"),
                                        x_ps[:, slot % 2, 0:DC * RT]).then_inc(x_ready, 1)
                    m, _, real, tile = unit(n, s, 0, peeled)
                    if real:
                        dve.wait_ge(silu_done, m + 1)
                        if not peeled or m >= 2:
                            dve.wait_ge(act_turned, m - 1)
                        rows_n = RT if tile else Q
                        dve.tensor_tensor(hid[0:rows_n, s % 2, :], gu_ps[0:rows_n, s % 2, FFN:2 * FFN],
                                          silu[0:rows_n, s % 2, :], ALU.mult).then_inc(act_done, 1)
                    m, _, real, tile = unit(n, s, 2, peeled)
                    if real and not tile and m % SHARED == SHARED - 1:
                        b = m // SHARED
                        dve.wait_ge(down_done, m + 1)
                        dve.tensor_tensor(X[0:Q, b, :], X[0:Q, b, :], y_ps[0:Q, b % 2, 0:D], ALU.add)\
                           .then_inc(shared_added, 1)
                    if peeled and n == U0 - 2:
                        weights_of_experts()

                def weights_of_experts():
                    for i in range(TOPK):
                        chain.then_wait(dve, dve.tensor_tensor(
                            eq[0:Q, :, :], key[0:Q, :, :],
                            chosen[0:Q, :, i:i + 1].to_broadcast([Q, NB, ROUTED]), ALU.is_equal))
                        chain.then_wait(dve, dve.tensor_tensor(eq[0:Q, :, :], eq[0:Q, :, :], p[0:Q, :, :], ALU.mult))
                        chain.then_wait(dve, dve.tensor_reduce(weight[0:Q, :, i:i + 1].rearrange("p b o -> p (b o)"),
                                                               eq[0:Q, :, :], AX_X, ALU.add))
                    chain.then_wait(dve, dve.tensor_tensor(
                        weight[0:Q, :, :], weight[0:Q, :, :],
                        tot[0:Q, :].unsqueeze(2).to_broadcast([Q, NB, TOPK]), ALU.mult))
                run(dve, step)
                dve.wait_ge(shared_added, NB)
                for i in range(TOPK):
                    dve.wait_ge(back[i], 16 * NB)
                    for b in range(NB):
                        if i:
                            dve.wait_ge(added, (i - 1) * NB + b + 1)
                        dve.scalar_tensor_tensor(out=X[0:Q, b, :], in0=got[0:Q, i, b, :], scalar=weight[0:Q, b, i:i + 1],
                                                 in1=X[0:Q, b, :], op0=ALU.mult, op1=ALU.add).then_inc(added, 1)
    k.phase = k.whole


def program(nc, a, out, upto=9):
    with ExitStack() as whole:
        k = Core(nc, whole)
        X, ident = k.sb("X", [128, NB, D]), k.sb("ident", [128, 128])
        sel = k.sb("sel", [128, H, 128], BF16)
        sc = k.sb("sc", [128, NB * H])
        rT = nc.dram_tensor("r_rows", (NB, 3, H, KEYS), BF16).ap()
        token_rows = nc.dram_tensor("token_rows", (ROWS, D), F32).ap()
        result_rows = nc.dram_tensor("result_rows", (ROWS, D), F32).ap()
        xnT = k.sb("xnT", [128, DC, NB, Q])
        sc_made = k.sem("sc_made")
        setup_phase(k, a["x"], X, ident, sel)
        with nc.Block() as block:
            @block.vector
            def _(dve):
                dve.memset(sc[:], INV).then_inc(sc_made, 1)

        for layer, kv in ((0, H // 2), (1, H)):
            t = f"l{layer}"
            if upto <= 2 * layer: break
            if upto == 100 and layer == 0:
                zero = k.sb("zero_rows", [128, TILES * D // 16])
                cleared = clear_rows_phase(k, zero, token_rows)
                k.end_layer([cleared])
                continue
            with ExitStack() as k.whole_layer:
              if upto != 100:
                A = k.whole_layer.enter_context(nc.sbuf_tensor(f"{t}_A", [128, DC, H, C], F32))
                Bw = k.whole_layer.enter_context(nc.sbuf_tensor(f"{t}_B", [128, H, D], F32))
                if layer:
                    key_norm_phase(k, ident, a["ctxT"], a["Wk1"], rT)
                combine_phase(k, f"{t}c", kv, a[f"WqT{layer}"], a[f"WkT{layer}"], a[f"WvT{layer}"], a[f"Wo{layer}"],
                              (a["gq"], a["gk"]) if layer else None, A, Bw)
                with nc.sbuf_tensor(f"{t}_xn", [128, NB, D], F32) as xn:
                    norm_phase(k, f"{t}n", X, ident, xn, xnT)
                if layer == 0:
                    zero = k.whole_layer.enter_context(nc.sbuf_tensor("zero_rows", [128, TILES * D // 16], F32))
                    cleared = clear_rows_phase(k, zero, token_rows)
                if layer:
                    query_norm_phase(k, xnT, a["Wq1"], sc)
                attention_phase(k, t, bool(layer), X, xnT, ident, sel, A, Bw, sc, a["ctxT"], a["ctxN"],
                                a["mask"], rT)
            if upto <= 2 * layer + 1: break
            if layer == 0:
                with nc.sbuf_tensor("f0_xn", [128, NB, D], F32) as xn:
                    norm_phase(k, "f0", X, ident, xn, xnT, after=ternary)
                ternary_phase(k, X, ident, xnT, a["wT"], a["rramT"])
                k.end_layer([cleared])
            else:
                hold = lambda name, shape, dt=F32: moe.enter_context(nc.sbuf_tensor(f"m1_{name}", shape, dt))
                with ExitStack() as moe:
                    xn = hold("xn", [128, NB, D])
                    norm_phase(k, "m1", X, ident, xn, xnT)
                    routing = (hold("p", [128, NB, ROUTED]), hold("tot", [128, NB]), hold("chosen", [128, NB, 8]),
                               hold("place", [128, NB, TOPK], U32), hold("key", [128, NB, ROUTED]),
                               hold("tile_expert", [128, TILES], I32))
                    router_phase(k, xnT, ident, a["gateT"], *routing)
                    experts_phase(k, X, xn, xnT, ident, *routing, a["wgu"], a["wd"], token_rows,
                                  result_rows, out)
        if upto < 9:
            s = k.sem("dbg")
            with nc.Block() as block:
                @block.sync
                def _(sp):
                    sp.dma_start(out.rearrange("b q d -> q b d"), X[0:Q]).then_inc(s, 16)
                    sp.wait_ge(s, 16)


def laid_out(i):
    import numpy as np

    def heads_T(w, n):
        return np.ascontiguousarray(w.reshape(w.shape[0], n, HD).transpose(2, 1, 0))

    a = {"x": i["x"], "ctxN": i["ctx_1024"], "ctxT": np.ascontiguousarray(i["ctx_1024"].transpose(0, 2, 1)),
         "mask": i["mask_BxS2_bf1"].view(np.uint8)}
    for layer, kv in ((0, H // 2), (1, H)):
        w = {n: i[f"L{layer}_xattn_{n}"] for n in ("Wq", "Wk", "Wv", "Wo")}
        a[f"WqT{layer}"] = heads_T(w["Wq"], H)
        a[f"WkT{layer}"] = heads_T(w["Wk"], kv)
        a[f"WvT{layer}"] = heads_T(w["Wv"], kv)
        a[f"Wo{layer}"] = np.ascontiguousarray(w["Wo"].reshape(H, HD, D).transpose(1, 0, 2))
    a["Wq1"] = np.ascontiguousarray(i["L1_xattn_Wq"].reshape(DC, 128, H * HD).transpose(1, 0, 2))
    a["Wk1"] = i["L1_xattn_Wk"]
    a["gq"], a["gk"] = i["L1_xattn_gq"].reshape(HD, 1), i["L1_xattn_gk"].reshape(HD, 1)
    for n, m in (("wT", "weight"), ("rramT", "rram_variation")):
        a[n] = np.ascontiguousarray(i[f"L0_ffn_{m}"].T.reshape(DC, 128, D).transpose(1, 0, 2))
    a["gateT"] = np.ascontiguousarray(i["L1_ffn_gate_w"].T.reshape(DC, 128, ROUTED).transpose(1, 0, 2))
    sgu = i["L1_ffn_ws_gate_up"].reshape(2, 2, FFN, D).transpose(1, 0, 2, 3).reshape(2, 2 * FFN, D)
    gu = np.concatenate([i["L1_ffn_w_gate_up"], sgu])
    a["wgu"] = np.ascontiguousarray(gu.transpose(0, 2, 1).reshape(ROUTED + SHARED, DC, 128, 2 * FFN).transpose(0, 2, 1, 3))
    down = np.concatenate([i["L1_ffn_w_down"], i["L1_ffn_ws_down"].reshape(D, 2, FFN).transpose(1, 0, 2)])
    down = down.transpose(0, 2, 1)
    a["wd"] = np.zeros((ROUTED + SHARED, FC, NF, D), down.dtype)
    a["wd"][:, :, 0] = down[:, 0:FC]
    a["wd"][:, FC - FS:, 1] = down[:, FC:]
    return {n: np.ascontiguousarray(v) for n, v in a.items()}


def kernel(**inputs):
    import numpy as np
    import concourse.bacc as bacc
    from concourse.bass_utils import run_bass_kernel_spmd

    arrays = laid_out({n: np.asarray(v) for n, v in inputs.items()})
    nc = bacc.Bacc("TRN2", target_bir_lowering=False, num_devices=1)
    aps = {n: nc.dram_tensor(f"in_{n}", v.shape, mybir.dt.from_np(v.dtype), kind="ExternalInput").ap()
           for n, v in arrays.items()}
    out = nc.dram_tensor("out", (NB, Q, D), F32, kind="ExternalOutput").ap()
    program(nc, aps, out)
    r = run_bass_kernel_spmd(nc, [{f"in_{n}": v for n, v in arrays.items()}], core_ids=[0])
    return r.results[0]["out"]
```

```python
from contextlib import ExitStack

import concourse.bass as bass
from concourse import mybir

F32 = mybir.dt.float32
F32R = mybir.dt.float32r
U8 = mybir.dt.uint8
U32 = mybir.dt.uint32
I32 = mybir.dt.int32
ALU = mybir.AluOpType
ACT = mybir.ActivationFunctionType
AX_X = mybir.AxisListType.X

NB = 8
Q = 100
D = 256
DC = D // 128
C = 128
KEYS = 1444
H = 16
HD = 128
KB = -(-KEYS // 128)
KT = KEYS - (KB - 1) * 128
HG = 4
NG = H // HG
STEPS = NB * NG
CHUNKS = [(0, 512), (512, 512), (1024, KEYS - 1024)]
TB = 4
NT = KB // TB
SLOTS = 3 * HG
SEEN_AT = 5
QN = 1
INV = float(HD) ** -0.5
BIG = 1.0e30
LN_EPS = 1e-5


class Count:

    def __init__(self, sem):
        self.sem, self.n = sem, 0

    def by(self, instruction, step=1):
        instruction.then_inc(self.sem, step)
        self.n += step

    def then_wait(self, engine, instruction, step=1):
        self.by(instruction, step)
        engine.wait_ge(self.sem, self.n)


class Core:

    def __init__(self, nc, whole):
        self.nc, self.whole, self.phase = nc, whole, whole
        self.layer, self.sems = ExitStack(), []

    def sem(self, name):
        self.sems.append(self.layer.enter_context(self.nc.semaphore(name)))
        return self.sems[-1]

    def end_layer(self):
        with self.nc.Block() as block:
            @block.gpsimd
            def _(pool):
                for s in self.sems:
                    pool.sem_clear(s)
        self.layer.close()
        self.layer, self.sems = ExitStack(), []

    def sb(self, name, shape, dt=F32):
        return self.phase.enter_context(self.nc.sbuf_tensor(name, shape, dt))

    def ps(self, name, shape, dt=F32):
        return self.phase.enter_context(self.nc.psum_tensor(name, shape, dt))


def newton_rsqrt(dve, chain, v, root, r, t):
    chain.then_wait(dve, dve.reciprocal(r, root))
    chain.then_wait(dve, dve.tensor_tensor(t, r, r, ALU.mult))
    chain.then_wait(dve, dve.tensor_tensor(t, t, v, ALU.mult))
    chain.then_wait(dve, dve.tensor_scalar(t, t, -0.5, 1.5, ALU.mult, ALU.add))
    chain.then_wait(dve, dve.tensor_tensor(r, r, t, ALU.mult))


def setup_phase(k, x_in, X, ident, sc, load_ahead):
    nc = k.nc
    loaded, made, sc_made = k.sem("x_loaded"), k.sem("consts_made"), k.sem("sc_made")
    with nc.Block() as block:
        @block.sync
        def _(sp):
            load_ahead(sp)
            sp.dma_start(X[0:Q, :, :], x_in.rearrange("b q d -> q b d")).then_inc(loaded, 16)

        @block.vector
        def _(dve):
            dve.memset(sc[:], INV).then_inc(sc_made, 1)

        @block.gpsimd
        def _(pool):
            chain = Count(made)
            chain.then_wait(pool, pool.memset(ident[:], 0.0))
            chain.then_wait(pool, pool.affine_select(out=ident[:], in_=ident[:], compare_op=ALU.not_equal, fill=1.0,
                                                     base=0, pattern=[[-1, 128]], channel_multiplier=1))
    return loaded


def norm_phase(k, tag, X, ident, xn, xnT, after=None, load_ahead=lambda sp: None):
    nc = k.nc
    dve_s, root_s, var_s = k.sem(f"{tag}_dve"), k.sem(f"{tag}_root"), k.sem(f"{tag}_var")
    tr_s, out_s = k.sem(f"{tag}_turned"), k.sem(f"{tag}_taken")
    with ExitStack() as k.phase:
        stats, mv = k.sb(f"{tag}_stats", [128, NB, 6]), k.sb(f"{tag}_mv", [128, NB, 2])
        var, root = k.sb(f"{tag}_varr", [128, NB]), k.sb(f"{tag}_rootv", [128, NB])
        rstd, t = k.sb(f"{tag}_rstd", [128, NB]), k.sb(f"{tag}_t", [128, NB])
        u, w = (k.sb(f"{tag}_{n}", [128, NB, D]) for n in "uw") if after else (None, None)
        turned = k.ps(f"{tag}_ps", [128, 4, 512])
        with nc.Block() as block:
            @block.sync
            def _(sp):
                load_ahead(sp)

            @block.vector
            def _(dve):
                chain = Count(dve_s)
                for b in range(NB):
                    chain.by(dve.bn_stats(stats[0:Q, b, :], X[0:Q, b, :]))
                dve.wait_ge(dve_s, chain.n)
                for b in range(NB):
                    chain.by(dve.bn_aggr(mv[0:Q, b, :], stats[0:Q, b, :]))
                dve.wait_ge(dve_s, chain.n)
                dve.tensor_scalar(var[0:Q, :], mv[0:Q, :, 1], LN_EPS, None, ALU.add).then_inc(var_s, 1)
                dve.wait_ge(root_s, 1)
                dve.wait_ge(var_s, 1)
                newton_rsqrt(dve, chain, var[0:Q, :], root[0:Q, :], rstd[0:Q, :], t[0:Q, :])
                for b in range(NB):
                    ins = dve.tensor_scalar(xn[0:Q, b, :], X[0:Q, b, :], mv[0:Q, b, 0:1], rstd[0:Q, b:b + 1],
                                            ALU.subtract, ALU.mult)
                    chain.by(ins)
                dve.wait_ge(dve_s, chain.n)
                if after:
                    after(dve, chain, xn, u, w)
                dve.tensor_copy(t[0:Q, :], rstd[0:Q, :]).then_inc(var_s, 1)
                for i in range(NB * DC // 4):
                    dve.wait_ge(tr_s, i + 1)
                    for j in range(4):
                        b, c = divmod(4 * i + j, DC)
                        ins = dve.tensor_copy(xnT[:, c, b, :], turned[:, i, 128 * j:128 * j + Q])
                    ins.then_inc(out_s, 1)
                dve.wait_ge(out_s, NB * DC // 4)

            @block.scalar
            def _(act):
                act.wait_ge(var_s, 1)
                act.activation(root[0:Q, :], var[0:Q, :], ACT.Sqrt).then_inc(root_s, 1)

            @block.tensor
            def _(pe):
                pe.wait_ge(var_s, 2)
                for i in range(NB * DC // 4):
                    for j in range(4):
                        b, c = divmod(4 * i + j, DC)
                        ins = pe.transpose(turned[:, i, 128 * j:128 * j + Q], xn[0:Q, b, 128 * c:128 * (c + 1)],
                                           ident[0:Q, 0:Q])
                    ins.then_inc(tr_s, 1)
    k.phase = k.whole


class CombineWeights:

    def __init__(self, k, stack, tag, kv, sources, gains):
        hold = lambda name, shape: stack.enter_context(k.nc.sbuf_tensor(f"{tag}_{name}", shape, F32))
        self.WqT, self.WkT, self.WvT, self.Wo = (
            hold("WqT", [128, H, D]), hold("WkT", [128, kv, C]), hold("WvT", [128, kv, C]), hold("Wo", [128, H, D]))
        self.g = hold("g", [128, 3])
        self.sources, self.gains = sources, gains
        self.wk_in, self.wv_in, self.gin = k.sem(f"{tag}_wk_in"), k.sem(f"{tag}_wv_in"), k.sem(f"{tag}_gin")
        self.wq_in, self.wo_in = ([k.sem(f"{tag}_{n}_in{i}") for i in range(2)] for n in ("wq", "wo"))

    def load(self, sp):
        WqT_in, WkT_in, WvT_in, Wo_in = self.sources
        sp.dma_start(self.WkT[:], WkT_in).then_inc(self.wk_in, 16)
        if self.gains:
            for i in range(2):
                sp.dma_start(self.g[:, i:i + 1], self.gains[i]).then_inc(self.gin, 16)
        for half in range(2):
            hs = slice(half * H // 2, (half + 1) * H // 2)
            sp.dma_start(self.WqT[:, hs, :], WqT_in[:, hs, :]).then_inc(self.wq_in[half], 16)
        sp.dma_start(self.WvT[:], WvT_in).then_inc(self.wv_in, 16)
        for half in range(2):
            hs = slice(half * H // 2, (half + 1) * H // 2)
            sp.dma_start(self.Wo[:, hs, :], Wo_in[:, hs, :]).then_inc(self.wo_in[half], 16)


def combine_phase(k, tag, kv, weights, load, A_hi, A_lo, Bw):
    nc = k.nc
    gain_s = k.sem(f"{tag}_gain")
    mm_s, hi_s, out_s = k.sem(f"{tag}_mm"), k.sem(f"{tag}_hi"), k.sem(f"{tag}_out")
    WqT, WkT, WvT, Wo, g, gains = weights.WqT, weights.WkT, weights.WvT, weights.Wo, weights.g, weights.gains
    wk_in, wv_in, wq_in, wo_in, gin = weights.wk_in, weights.wv_in, weights.wq_in, weights.wo_in, weights.gin
    with ExitStack() as k.phase:
        ps = k.ps(f"{tag}_ps", [128, 8, 512])
        with nc.Block() as block:
            @block.sync
            def _(sp):
                load(sp)

            @block.tensor
            def _(pe):
                pe.wait_ge(wk_in, 16)
                if gains:
                    pe.wait_ge(gain_s, 2)
                for h in range(H):
                    pe.wait_ge(wq_in[h // (H // 2)], 16)
                    if h >= 8:
                        pe.wait_ge(out_s, h - 7)
                    for c in range(DC):
                        ins = pe.matmul(ps[:, h % 8, C * c:C * (c + 1)], WqT[:, h, 128 * c:128 * (c + 1)],
                                        WkT[:, h * kv // H, :], start=True, stop=True)
                    ins.then_inc(mm_s, 1)
                pe.wait_ge(wv_in, 16)
                for h in range(H):
                    pe.wait_ge(wo_in[h // (H // 2)], 16)
                    pe.wait_ge(out_s, H + h - 7)
                    pe.matmul(ps[:, h % 8, 0:D], WvT[:, h * kv // H, :], Wo[:, h, :],
                              start=True, stop=True).then_inc(mm_s, 1)

            @block.scalar
            def _(act):
                for h in range(H):
                    act.wait_ge(mm_s, h + 1)
                    act.activation(A_hi[:, :, h, :], ps[:, h % 8, 0:DC * C].rearrange("p (c n) -> p c n", c=DC),
                                   ACT.Copy).then_inc(hi_s, 1)

            @block.vector
            def _(dve):
                if gains:
                    dve.wait_ge(gin, 32)
                    dve.tensor_tensor(g[:, 2:3], g[:, 0:1], g[:, 1:2], ALU.mult).then_inc(gain_s, 1)
                    dve.wait_ge(gain_s, 1)
                    dve.wait_ge(wk_in, 16)
                    dve.tensor_scalar(WkT[:], WkT[:], g[:, 2:3], None, ALU.mult).then_inc(gain_s, 1)
                for h in range(H):
                    dve.wait_ge(hi_s, h + 1)
                    dve.tensor_tensor(A_lo[:, :, h, :], ps[:, h % 8, 0:DC * C].rearrange("p (c n) -> p c n", c=DC),
                                      A_hi[:, :, h, :], ALU.subtract).then_inc(out_s, 1)
                for h in range(H):
                    dve.wait_ge(mm_s, H + h + 1)
                    dve.tensor_copy(Bw[:, h, :], ps[:, h % 8, 0:D]).then_inc(out_s, 1)
    k.phase = k.whole


def attention_phase(k, tag, rms, X, xnT, ident, A_hi, A_lo, Bw, sc, ctxT_in, ctxN_in, mask_in, r_in):
    nc = k.nc
    sem = lambda name: k.sem(f"{tag}_{name}")
    ctxT_loaded, ctxN_loaded, side_loaded = sem("ctxT_loaded"), sem("ctxN_loaded"), sem("side_loaded")
    ctxT_hi_s, ctxT_split = sem("ctxT_hi"), sem("ctxT_split")
    ctxN_hi_s, ctxN_split = sem("ctxN_hi"), sem("ctxN_split")
    side_made = sem("side_made")
    xhi_s, xlo_s, qnat_ready, qn_scaled, qT_ready, q_copied, qhi_s, qlo_s = (
        sem(n) for n in ("xhi", "xlo", "qnat_ready", "qn_scaled", "qT_ready", "q_copied", "qhi", "qlo"))
    r_loaded = [sem(f"r_loaded{h}") for h in range(HG)]
    scores_ready, scores_taken, max_ready, exp_done = (
        sem(n) for n in ("scores_ready", "scores_taken", "max_ready", "exp_done"))
    turned, ehi_s, elo_s = sem("turned"), sem("ehi"), sem("elo")
    pv_thirds, o_copied, y_ready, y_added, rden_s = (
        sem(n) for n in ("pv_thirds", "o_copied", "y_ready", "y_added", "rden"))
    zeroed, passed, passed_pool, passed_sp = (sem(n) for n in ("zeroed", "passed", "passed_pool", "passed_sp"))

    with ExitStack() as k.phase:
        sb, ps = (lambda n, s, d=F32: k.sb(f"{tag}_{n}", s, d)), (lambda n: k.ps(f"{tag}_{n}", [128, 512]))
        ctxT_raw, ctxN_raw = sb("ctxT_raw", [128, KEYS]), sb("ctxN_raw", [128, KB, C])
        ctxT_hi, ctxT_lo = sb("ctxT_hi", [128, 2, KEYS], F32R), sb("ctxT_lo", [128, 2, KEYS], F32R)
        ctxN_hi, ctxN_lo = sb("ctxN_hi", [128, KB, C], F32R), sb("ctxN_lo", [128, KB, C], F32R)
        xs_hi, xs_lo = sb("xs_hi", [128, DC, Q], F32R), sb("xs_lo", [128, DC, Q], F32R)
        qn, qT = sb("qn", [128, HG, C]), sb("qT", [128, HG, Q])
        q_hi, q_lo = sb("q_hi", [128, HG, Q], F32R), sb("q_lo", [128, HG, Q], F32R)
        E = sb("E", [128, HG, KB * 128])
        e_hi, e_lo = sb("e_hi", [128, KB, HG, Q], F32R), sb("e_lo", [128, KB, HG, Q], F32R)
        side = sb("side", [128, HG if rms else 1, KEYS])
        mx, negm, den = sb("mx", [128, HG, 3]), sb("negm", [128, HG]), sb("den", [128, 2 * HG * 3])
        rden = sb("rden", [128, HG])
        OT = sb("OT", [128, HG, Q])
        if not rms:
            mask_u8 = sb("mask_u8", [128, KEYS], U8)
            seen = sb("seen", [128, 2])
        S_ps = [ps("S0"), ps("S1")]
        T_ps = [ps("T0"), ps("T1"), ps("T2")]
        O_ps, misc = ps("O"), ps("misc")

        def batch_of(G):
            return (G % STEPS) // NG

        def group_of(G):
            return G % NG

        def run(eng, step, drain):
            step(0, False, True)
            with eng.Fori(1, NG) as g:
                step(g, True, False)
            with eng.Fori(1, NB) as b:
                step(NG * b, True, True)
                with eng.Fori(1, NG) as g:
                    step(NG * b + g, True, False)
            drain(STEPS)

        with nc.Block() as block:
            @block.sync
            def _(sp):
                def load_T(b):
                    sp.dma_start(ctxT_raw[:], ctxT_in[b]).then_inc(ctxT_loaded, 16)

                def load_N(b):
                    n = (KB - 1) * 128
                    sp.dma_start(ctxN_raw[:, 0:KB - 1, :], ctxN_in[b, 0:n, :].rearrange("(j p) c -> p j c", p=128))\
                      .then_inc(ctxN_loaded, 16)
                    sp.dma_start(ctxN_raw[0:KT, KB - 1, :], ctxN_in[b, n:KEYS, :]).then_inc(ctxN_loaded, 16)

                def load_side(b, slot):
                    if not rms:
                        sp.dma_start(mask_u8[0:Q, :], mask_in[b].partition_broadcast(Q)).then_inc(side_loaded, 16)

                load_T(0)
                load_side(0, 0)
                sp.wait_ge(zeroed, 2)
                load_N(0)
                with sp.Fori(0, NB) as b:
                    nb = (b + 1) % NB
                    sp.wait_ge(ctxT_split, 3 * (b + 1))
                    load_T(nb)
                    if not rms:
                        sp.wait_ge(side_made, 4 * (b + 1))
                    sp.sem_inc(passed_sp, 1)
                    load_side(nb, (b + 1) % 2)
                    sp.wait_ge(ctxN_split, 3 * (b + 1))
                    load_N(nb)
                sp.wait_ge(ctxT_loaded, 16 * (NB + 1))
                sp.wait_ge(ctxN_loaded, 32 * (NB + 1))
                if not rms:
                    sp.wait_ge(side_loaded, 16 * (NB + 1))

            @block.gpsimd
            def _(pool):
                def load_r(G, h):
                    pool.dma_start(side[0:Q, h, :], r_in[HG * G + h].partition_broadcast(Q)).then_inc(r_loaded[h], 16)

                if rms:
                    for h in range(HG):
                        load_r(0, h)
                pool.memset(ctxN_raw[:, KB - 1, :], 0.0).then_inc(zeroed, 1)
                pool.memset(E[:, :, KEYS:], 0.0).then_inc(zeroed, 1)
                if rms:
                    with pool.Fori(1, STEPS) as G:
                        for h in range(HG):
                            pool.wait_ge(scores_taken, 12 * (G - 1) + 3 * (h + 1))
                            pool.sem_inc(passed_pool, 1)
                            load_r(G, h)

            @block.tensor
            def _(pe):
                def scores(G, h, c):
                    b = batch_of(G)
                    lo, w = CHUNKS[c]
                    n3 = 3 * h + c
                    if h == 0:
                        pe.wait_ge(ctxT_split, 3 * b + c + 1)
                    if c == 0:
                        pe.wait_ge(qlo_s, HG * G + h + 1)
                    if not (isinstance(G, int) and G == 0 and n3 < 2):
                        pe.wait_ge(scores_taken, 12 * G + n3 - 1)
                    out = S_ps[n3 % 2][0:Q, 0:w]
                    hi, lo_ = ctxT_hi[:, b % 2, lo:lo + w], ctxT_lo[:, b % 2, lo:lo + w]
                    pe.matmul(out, q_hi[:, h, :], hi, start=True, stop=False)
                    pe.matmul(out, q_hi[:, h, :], lo_, start=False, stop=False)
                    pe.matmul(out, q_lo[:, h, :], hi, start=False, stop=True).then_inc(scores_ready, 1)

                def q_natural(G, c):
                    if c == 0:
                        pe.wait_ge(xlo_s, G + 1)
                        if not (isinstance(G, int) and G < 2):
                            pe.wait_ge(y_added, 4 * (G - 2) + 1)
                    hi, lo = (m[:, c, bass.ds(HG * group_of(G), HG), :].rearrange("p h n -> p (h n)")
                              for m in (A_hi, A_lo))
                    pe.matmul(misc[0:Q, :], xs_hi[:, c, :], hi, start=(c == 0), stop=False)
                    pe.matmul(misc[0:Q, :], xs_hi[:, c, :], lo, start=False, stop=False)
                    ins = pe.matmul(misc[0:Q, :], xs_lo[:, c, :], hi, start=False, stop=(c == DC - 1))
                    if c == DC - 1:
                        ins.then_inc(qnat_ready, 1)

                def q_turn(G):
                    pe.wait_ge(qn_scaled, G + 1)
                    for h in range(HG):
                        ins = pe.transpose(misc[:, Q * h:Q * (h + 1)], qn[0:Q, h, :], ident[0:Q, 0:Q])
                    ins.then_inc(qT_ready, 1)

                def turn(G, h, t):
                    n3 = NT * h + t
                    pe.wait_ge(exp_done, 12 * G + n3 + 1)
                    if not (isinstance(G, int) and G == 0 and n3 < 3):
                        pe.wait_ge(elo_s, 12 * G + n3 - 2)
                    for j in range(TB):
                        ins = pe.transpose(T_ps[n3 % 3][:, 128 * j:128 * j + Q],
                                           E[0:Q, h, 128 * (TB * t + j):128 * (TB * t + j + 1)], ident[0:Q, 0:Q])
                    ins.then_inc(turned, 1)

                def context_product(G, t):
                    if t == 0:
                        pe.wait_ge(y_added, 4 * G + 1)
                    pe.wait_ge(ctxN_split, 3 * batch_of(G) + t + 1)
                    pe.wait_ge(elo_s, 12 * G + 10 + t)
                    out = O_ps[:, 0:HG * Q]
                    for j in range(TB * t, TB * (t + 1)):
                        eh = e_hi[:, j, :, :].rearrange("p h q -> p (h q)")
                        el = e_lo[:, j, :, :].rearrange("p h q -> p (h q)")
                        pe.matmul(out, ctxN_hi[:, j, :], eh, start=(j == 0), stop=False)
                        pe.matmul(out, ctxN_hi[:, j, :], el, start=False, stop=False)
                        ins = pe.matmul(out, ctxN_lo[:, j, :], eh, start=False, stop=(j == KB - 1))
                    ins.then_inc(pv_thirds, 1)

                def project(G, pair):
                    if pair == 0:
                        pe.wait_ge(o_copied, G + 2)
                        pe.wait_ge(q_copied, G + 2)
                    for i in range(2):
                        h = 2 * pair + i
                        ins = pe.matmul((misc, O_ps)[pair][0:Q, D * i:D * (i + 1)], OT[:, h, :], Bw[:, HG * group_of(G) + h, :],
                                        start=True, stop=True)
                    ins.then_inc(y_ready, 1)

                def step(G, lag, new):
                    for s in range(SLOTS):
                        h, c = divmod(s, 3)
                        scores(G, h, c)
                        if s >= 6 or lag:
                            turn(G - (s < 6), (h + 2) % HG, c)
                        if s in (QN, QN + 1):
                            q_natural(G + 1, s - QN)
                        if s == QN + 4:
                            q_turn(G + 1)
                        if lag and s in (6, 7, 8):
                            context_product(G - 1, s - 6)
                        if lag and s == 11:
                            for pair in range(2):
                                project(G - 1, pair)

                def drain(G):
                    for h in (2, 3):
                        for t in range(NT):
                            turn(G - 1, h, t)
                    for t in range(NT):
                        context_product(G - 1, t)
                    for pair in range(2):
                        project(G - 1, pair)

                pe.sem_inc(y_ready, 1)
                q_natural(0, 0)
                q_natural(0, 1)
                q_turn(0)
                pe.wait_ge(zeroed, 2)

                run(pe, step, drain)

            @block.vector
            def _(dve):
                def split_T(b, slot, c):
                    lo, w = CHUNKS[c]
                    dve.wait_ge(ctxT_hi_s, 3 * b + c + 1)
                    dve.tensor_tensor(ctxT_lo[:, slot, lo:lo + w], ctxT_raw[:, lo:lo + w],
                                      ctxT_hi[:, slot, lo:lo + w], ALU.subtract).then_inc(ctxT_split, 1)

                def make_side(b, c):
                    lo, w = CHUNKS[c]
                    if c == 0:
                        dve.wait_ge(side_loaded, 16 * (b + 1))
                    dve.tensor_scalar(side[0:Q, 0, lo:lo + w], mask_u8[0:Q, lo:lo + w], BIG, -BIG, ALU.mult, ALU.add)\
                       .then_inc(side_made, 1)
                    dve.wait_ge(side_made, 4 * b + c + 1)

                def find_seen(b):
                    dve.tensor_reduce(seen[0:Q, bass.ds(b % 2, 1)], mask_u8[0:Q, :], AX_X, ALU.max)\
                       .then_inc(side_made, 1)

                def split_N(b, t):
                    js = slice(TB * t, TB * (t + 1))
                    dve.wait_ge(ctxN_hi_s, 3 * b + t + 1)
                    dve.tensor_tensor(ctxN_lo[:, js, :], ctxN_raw[:, js, :], ctxN_hi[:, js, :],
                                      ALU.subtract).then_inc(ctxN_split, 1)

                def soft(G, h, c):
                    lo, w = CHUNKS[c]
                    n3 = 3 * h + c
                    dve.wait_ge(scores_ready, 12 * G + n3 + 1)
                    if rms and c == 0:
                        dve.wait_ge(r_loaded[h], 16 * (G + 1))
                    if c == 0 and not (isinstance(G, int) and G == 0):
                        dve.wait_ge(turned, 12 * (G - 1) + NT * (h + 1))
                    dve.sem_inc(passed, 1)
                    dve.tensor_tensor_reduce(E[0:Q, h, lo:lo + w], S_ps[n3 % 2][0:Q, 0:w],
                                             side[0:Q, h if rms else 0, lo:lo + w], 1.0, -3.0e38,
                                             ALU.mult if rms else ALU.add, ALU.max,
                                             mx[0:Q, h, c:c + 1]).then_inc(scores_taken, 1)

                def maximum(G, h):
                    dve.wait_ge(scores_taken, 12 * G + 3 * (h + 1))
                    dve.tensor_reduce(negm[0:Q, h:h + 1], mx[0:Q, h, :], AX_X, ALU.max, negate=True)\
                       .then_inc(max_ready, 1)

                def x_low(G):
                    dve.wait_ge(xhi_s, G + 1)
                    dve.tensor_tensor(xs_lo[:], xnT[:, :, batch_of(G), :], xs_hi[:], ALU.subtract).then_inc(xlo_s, 1)

                def scale_q(G):
                    dve.wait_ge(qnat_ready, G + 1)
                    if not (isinstance(G, int) and G == 0):
                        dve.wait_ge(qT_ready, G)
                    s = sc[0:Q, bass.ds(H * batch_of(G) + HG * group_of(G), HG)]
                    dve.tensor_tensor(qn[0:Q, :, :], misc[0:Q, :].rearrange("p (h n) -> p h n", h=HG),
                                      s.unsqueeze(2).to_broadcast([Q, HG, C]), ALU.mult).then_inc(qn_scaled, 1)

                def q_low(G, h):
                    dve.wait_ge(qhi_s, HG * G + h + 1)
                    dve.tensor_tensor(q_lo[:, h, :], qT[:, h, :], q_hi[:, h, :],
                                      ALU.subtract).then_inc(qlo_s, 1)

                def e_low(G, h, t):
                    n3 = NT * h + t
                    dve.wait_ge(ehi_s, 12 * G + n3 + 1)
                    dve.tensor_tensor(e_lo[:, TB * t:TB * (t + 1), h, :],
                                      T_ps[n3 % 3][:, :].rearrange("p (j q) -> p j q", j=TB)[:, :, 0:Q],
                                      e_hi[:, TB * t:TB * (t + 1), h, :], ALU.subtract).then_inc(elo_s, 1)

                def reciprocals(G):
                    k_s = 2 if rms else 3
                    dve.wait_ge(exp_done, 12 * (G + 1))
                    dve.tensor_reduce(rden[0:Q, :], den[0:Q, bass.ds(12 * (G % 2), 12)]
                                      .rearrange("p (h c) -> p h c", c=3), AX_X, ALU.add).then_inc(rden_s, 1)
                    dve.wait_ge(rden_s, k_s * G + 1)
                    dve.reciprocal(rden[0:Q, :], rden[0:Q, :]).then_inc(rden_s, 1)
                    if not rms:
                        dve.wait_ge(side_made, 4 * (batch_of(G) + 1))
                        dve.wait_ge(rden_s, k_s * G + 2)
                        dve.tensor_scalar(rden[0:Q, :], rden[0:Q, :], seen[0:Q, bass.ds(batch_of(G) % 2, 1)], None,
                                          ALU.mult).then_inc(rden_s, 1)

                def add_y(G, pair):
                    dve.wait_ge(y_ready, 2 * G + pair + 2)
                    if pair == 0:
                        dve.wait_ge(rden_s, (2 if rms else 3) * (G + 1))
                    for i in range(2):
                        h = 2 * pair + i
                        dve.wait_ge(y_added, 4 * G + h + 1)
                        x = X[0:Q, batch_of(G), :]
                        dve.scalar_tensor_tensor(out=x, in0=(misc, O_ps)[pair][0:Q, D * i:D * (i + 1)], scalar=rden[0:Q, h:h + 1],
                                                 in1=x, op0=ALU.mult, op1=ALU.add).then_inc(y_added, 1)

                def step(G, lag, new):
                    for s in range(SLOTS):
                        h, c = divmod(s, 3)
                        if new and not rms and s < 3:
                            make_side(batch_of(G), c)
                        soft(G, h, c)
                        if new and not rms and s == SEEN_AT:
                            find_seen(batch_of(G))
                        if c == 2:
                            maximum(G, h)
                        if s == QN + 4:
                            x_low(G + 2)
                        if s == QN + 2:
                            scale_q(G + 1)
                        if s >= 7:
                            e_low(G, (s - 7) // 3, (s - 7) % 3)
                        elif lag:
                            e_low(G - 1, (s + 5) // 3, (s + 5) % 3)
                        if s in (QN + 5, QN + 6, QN + 8):
                            q_low(G + 1, {QN + 5: 0, QN + 6: 1, QN + 8: 2}[s])
                        if lag and s == 6:
                            reciprocals(G - 1)
                        if lag and s == 11:
                            add_y(G - 1, 0)
                        if new and s in (7, 8, 9):
                            split_T(batch_of(G) + 1, (batch_of(G) + 1) % 2, s - 7)
                        if new and s >= 10:
                            split_N(batch_of(G), s - 10)
                    if lag:
                        add_y(G - 1, 1)
                    q_low(G + 1, 3)
                    if new:
                        split_N(batch_of(G), 2)

                def drain(G):
                    for i in range(5, 12):
                        e_low(G - 1, i // 3, i % 3)
                    reciprocals(G - 1)
                    for pair in range(2):
                        add_y(G - 1, pair)
                    dve.wait_ge(y_added, 4 * G + 1)

                dve.sem_inc(y_added, 1)
                for c in range(3):
                    split_T(0, 0, c)
                x_low(0)
                scale_q(0)
                for h in range(HG):
                    q_low(0, h)
                x_low(1)
                dve.wait_ge(zeroed, 2)
                run(dve, step, drain)

            @block.scalar
            def _(act):
                def split_T(b, slot, c):
                    lo, w = CHUNKS[c]
                    act.wait_ge(ctxT_loaded, 16 * (b + 1))
                    act.activation(ctxT_hi[:, slot, lo:lo + w], ctxT_raw[:, lo:lo + w], ACT.Copy)\
                       .then_inc(ctxT_hi_s, 1)

                def split_N(b, t):
                    js = slice(TB * t, TB * (t + 1))
                    act.wait_ge(ctxN_loaded, 32 * (b + 1))
                    if not (isinstance(b, int) and b == 0):
                        act.wait_ge(pv_thirds, NT * NG * b)
                    act.activation(ctxN_hi[:, js, :], ctxN_raw[:, js, :], ACT.Copy).then_inc(ctxN_hi_s, 1)

                def copy_x(G):
                    if not (isinstance(G, int) and G == 0):
                        act.wait_ge(qnat_ready, G)
                    act.activation(xs_hi[:], xnT[:, :, batch_of(G), :], ACT.Copy).then_inc(xhi_s, 1)

                def exps(G, h, c):
                    lo, w = CHUNKS[c]
                    if c == 0:
                        act.wait_ge(max_ready, HG * G + h + 1)
                    act.activation(E[0:Q, h, lo:lo + w], E[0:Q, h, lo:lo + w], ACT.Exp, bias=negm[0:Q, h:h + 1],
                                   accum_out=den[0:Q, bass.ds(12 * (G % 2) + 3 * h + c, 1)]).then_inc(exp_done, 1)

                def copy_q(G):
                    act.wait_ge(qT_ready, G + 1)
                    if not (isinstance(G, int) and G == 0):
                        act.wait_ge(qlo_s, HG * G)
                    act.activation(qT[:].rearrange("p h q -> p (h q)"), misc[:, 0:HG * Q], ACT.Copy)\
                       .then_inc(q_copied, 1)
                    act.wait_ge(q_copied, G + 1)

                def q_high(G, h):
                    if not (isinstance(G, int) and G == 0):
                        act.wait_ge(scores_ready, 12 * (G - 1) + 3 * (h + 1))
                    act.activation(q_hi[:, h, :], qT[:, h, :], ACT.Copy).then_inc(qhi_s, 1)

                def e_high(G, h, t):
                    n3 = NT * h + t
                    act.wait_ge(turned, 12 * G + n3 + 1)
                    if h == 0 and not (isinstance(G, int) and G == 0):
                        act.wait_ge(pv_thirds, NT * (G - 1) + t + 1)
                    act.activation(e_hi[:, TB * t:TB * (t + 1), h, :],
                                   T_ps[n3 % 3][:, :].rearrange("p (j q) -> p j q", j=TB)[:, :, 0:Q],
                                   ACT.Copy).then_inc(ehi_s, 1)

                def copy_o(G):
                    act.wait_ge(pv_thirds, NT * (G + 1))
                    act.wait_ge(y_ready, 2 * G + 1)
                    act.activation(OT[:].rearrange("p h q -> p (h q)"), O_ps[:, 0:HG * Q], ACT.Copy)\
                       .then_inc(o_copied, 1)

                def step(G, lag, new):
                    for s in range(SLOTS):
                        h, c = divmod(s, 3)
                        if s >= 6 or lag:
                            e_high(G - (s < 6), (h + 2) % HG, c)
                        if s >= 3:
                            exps(G, h - 1, c)
                        elif lag:
                            exps(G - 1, HG - 1, c)
                        if s == QN + 3:
                            copy_x(G + 2)
                        if s == QN + 4:
                            copy_q(G + 1)
                        if s in (QN + 5, QN + 6, QN + 7):
                            q_high(G + 1, s - QN - 5)
                        if lag and s == 8:
                            copy_o(G - 1)
                        if new and s in (5, 6, 7):
                            split_T(batch_of(G) + 1, (batch_of(G) + 1) % 2, s - 5)
                        if new and s >= 9:
                            split_N(batch_of(G), s - 9)
                    q_high(G + 1, 3)

                def drain(G):
                    for c in range(3):
                        exps(G - 1, HG - 1, c)
                    for i in range(6, 12):
                        e_high(G - 1, i // 3, i % 3)
                    copy_o(G - 1)

                act.sem_inc(o_copied, 1)
                act.wait_ge(zeroed, 2)
                copy_x(0)
                for c in range(3):
                    split_T(0, 0, c)
                copy_q(0)
                for h in range(HG):
                    q_high(0, h)
                copy_x(1)
                run(act, step, drain)
    k.phase = k.whole


def ternary_phase(k, X, xnT, w, r, win):
    nc = k.nc
    w_s, mm, added = k.sem("ffn_w"), k.sem("ffn_mm"), k.sem("ffn_added")
    with ExitStack() as k.phase:
        a, b2 = k.sb("ffn_a", [128, DC, D]), k.sb("ffn_b", [128, DC, D])
        ps = k.ps("ffn_ps", [128, NB, 512])
        with nc.Block() as block:
            @block.vector
            def _(dve):
                chain = Count(w_s)
                dve.wait_ge(win, 32)
                chain.by(dve.tensor_scalar(a[:], w[:], 0.2, 0.6, ALU.is_gt, ALU.mult))
                chain.then_wait(dve, dve.tensor_scalar(b2[:], w[:], -0.2, 0.6, ALU.is_lt, ALU.mult))
                chain.then_wait(dve, dve.tensor_tensor(a[:], a[:], b2[:], ALU.subtract))
                chain.by(dve.tensor_tensor(w[:], a[:], r[:], ALU.add))
                for b in range(NB):
                    dve.wait_ge(mm, b + 1)
                    dve.tensor_tensor(X[0:Q, b, :], X[0:Q, b, :], ps[0:Q, b, 0:D],
                                      ALU.add).then_inc(added, 1)
                dve.wait_ge(added, NB)

            @block.tensor
            def _(pe):
                pe.wait_ge(w_s, 4)
                for b in range(NB):
                    for c in range(DC):
                        ins = pe.matmul(ps[0:Q, b, 0:D], xnT[:, c, b, :], w[:, c, :],
                                        start=(c == 0), stop=(c == DC - 1))
                    ins.then_inc(mm, 1)
    k.phase = k.whole


def ternary(dve, chain, xn, u, w):
    chain.by(dve.tensor_scalar(u[0:Q], xn[0:Q], 0.33, 0.5, ALU.is_gt, ALU.mult))
    chain.then_wait(dve, dve.tensor_scalar(w[0:Q], xn[0:Q], -0.33, 0.5, ALU.is_lt, ALU.mult))
    chain.then_wait(dve, dve.tensor_tensor(xn[0:Q], u[0:Q], w[0:Q], ALU.subtract))


def query_norm_phase(k, xnT, Wq, win, sc):
    nc = k.nc
    mm, sq_s, red_s, root_s, dve_s, hi_s, lo_s = (
        k.sem(f"qn_{n}") for n in ("mm", "sq", "red", "root", "dve", "hi", "lo"))
    with ExitStack() as k.phase:
        x_hi, x_lo = (k.sb(f"qn_x{n}", [128, DC, NB, Q], F32R) for n in ("hi", "lo"))
        W_hi, W_lo = (k.sb(f"qn_W{n}", [128, 2, DC, 512], F32R) for n in ("hi", "lo"))
        sq = k.sb("qn_sqb", [128, 4, 512])
        ss, root, t = k.sb("qn_ss", [128, NB * H]), k.sb("qn_rootv", [128, NB * H]), k.sb("qn_t", [128, NB * H])
        ps = k.ps("qn_ps", [128, 4, 512])
        with nc.Block() as block:
            @block.tensor
            def _(pe):
                for n in range(STEPS):
                    g, b = divmod(n, NB)
                    if b == 0:
                        pe.wait_ge(lo_s, g + 2)
                    if n >= 4:
                        pe.wait_ge(sq_s, n - 3)
                    for c in range(DC):
                        pe.matmul(ps[0:Q, n % 4, :], x_hi[:, c, b, :], W_hi[:, g % 2, c, :], start=(c == 0), stop=False)
                        pe.matmul(ps[0:Q, n % 4, :], x_hi[:, c, b, :], W_lo[:, g % 2, c, :], start=False, stop=False)
                        ins = pe.matmul(ps[0:Q, n % 4, :], x_lo[:, c, b, :], W_hi[:, g % 2, c, :],
                                        start=False, stop=(c == DC - 1))
                    ins.then_inc(mm, 1)

            @block.scalar
            def _(act):
                def split(g):
                    if g >= 2:
                        act.wait_ge(mm, NB * (g - 1))
                    act.activation(W_hi[:, g % 2], Wq[:, :, 512 * g:512 * (g + 1)], ACT.Copy).then_inc(hi_s, 1)

                act.activation(x_hi[:], xnT[:], ACT.Copy).then_inc(hi_s, 1)
                act.wait_ge(win, 32)
                split(0)
                split(1)
                for n in range(STEPS):
                    g, b = divmod(n, NB)
                    if b == 1 and 1 <= g < NG - 1:
                        split(g + 1)
                    act.wait_ge(mm, n + 1)
                    if n >= 4:
                        act.wait_ge(red_s, n - 3)
                    act.activation(sq[0:Q, n % 4, :], ps[0:Q, n % 4, :], ACT.Square).then_inc(sq_s, 1)
                act.wait_ge(dve_s, 1)
                act.activation(root[0:Q, :], ss[0:Q, :], ACT.Sqrt).then_inc(root_s, 1)

            @block.vector
            def _(dve):
                def split(g):
                    dve.wait_ge(hi_s, g + 2)
                    dve.tensor_tensor(W_lo[:, g % 2], Wq[:, :, 512 * g:512 * (g + 1)], W_hi[:, g % 2],
                                      ALU.subtract).then_inc(lo_s, 1)

                dve.wait_ge(hi_s, 1)
                dve.tensor_tensor(x_lo[:], xnT[:], x_hi[:], ALU.subtract).then_inc(lo_s, 1)
                split(0)
                split(1)
                for n in range(STEPS):
                    g, b = divmod(n, NB)
                    if b == 1 and 1 <= g < NG - 1:
                        split(g + 1)
                    dve.wait_ge(sq_s, n + 1)
                    dve.tensor_reduce(ss[0:Q, H * b + HG * g:H * b + HG * (g + 1)],
                                      sq[0:Q, n % 4, :].rearrange("p (h d) -> p h d", h=HG), AX_X,
                                      ALU.add).then_inc(red_s, 1)
                dve.wait_ge(red_s, STEPS)
                chain = Count(dve_s)
                chain.then_wait(dve, dve.tensor_scalar(ss[0:Q, :], ss[0:Q, :], 1.0 / HD, LN_EPS, ALU.mult, ALU.add))
                dve.wait_ge(root_s, 1)
                newton_rsqrt(dve, chain, ss[0:Q, :], root[0:Q, :], sc[0:Q, :], t[0:Q, :])
                chain.then_wait(dve, dve.tensor_scalar(sc[0:Q, :], sc[0:Q, :], INV, None, ALU.mult))
    k.phase = k.whole


def key_norm_phase(k, ident, ctxT_in, Wk_in, r_out, rows_out, load_ahead):
    nc = k.nc
    sem = lambda n: k.sem(f"kn_{n}")
    win, whi, wlo = sem("w_in"), sem("w_hi"), sem("w_lo")
    raw_in, chi, clo, mm, sq_s, red_s = (sem(n) for n in ("raw_in", "ctx_hi", "ctx_lo", "mm", "sq", "red"))
    zero_s, root_s, var_s, chain_s, turned, r_s, rows_s, stored, passed, passed_pe, passed_pool, cleared = (
        sem(n) for n in ("zero", "root", "var", "chain", "turned", "r", "rows", "stored", "passed", "passed_pe", "passed_pool", "cleared"))
    W = H * HD
    NCH = W // 512
    CHAIN = 4
    CLEARS = 16
    width = -(-TILES * RW // CLEARS)
    with ExitStack() as k.phase:
        Wk, Wk_hi, Wk_lo = k.sb("kn_W", [128, W]), k.sb("kn_Wh", [128, W], F32R), k.sb("kn_Wl", [128, W], F32R)
        raw = k.sb("kn_raw", [128, 2, KB * 128])
        c_hi, c_lo = k.sb("kn_ch", [128, KB, 128], F32R), k.sb("kn_cl", [128, KB, 128], F32R)
        sq = k.sb("kn_sqb", [128, 4, 512])
        ss = k.sb("kn_ss", [128, 2, KB, H])
        root, r, t = (k.sb(f"kn_{n}", [128, KB, H]) for n in ("rootv", "r", "t"))
        rows = k.sb("kn_rowsb", [128, NT, 512])
        zero = k.sb("kn_zeros", [128, width])
        ps = k.ps("kn_ps", [128, 4, 512])
        tp = k.ps("kn_tp", [128, NT, 512])
        with nc.Block() as block:
            @block.gpsimd
            def _(pool):
                pool.memset(raw[:, :, KEYS:], 0.0).then_inc(zero_s, 1)
                pool.memset(zero[:], 0.0).then_inc(zero_s, 1)
                pool.wait_ge(zero_s, 2)

                def split(b, j):
                    pool.wait_ge(chi, KB * b + j + 1)
                    pool.sem_inc(passed_pool, 1)
                    pool.tensor_tensor(c_lo[:, j, :], raw[:, b % 2, 128 * j:128 * (j + 1)], c_hi[:, j, :],
                                       ALU.subtract).then_inc(clo, 1)

                with pool.Fori(0, NB) as b:
                    for j in range(KB):
                        split(b, j)

            @block.sync
            def _(sp):
                def load(b):
                    sp.dma_start(raw[:, b % 2, 0:KEYS], ctxT_in[b % NB]).then_inc(raw_in, 16)

                def store(b):
                    sp.wait_ge(rows_s, b + 2)
                    sp.sem_inc(passed, 1)
                    sp.dma_start(r_out[b], rows[0:H, :, :].rearrange("p t n -> p (t n)")[:, 0:KEYS])\
                      .then_inc(stored, 16)

                sp.dma_start(Wk[:], Wk_in).then_inc(win, 16)
                sp.sem_inc(stored, 1)
                load(0)
                sp.wait_ge(clo, 1)
                load(1)
                load_ahead(sp)
                sp.wait_ge(zero_s, 2)
                flat = rows_out.rearrange("(p a) d -> p (a d)", p=128)
                for i in range(CLEARS):
                    w = min(width, TILES * RW - width * i)
                    sp.dma_start(flat[:, width * i:width * i + w], zero[:, 0:w]).then_inc(cleared, 16)
                with sp.Fori(1, NB) as b:
                    sp.wait_ge(clo, KB * b + 1)
                    sp.sem_inc(passed, 1)
                    load(b + 1)
                    store(b - 1)
                store(NB - 1)
                sp.wait_ge(stored, 16 * NB + 1)
                sp.wait_ge(raw_in, 16 * (NB + 1))
                sp.wait_ge(cleared, 16 * CLEARS)

            @block.tensor
            def _(pe):
                def turn(b):
                    pe.wait_ge(r_s, b + 1)
                    pe.wait_ge(rows_s, b + 1)
                    pe.sem_inc(passed_pe, 1)
                    for j in range(KB):
                        ins = pe.transpose(tp[0:H, j // 4, 128 * (j % 4):128 * (j % 4 + 1)], r[:, j, :], ident[:])
                    ins.then_inc(turned, 1)

                def batch(b, lag):
                    for j in range(KB):
                        pe.wait_ge(clo, KB * b + j + 1)
                        for m in range(NCH):
                            n = NCH * j + m
                            out = ps[:, n % 4, :]
                            pe.wait_ge(sq_s, NCH * KB * b + n + 1)
                            ws = slice(512 * m, 512 * (m + 1))
                            pe.matmul(out, c_hi[:, j, :], Wk_hi[:, ws], start=True, stop=False)
                            pe.matmul(out, c_hi[:, j, :], Wk_lo[:, ws], start=False, stop=False)
                            pe.matmul(out, c_lo[:, j, :], Wk_hi[:, ws], start=False, stop=True).then_inc(mm, 1)
                        if lag and j == 6:
                            turn(b - 1)

                pe.sem_inc(turned, 1)
                pe.wait_ge(wlo, NCH)
                pe.wait_ge(zero_s, 1)
                batch(0, False)
                with pe.Fori(1, NB) as b:
                    batch(b, True)
                turn(NB - 1)

            @block.scalar
            def _(act):
                def take_root(b):
                    act.wait_ge(var_s, b + 1)
                    act.activation(root[:], ss[:, b % 2, :, :], ACT.Sqrt).then_inc(root_s, 1)

                def take_rows(b):
                    act.wait_ge(turned, b + 2)
                    act.wait_ge(stored, 16 * b + 1)
                    act.activation(rows[0:H, :, :], tp[0:H, :, :], ACT.Copy).then_inc(rows_s, 1)

                def split(b, j):
                    act.activation(c_hi[:, j, :], raw[:, b % 2, 128 * j:128 * (j + 1)], ACT.Copy).then_inc(chi, 1)

                def batch(b, lag):
                    act.wait_ge(raw_in, 16 * (b + 1))
                    split(b, 0)
                    for j in range(KB):
                        if j + 1 < KB:
                            split(b, j + 1)
                        for m in range(NCH):
                            n = NCH * j + m
                            act.wait_ge(mm, NCH * KB * b + n + 1)
                            act.wait_ge(red_s, NCH * KB * b + n + 1)
                            act.activation(sq[:, n % 4, :], ps[:, n % 4, :], ACT.Square).then_inc(sq_s, 1)
                        if lag and j == 1:
                            take_root(b - 1)
                        if lag and j == 8:
                            take_rows(b - 1)

                act.sem_inc(rows_s, 1)
                act.wait_ge(win, 16)
                for m in range(NCH):
                    ws = slice(512 * m, 512 * (m + 1))
                    act.activation(Wk_hi[:, ws], Wk[:, ws], ACT.Copy).then_inc(whi, 1)
                act.wait_ge(zero_s, 1)
                for i in range(4):
                    act.activation(sq[:, i, 0:1], Wk[:, 0:1], ACT.Copy).then_inc(sq_s, 1)
                batch(0, False)
                with act.Fori(1, NB) as b:
                    batch(b, True)
                take_root(NB - 1)
                take_rows(NB - 1)

            @block.vector
            def _(dve):
                def variances(b):
                    dve.wait_ge(red_s, NCH * KB * (b + 1) + 4)
                    v = ss[:, b % 2, :, :]
                    dve.tensor_scalar(v, v, 1.0 / HD, LN_EPS, ALU.mult, ALU.add).then_inc(var_s, 1)

                def norm(b, i):
                    if i == 0:
                        dve.wait_ge(root_s, b + 1)
                        dve.wait_ge(var_s, b + 1)
                        dve.wait_ge(turned, b + 1)
                        ins = dve.reciprocal(r[:], root[:])
                    else:
                        dve.wait_ge(chain_s, CHAIN * b + i)
                        if i == 1:
                            ins = dve.tensor_tensor(t[:], r[:], r[:], ALU.mult)
                        elif i == 2:
                            ins = dve.tensor_tensor(t[:], t[:], ss[:, b % 2, :, :], ALU.mult)
                        elif i == 3:
                            ins = dve.tensor_scalar(t[:], t[:], -0.5, 1.5, ALU.mult, ALU.add)
                        else:
                            ins = dve.tensor_tensor(r[:], r[:], t[:], ALU.mult)
                    ins.then_inc(chain_s if i < CHAIN else r_s, 1)

                def batch(b, lag):
                    for j in range(KB):
                        for m in range(NCH):
                            n = NCH * j + m
                            dve.wait_ge(sq_s, NCH * KB * b + n + 5)
                            dve.tensor_reduce(ss[:, b % 2, j, HG * m:HG * (m + 1)],
                                              sq[:, n % 4, :].rearrange("p (h d) -> p h d", h=HG), AX_X,
                                              ALU.add).then_inc(red_s, 1)
                            if lag and 0 <= n - 2 * NCH <= CHAIN:
                                norm(b - 1, n - 2 * NCH)
                        if lag and j == 0:
                            variances(b - 1)

                for m in range(NCH):
                    ws = slice(512 * m, 512 * (m + 1))
                    dve.wait_ge(whi, m + 1)
                    dve.tensor_tensor(Wk_lo[:, ws], Wk[:, ws], Wk_hi[:, ws], ALU.subtract).then_inc(wlo, 1)
                dve.wait_ge(sq_s, 4)
                for i in range(4):
                    dve.memset(t[:, 0, i:i + 1], 0.0).then_inc(red_s, 1)
                batch(0, False)
                with dve.Fori(1, NB) as b:
                    batch(b, True)
                variances(NB - 1)
                for i in range(CHAIN + 1):
                    norm(NB - 1, i)
    k.phase = k.whole


ROUTED = 64
TOPK = 6
FFN = 176
SHARED = 2
NF = 2
FC = 96
FS = FFN - FC
RT = 128
TILES = (NB * Q * TOPK + ROUTED * (RT - 1)) // RT
ROWS = TILES * RT
FAR = 16384.0
U0 = NB * SHARED
UNITS = U0 + TILES
RW = D + 1
PAIRS = NB * Q * TOPK
WS = 8
STORE_LAG = 5


def router_phase(k, xn, xnT, ident, gateT_in, p, tot, chosen, place, key, tile_expert, copies, spare):
    nc = k.nc
    sem = lambda n: k.sem(f"rt_{n}")
    gin, mm, chain_s, exp_s, neg_s, picked, made, counted, numbered, spread = (
        sem(n) for n in ("in", "mm", "chain", "exp", "neg", "picked", "made", "counted", "numbered", "spread"))
    copied = sem("copied")
    with ExitStack() as k.phase:
        gate = k.sb("rt_gate", [128, DC, ROUTED])
        ones, before = k.sb("rt_ones", [128, 128]), k.sb("rt_before", [128, 128])
        neg, Z = k.sb("rt_negm", [128, NB]), k.sb("rt_Z", [128, NB])
        top, rest = k.sb("rt_top", [128, NB, 8]), k.sb("rt_rest", [128, NB, ROUTED])
        mask, seen = k.sb("rt_mask", [128, NB, ROUTED]), k.sb("rt_seen", [128, NB, ROUTED])
        count, tiles = k.sb("rt_count", [128, ROUTED]), k.sb("rt_tiles", [128, 2, ROUTED])
        ends, first = k.sb("rt_ends", [128, 2, ROUTED]), k.sb("rt_first", [128, ROUTED])
        number, expert, le = k.sb("rt_number", [128, 1]), k.sb("rt_expert", [128, 1]), k.sb("rt_le", [128, ROUTED])
        ids, first_spare = k.sb("rt_ids", [128, TOPK, NB], I32), k.sb("rt_first_spare", [128, 1], I32)
        ps = k.ps("rt_ps", [128, NB, ROUTED])
        rank = k.ps("rt_rank", [128, NB, ROUTED])
        misc = k.ps("rt_misc", [128, 512])
        numps = k.ps("rt_numps", [128, 512])
        with nc.Block() as block:
            @block.sync
            def _(sp):
                sp.dma_start(gate[:], gateT_in).then_inc(gin, 16)
                sp.wait_ge(gin, 16)

            @block.gpsimd
            def _(pool):
                chain = Count(made)
                chain.then_wait(pool, pool.memset(ones[:], 1.0))
                chain.then_wait(pool, pool.affine_select(out=before[:], in_=ones[:], compare_op=ALU.is_gt, fill=0.0,
                                                         base=0, pattern=[[1, 128]], channel_multiplier=-1))
                pool.iota(ids[:], pattern=[[1, TOPK], [Q * TOPK, NB]], base=1, channel_multiplier=TOPK)\
                    .then_inc(copied, 1)
                pool.iota(first_spare[:], pattern=[[0, 1]], base=PAIRS + 1, channel_multiplier=1).then_inc(copied, 1)
                pool.wait_ge(copied, 2)
                pool.tensor_copy(copies[:, :, :, D], ids[:]).then_inc(made, 1)
                pool.tensor_copy(spare[:], first_spare[:]).then_inc(made, 1)

            @block.tensor
            def _(pe):
                pe.wait_ge(gin, 16)
                for b in range(NB):
                    for c in range(DC):
                        ins = pe.matmul(ps[0:Q, b, :], xnT[:, c, b, :], gate[:, c, :],
                                        start=(c == 0), stop=(c == DC - 1))
                ins.then_inc(mm, 1)
                pe.wait_ge(made, 2)
                pe.matmul(numps[:, 0:1], before[:], ones[:, 0:1], start=True, stop=True).then_inc(numbered, 1)
                pe.wait_ge(picked, 1)
                pe.matmul(misc[:, 0:ROUTED], ones[0:Q, :], seen[0:Q, NB - 1, :], start=True, stop=True)\
                  .then_inc(counted, 1)
                for b in range(NB):
                    pe.matmul(rank[0:Q, b, :], before[0:Q, 0:Q], mask[0:Q, b, :], start=True, stop=(b == 0))
                    if b:
                        ins = pe.matmul(rank[0:Q, b, :], ones[0:Q, 0:Q], seen[0:Q, b - 1, :], start=False, stop=True)
                ins.then_inc(counted, 1)
                pe.wait_ge(spread, 1)
                pe.transpose(misc[0:1, 0:128], expert[:], ident[:]).then_inc(counted, 1)

            @block.scalar
            def _(act):
                act.wait_ge(neg_s, 1)
                for b in range(NB):
                    act.activation(p[0:Q, b, :], ps[0:Q, b, :], ACT.Exp, bias=neg[0:Q, b:b + 1],
                                   accum_out=Z[0:Q, b:b + 1]).then_inc(exp_s, 1)
                for i in range(TOPK):
                    act.activation(copies[0:Q, i, :, 0:D], xn[0:Q, :, :], ACT.Copy)

            @block.vector
            def _(dve):
                chain = Count(chain_s)
                dve.wait_ge(mm, 1)
                dve.tensor_reduce(neg[0:Q, :], ps[0:Q, :, :], AX_X, ALU.max, negate=True).then_inc(neg_s, 1)
                dve.wait_ge(exp_s, NB)
                chain.then_wait(dve, dve.reciprocal(Z[0:Q, :], Z[0:Q, :]))
                for b in range(NB):
                    chain.by(dve.tensor_scalar(p[0:Q, b, :], p[0:Q, b, :], Z[0:Q, b:b + 1], None, ALU.mult))
                dve.wait_ge(chain_s, chain.n)
                for b in range(NB):
                    chain.by(dve.max(top[0:Q, b, :], p[0:Q, b, :]))
                dve.wait_ge(chain_s, chain.n)
                chain.by(dve.tensor_reduce(tot[0:Q, :], top[0:Q, :, 0:TOPK], AX_X, ALU.add))
                chain.then_wait(dve, dve.memset(top[0:Q, :, TOPK:8], -2.0))
                for b in range(NB):
                    chain.by(dve.match_replace(rest[0:Q, b, :], top[0:Q, b, :], p[0:Q, b, :], -1.0))
                dve.wait_ge(chain_s, chain.n)
                chain.then_wait(dve, dve.tensor_scalar(mask[0:Q, :, :], rest[0:Q, :, :], 0.0, None, ALU.is_lt))
                chain.then_wait(dve, dve.tensor_copy(seen[0:Q, 0, :], mask[0:Q, 0, :]))
                for b in range(1, NB):
                    chain.then_wait(dve, dve.tensor_tensor(seen[0:Q, b, :], seen[0:Q, b - 1, :], mask[0:Q, b, :],
                                                           ALU.add))
                dve.memset(le[:, 0:1], 0.0).then_inc(picked, 1)
                chain.then_wait(dve, dve.tensor_scalar(tot[0:Q, :], tot[0:Q, :], 1e-20, None, ALU.add))
                chain.then_wait(dve, dve.reciprocal(tot[0:Q, :], tot[0:Q, :]))
                dve.wait_ge(numbered, 1)
                chain.by(dve.tensor_copy(number[:], numps[:, 0:1]))
                dve.wait_ge(counted, 1)
                chain.then_wait(dve, dve.tensor_copy(count[:], misc[:, 0:ROUTED]))
                chain.then_wait(dve, dve.tensor_scalar(tiles[:, 0, :], count[:], 0.0, None, ALU.is_gt))
                last = -(-NB * Q // RT) - 1
                for i in range(1, last + 1):
                    chain.then_wait(dve, dve.scalar_tensor_tensor(
                        out=tiles[:, i % 2, :], in0=count[:], scalar=float(RT * i), in1=tiles[:, 1 - i % 2, :],
                        op0=ALU.is_gt, op1=ALU.add))
                src, step, side = tiles[:, last % 2, :], 1, 0
                while step < ROUTED:
                    dst = ends[:, side, :]
                    chain.by(dve.tensor_copy(dst[:, 0:step], src[:, 0:step]))
                    chain.then_wait(dve, dve.tensor_tensor(dst[:, step:], src[:, step:], src[:, :ROUTED - step], ALU.add))
                    src, step, side = dst, 2 * step, 1 - side
                chain.then_wait(dve, dve.tensor_tensor(first[:], src, tiles[:, last % 2, :], ALU.subtract))
                chain.then_wait(dve, dve.tensor_scalar(le[:], first[:], number[:, 0:1], None, ALU.is_le))
                chain.then_wait(dve, dve.tensor_reduce(expert[:], le[:], AX_X, ALU.add))
                dve.tensor_scalar(expert[:], expert[:], -1.0, None, ALU.add).then_inc(spread, 1)
                chain.then_wait(dve, dve.tensor_scalar(first[:], first[:], -float(RT), FAR, ALU.mult, ALU.add))
                dve.wait_ge(counted, 2)
                chain.then_wait(dve, dve.scalar_tensor_tensor(
                    out=key[0:Q, :, :], in0=rank[0:Q, :, :], scalar=-1.0,
                    in1=first[0:Q, :].unsqueeze(1).to_broadcast([Q, NB, ROUTED]), op0=ALU.mult, op1=ALU.add))
                chain.then_wait(dve, dve.tensor_tensor(key[0:Q, :, :], key[0:Q, :, :], mask[0:Q, :, :], ALU.mult))
                for b in range(NB):
                    chain.by(dve.max(chosen[0:Q, b, :], key[0:Q, b, :]))
                dve.wait_ge(chain_s, chain.n)
                chain.by(dve.tensor_scalar(place[0:Q, :, :], chosen[0:Q, :, 0:TOPK], -1.0, FAR, ALU.mult, ALU.add))
                dve.wait_ge(counted, 3)
                chain.then_wait(dve, dve.tensor_copy(tile_expert[0:1, :], misc[0:1, 0:TILES]))
    k.phase = k.whole


def experts_phase(k, X, xnT, ident, p, tot, chosen, place, key, tile_expert, copies, spare, wgu_in, wd_in, rows_in,
                  results, out):
    nc = k.nc
    sem = lambda n: k.sem(f"ex_{n}")
    w_in = [sem(f"w_in{s}") for s in range(WS)]
    x_in = [sem(f"x_in{s}") for s in range(WS)]
    y_out = [sem(f"y_out{s}") for s in range(WS)]
    back = [sem(f"back{b}") for b in range(NB)]
    ids_s, passed_pool = sem("ids"), sem("pool_passed")
    shared_in, scattered, x_turned, x_ready, up_done, silu_done, act_done, act_turned, act_ready, down_done, \
        shared_added, y_ready, weight_s, added, stored = (
            sem(n) for n in ("shared_in", "scattered", "x_turned", "x_ready", "up", "silu", "act", "act_turned",
                             "act_ready", "down", "shared_added", "y_ready", "weight", "added", "stored"))
    with ExitStack() as k.phase:
        wgu, wd = k.sb("ex_wgu", [128, WS, DC, 2 * FFN]), k.sb("ex_wd", [128, WS, NF, D])
        sgu, sd = k.sb("ex_sgu", [128, SHARED, DC, 2 * FFN]), k.sb("ex_sd", [128, SHARED, NF, D])
        rows = k.sb("ex_rows", [128, WS, RW])
        unused, to = k.sb("ex_unused", [128, 1]), k.sb("ex_to", [128, WS], U32)
        rowsT = k.sb("ex_rowsT", [128, 2, DC, RT])
        silu, hid = k.sb("ex_silu", [128, 2, FFN]), k.sb("ex_hid", [128, 2, FFN])
        hidT = k.sb("ex_hidT", [128, 2, NF, RT])
        y = k.sb("ex_y", [128, WS, D])
        got = k.sb("ex_got", [128, NB, TOPK * D])
        eq, weight = k.sb("ex_eq", [128, NB, ROUTED]), k.sb("ex_weight", [128, NB, TOPK])
        gu_ps = k.ps("ex_gu_ps", [128, 2, 512])
        x_ps, hid_ps = k.ps("ex_x_ps", [128, 2, 512]), k.ps("ex_hid_ps", [128, 2, 512])
        y_ps = k.ps("ex_y_ps", [128, 2, 512])

        def run(engine, step):
            start = U0 + 2 * WS
            groups = (UNITS - 1 - start) // WS
            for n in range(start):
                step(n, n % WS, n // WS, True)
            with engine.Fori(start // WS, start // WS + groups) as g:
                for s in range(WS):
                    step(WS * g + s, s, g, False)
            for n in range(start + WS * groups, UNITS + 2):
                step(n, n % WS, n // WS, True)

        def unit(n, s, lag, peeled):
            m = n - lag
            return m, (s - lag) % WS, (not peeled) or 0 <= m < UNITS, (not peeled) or U0 <= m < UNITS

        def number_of(b, i):
            return 2 * TOPK * (b // 2) + 2 * i + b % 2 + 1

        with nc.Block() as block:
            @block.gpsimd
            def _(pool):
                for b in range(NB):
                    for i in range(TOPK):
                        pool.indirect_dma_start(rows_in, bass.IndirectOffsetOnAxis(place[0:Q, b, i:i + 1], 0),
                                                copies[0:Q, i, b, :], None).then_inc(scattered, 16)

                def step(n, s, g, peeled):
                    m, slot, _, tile = unit(n, s, 3, peeled)
                    if tile:
                        pool.wait_ge(ids_s, 3 * (m - U0) + 3)
                        pool.wait_ge(y_ready, m - U0 + 1)
                        pool.sem_inc(passed_pool, 1)
                        pool.indirect_dma_start(results, bass.IndirectOffsetOnAxis(to[:, slot:slot + 1], 0),
                                                y[:, slot, :], None).then_inc(y_out[slot], 16)
                run(pool, step)
                step(UNITS + 2, (UNITS + 2) % WS, (UNITS + 2) // WS, True)

            @block.sync
            def _(sp):
                for h in range(SHARED):
                    sp.dma_start(sgu[:, h], wgu_in[ROUTED + h]).then_inc(shared_in, 16)
                    sp.dma_start(sd[0:FC, h], wd_in[ROUTED + h]).then_inc(shared_in, 16)

                def weights(j, s):
                    e = sp.value_load(tile_expert[0:1, j:j + 1] if isinstance(j, int)
                                      else tile_expert[0:1, bass.ds(j, 1)], min_val=0, max_val=ROUTED - 1)
                    sp.dma_start(wgu[:, s], wgu_in[e]).then_inc(w_in[s], 16)
                    sp.dma_start(wd[0:FC, s], wd_in[e]).then_inc(w_in[s], 16)

                def tokens(j, s):
                    at = RT * j
                    sp.dma_start(rows[:, s, :], rows_in[at:at + RT] if isinstance(j, int)
                                 else rows_in[bass.ds(at, RT)]).then_inc(x_in[s], 16)

                for j in range(WS):
                    weights(j, j)
                sp.wait_ge(scattered, 16 * NB * TOPK)
                for j in range(WS):
                    tokens(j, j)

                def step(n, s, g, peeled):
                    m, _, _, tile = unit(n, s, 0, peeled)
                    if tile and (not peeled or m >= U0 + WS):
                        sp.wait_ge(down_done, m - WS + 1)
                        sp.sem_inc(passed, 1)
                        weights(m - U0, s)
                        tokens(m - U0, s)
                passed = sem("sp_passed")
                run(sp, step)
                for s in range(WS):
                    sp.wait_ge(y_out[s], 16 * ((TILES - 1 - s) // WS + 1))
                for b in range(NB):
                    at = Q * TOPK * b
                    sp.dma_start(got[0:Q, b, :], results[at:at + Q * TOPK].rearrange("(q i) d -> q (i d)", i=TOPK))\
                      .then_inc(back[b], 16)
                for b in range(NB):
                    sp.wait_ge(added, number_of(b, TOPK - 1))
                    sp.dma_start(out[b], X[0:Q, b, :]).then_inc(stored, 16)
                sp.wait_ge(stored, 16 * NB)

            @block.tensor
            def _(pe):
                def step(n, s, g, peeled):
                    m, _, real, tile = unit(n, s, 0, peeled)
                    if real:
                        if tile:
                            pe.wait_ge(w_in[s], 32 * (g - U0 // WS + 1))
                            pe.wait_ge(x_ready, m - U0 + 1)
                        elif m == 0:
                            pe.wait_ge(shared_in, 32 * SHARED)
                        if not peeled or m >= 2:
                            pe.wait_ge(act_done, m - 1)
                        rows_n = RT if tile else Q
                        for c in range(DC):
                            x = rowsT[:, s % 2, c, :] if tile else xnT[:, c, m // SHARED, :]
                            w = wgu[:, s, c, :] if tile else sgu[:, m % SHARED, c, :]
                            ins = pe.matmul(gu_ps[0:rows_n, s % 2, 0:2 * FFN], x, w, start=(c == 0),
                                            stop=(c == DC - 1))
                        ins.then_inc(up_done, 1)
                    m, slot, real, tile = unit(n, s, 1, peeled)
                    if real:
                        pe.wait_ge(act_done, m + 1)
                        if not peeled or m >= 2:
                            pe.wait_ge(act_ready, m - 1)
                        rows_n = RT if tile else Q
                        for f in range(NF):
                            ins = pe.transpose(hid_ps[0:FC, slot % 2, RT * f:RT * f + rows_n],
                                               hid[0:rows_n, slot % 2, FS * f:FS * f + FC], ident[0:rows_n, 0:rows_n])
                        ins.then_inc(act_turned, 1)
                    m, slot, real, tile = unit(n, s, -1, peeled)
                    if tile:
                        j = m - U0
                        pe.wait_ge(x_in[slot], 16 * (g - U0 // WS + (1 if s < WS - 1 else 2)))
                        if not peeled or j >= 2:
                            pe.wait_ge(x_ready, j - 1)
                        for c in range(DC):
                            ins = pe.transpose(x_ps[:, slot % 2, RT * c:RT * (c + 1)],
                                               rows[:, slot, 128 * c:128 * (c + 1)], ident[:])
                        ins.then_inc(x_turned, 1)
                    m, slot, real, tile = unit(n, s, 2, peeled)
                    if real:
                        pe.wait_ge(act_ready, m + 1)
                        if tile:
                            j = m - U0
                            if peeled and j < 2:
                                pe.wait_ge(shared_added, NB - 1 + j)
                            else:
                                pe.wait_ge(y_ready, j - 1)
                        elif m % SHARED == 0 and m >= 2 * SHARED:
                            pe.wait_ge(shared_added, m // SHARED - 1)
                        rows_n, bank = (RT, slot % 2) if tile else (Q, m // SHARED % 2)
                        for f in range(NF):
                            ins = pe.matmul(y_ps[0:rows_n, bank, 0:D], hidT[0:FC, slot % 2, f, 0:rows_n],
                                            wd[0:FC, slot, f, :] if tile else sd[0:FC, m % SHARED, f, :],
                                            start=(f == 0 and (tile or m % SHARED == 0)),
                                            stop=(f == NF - 1 and (tile or m % SHARED == SHARED - 1)))
                        ins.then_inc(down_done, 1)
                run(pe, step)

            @block.scalar
            def _(act):
                def step(n, s, g, peeled):
                    m, _, real, tile = unit(n, s, 0, peeled)
                    if real:
                        act.wait_ge(up_done, m + 1)
                        if not peeled or m >= 2:
                            act.wait_ge(act_done, m - 1)
                        rows_n = RT if tile else Q
                        act.activation(silu[0:rows_n, s % 2, :], gu_ps[0:rows_n, s % 2, 0:FFN], ACT.Silu)\
                           .then_inc(silu_done, 1)
                    m, slot, real, tile = unit(n, s, 2, peeled)
                    if tile:
                        j = m - U0
                        act.wait_ge(down_done, m + 1)
                        if not peeled or j >= WS:
                            act.wait_ge(y_out[slot], 16 * (g - U0 // WS - (1 if s < 2 else 0)))
                        act.copy(y[:, slot, :], y_ps[:, slot % 2, 0:D]).then_inc(y_ready, 1)
                run(act, step)

            @block.vector
            def _(dve):
                chain = Count(weight_s)

                def step(n, s, g, peeled):
                    m, slot, real, tile = unit(n, s, 1, peeled)
                    if real:
                        dve.wait_ge(act_turned, m + 1)
                        if not peeled or m >= 2:
                            dve.wait_ge(down_done, m - 1)
                        rows_n = RT if tile else Q
                        dve.tensor_copy(hidT[0:FC, slot % 2, :, 0:rows_n],
                                        hid_ps[0:FC, slot % 2, 0:NF * RT].rearrange("p (f r) -> p f r", f=NF)
                                        [:, :, 0:rows_n]).then_inc(act_ready, 1)
                    m, slot, real, tile = unit(n, s, -1, peeled)
                    if tile:
                        dve.wait_ge(x_turned, m - U0 + 1)
                        dve.wait_ge(up_done, m - 1)
                        dve.tensor_copy(rowsT[:, slot % 2, :, :].rearrange("p c r -> p (c r)"),
                                        x_ps[:, slot % 2, 0:DC * RT]).then_inc(x_ready, 1)
                        j = m - U0
                        if not peeled or j >= 1:
                            dve.wait_ge(ids_s, 3 * j)
                        if not peeled or j >= WS:
                            dve.wait_ge(y_out[slot], 16 * (g - U0 // WS + (1 if s == WS - 1 else 0)))
                        said = rows[:, slot, D:RW]
                        dve.tensor_scalar(unused[:], said, 0.0, spare[:, 0:1], ALU.is_equal, ALU.mult).then_inc(ids_s, 1)
                        dve.wait_ge(ids_s, 3 * j + 1)
                        dve.tensor_scalar(spare[:], spare[:], float(RT), None, ALU.add).then_inc(ids_s, 1)
                        dve.scalar_tensor_tensor(out=to[:, slot:slot + 1], in0=said, scalar=-1.0, in1=unused[:],
                                                 op0=ALU.add, op1=ALU.add).then_inc(ids_s, 1)
                    m, _, real, tile = unit(n, s, 0, peeled)
                    if real:
                        dve.wait_ge(silu_done, m + 1)
                        if not peeled or m >= 2:
                            dve.wait_ge(act_turned, m - 1)
                        rows_n = RT if tile else Q
                        dve.tensor_tensor(hid[0:rows_n, s % 2, :], gu_ps[0:rows_n, s % 2, FFN:2 * FFN],
                                          silu[0:rows_n, s % 2, :], ALU.mult).then_inc(act_done, 1)
                    m, _, real, tile = unit(n, s, 2, peeled)
                    if real and not tile and m % SHARED == SHARED - 1:
                        b = m // SHARED
                        dve.wait_ge(down_done, m + 1)
                        dve.tensor_tensor(X[0:Q, b, :], X[0:Q, b, :], y_ps[0:Q, b % 2, 0:D], ALU.add)\
                           .then_inc(shared_added, 1)
                    if peeled and n == U0 - 2:
                        weights_of_experts()

                def weights_of_experts():
                    for i in range(TOPK):
                        chain.then_wait(dve, dve.tensor_tensor(
                            eq[0:Q, :, :], key[0:Q, :, :],
                            chosen[0:Q, :, i:i + 1].to_broadcast([Q, NB, ROUTED]), ALU.is_equal))
                        chain.then_wait(dve, dve.tensor_tensor(eq[0:Q, :, :], eq[0:Q, :, :], p[0:Q, :, :], ALU.mult))
                        chain.then_wait(dve, dve.tensor_reduce(weight[0:Q, :, i:i + 1].rearrange("p b o -> p (b o)"),
                                                               eq[0:Q, :, :], AX_X, ALU.add))
                    chain.then_wait(dve, dve.tensor_tensor(
                        weight[0:Q, :, :], weight[0:Q, :, :],
                        tot[0:Q, :].unsqueeze(2).to_broadcast([Q, NB, TOPK]), ALU.mult))
                run(dve, step)
                dve.wait_ge(shared_added, NB)
                for b0 in range(0, NB, 2):
                    for i in range(TOPK):
                        for b in (b0, b0 + 1):
                            if i == 0:
                                dve.wait_ge(back[b], 16)
                            else:
                                dve.wait_ge(added, number_of(b, i - 1))
                            dve.scalar_tensor_tensor(out=X[0:Q, b, :], in0=got[0:Q, b, D * i:D * (i + 1)],
                                                     scalar=weight[0:Q, b, i:i + 1], in1=X[0:Q, b, :],
                                                     op0=ALU.mult, op1=ALU.add).then_inc(added, 1)
    k.phase = k.whole


def attention_layer(k, layer, X, xnT, ident, sc, a, r_rows, token_rows):
    nc = k.nc
    t, kv = f"l{layer}", (H // 2, H)[layer]
    with ExitStack() as held:
        hold = lambda stack, name, shape, dt=F32: stack.enter_context(nc.sbuf_tensor(name, shape, dt))
        A_hi, A_lo = (hold(held, f"{t}_A{n}", [128, DC, H, C], F32R) for n in ("hi", "lo"))
        Bw = hold(held, f"{t}_B", [128, H, D])
        with ExitStack() as early:
            weights = CombineWeights(k, early, f"{t}c", kv, [a[f"{n}{layer}"] for n in ("WqT", "WkT", "WvT", "Wo")],
                                     (a["gq"], a["gk"]) if layer else None)
            if layer == 0:
                x_loaded = setup_phase(k, a["x"], X, ident, sc, weights.load)

                def load(sp):
                    sp.wait_ge(x_loaded, 16)
            else:
                key_norm_phase(k, ident, a["ctxT"], a["Wk1"], r_rows.rearrange("(b h) k -> b h k", b=NB), token_rows,
                               weights.load)
                Wq, wq_in = hold(early, "qn_W", [128, DC, H * HD]), k.sem("qn_in")

                def load(sp):
                    for c in range(DC):
                        sp.dma_start(Wq[:, c, :], a["Wq1"][:, c, :]).then_inc(wq_in, 16)

            combine_phase(k, f"{t}c", kv, weights, load, A_hi, A_lo, Bw)
            with nc.sbuf_tensor(f"{t}_xn", [128, NB, D], F32) as xn:
                norm_phase(k, f"{t}n", X, ident, xn, xnT)
            if layer:
                query_norm_phase(k, xnT, Wq, wq_in, sc)
        attention_phase(k, t, bool(layer), X, xnT, ident, A_hi, A_lo, Bw, sc, a["ctxT"], a["ctxN"], a["mask"], r_rows)


def program(nc, a, out):
    with ExitStack() as whole:
        k = Core(nc, whole)
        X, ident = k.sb("X", [128, NB, D]), k.sb("ident", [128, 128])
        sc = k.sb("sc", [128, NB * H])
        xnT = k.sb("xnT", [128, DC, NB, Q])
        r_rows = nc.dram_tensor("r_rows", (NB * H, KEYS), F32).ap()
        token_rows = nc.dram_tensor("token_rows", (ROWS, RW), F32).ap()
        result_rows = nc.dram_tensor("result_rows", (PAIRS + ROWS, D), F32).ap()

        attention_layer(k, 0, X, xnT, ident, sc, a, r_rows, token_rows)
        with nc.sbuf_tensor("ffn_wt", [128, DC, D], F32) as w, nc.sbuf_tensor("ffn_r", [128, DC, D], F32) as r:
            w_in = k.sem("ffn_in")

            def load(sp):
                sp.dma_start(w[:], a["wT"]).then_inc(w_in, 16)
                sp.dma_start(r[:], a["rramT"]).then_inc(w_in, 16)

            with nc.sbuf_tensor("f0_xn", [128, NB, D], F32) as xn:
                norm_phase(k, "f0", X, ident, xn, xnT, after=ternary, load_ahead=load)
            ternary_phase(k, X, xnT, w, r, w_in)
        k.end_layer()

        attention_layer(k, 1, X, xnT, ident, sc, a, r_rows, token_rows)
        with ExitStack() as held:
            hold = lambda name, shape, dt=F32: held.enter_context(nc.sbuf_tensor(f"m1_{name}", shape, dt))
            xn = hold("xn", [128, NB, D])
            norm_phase(k, "m1", X, ident, xn, xnT)
            routing = (hold("p", [128, NB, ROUTED]), hold("tot", [128, NB]), hold("chosen", [128, NB, 8]),
                       hold("place", [128, NB, TOPK], U32), hold("key", [128, NB, ROUTED]),
                       hold("tile_expert", [128, TILES], I32), hold("copies", [128, TOPK, NB, RW]),
                       hold("spare", [128, 1]))
            router_phase(k, xn, xnT, ident, a["gateT"], *routing)
            experts_phase(k, X, xnT, ident, *routing, a["wgu"], a["wd"], token_rows, result_rows, out)
        k.layer.close()


def laid_out(i):
    import numpy as np

    def heads_T(w, n):
        return np.ascontiguousarray(w.reshape(w.shape[0], n, HD).transpose(2, 1, 0))

    a = {"x": i["x"], "ctxN": i["ctx_1024"], "ctxT": np.ascontiguousarray(i["ctx_1024"].transpose(0, 2, 1)),
         "mask": i["mask_BxS2_bf1"].view(np.uint8)}
    for layer, kv in ((0, H // 2), (1, H)):
        w = {n: i[f"L{layer}_xattn_{n}"] for n in ("Wq", "Wk", "Wv", "Wo")}
        a[f"WqT{layer}"] = heads_T(w["Wq"], H)
        a[f"WkT{layer}"] = heads_T(w["Wk"], kv)
        a[f"WvT{layer}"] = heads_T(w["Wv"], kv)
        a[f"Wo{layer}"] = np.ascontiguousarray(w["Wo"].reshape(H, HD, D).transpose(1, 0, 2))
    a["Wq1"] = np.ascontiguousarray(i["L1_xattn_Wq"].reshape(DC, 128, H * HD).transpose(1, 0, 2))
    a["Wk1"] = i["L1_xattn_Wk"]
    a["gq"], a["gk"] = i["L1_xattn_gq"].reshape(HD, 1), i["L1_xattn_gk"].reshape(HD, 1)
    for n, m in (("wT", "weight"), ("rramT", "rram_variation")):
        a[n] = np.ascontiguousarray(i[f"L0_ffn_{m}"].T.reshape(DC, 128, D).transpose(1, 0, 2))
    a["gateT"] = np.ascontiguousarray(i["L1_ffn_gate_w"].T.reshape(DC, 128, ROUTED).transpose(1, 0, 2))
    sgu = i["L1_ffn_ws_gate_up"].reshape(2, 2, FFN, D).transpose(1, 0, 2, 3).reshape(2, 2 * FFN, D)
    gu = np.concatenate([i["L1_ffn_w_gate_up"], sgu])
    a["wgu"] = np.ascontiguousarray(gu.transpose(0, 2, 1).reshape(ROUTED + SHARED, DC, 128, 2 * FFN).transpose(0, 2, 1, 3))
    down = np.concatenate([i["L1_ffn_w_down"], i["L1_ffn_ws_down"].reshape(D, 2, FFN).transpose(1, 0, 2)])
    down = down.transpose(0, 2, 1)
    a["wd"] = np.zeros((ROUTED + SHARED, FC, NF, D), down.dtype)
    a["wd"][:, :, 0] = down[:, 0:FC]
    a["wd"][:, FC - FS:, 1] = down[:, FC:]
    return {n: np.ascontiguousarray(v) for n, v in a.items()}


def kernel(**inputs):
    import numpy as np
    import concourse.bacc as bacc
    from concourse.bass_utils import run_bass_kernel_spmd

    arrays = laid_out({n: np.asarray(v) for n, v in inputs.items()})
    nc = bacc.Bacc("TRN2", target_bir_lowering=False, num_devices=1)
    aps = {n: nc.dram_tensor(f"in_{n}", v.shape, mybir.dt.from_np(v.dtype), kind="ExternalInput").ap()
           for n, v in arrays.items()}
    out = nc.dram_tensor("out", (NB, Q, D), F32, kind="ExternalOutput").ap()
    program(nc, aps, out)
    r = run_bass_kernel_spmd(nc, [{f"in_{n}": v for n, v in arrays.items()}], core_ids=[0])
    return r.results[0]["out"]
```
